# Optimizing a Trainium2 kernel written in Bass

```python
import numpy as np
import jax
import jax.numpy as jnp

def _softmax(x, axis=-1):
    return jax.nn.softmax(x, axis=axis)
def _gelu(x):
    return jax.nn.gelu(x, approximate=True)
def _silu(x):
    return jax.nn.silu(x)
def _sigmoid(x):
    return jax.nn.sigmoid(x)
def _layernorm(x, axis=-1, eps=1e-5):
    m = jnp.mean(x, axis=axis, keepdims=True)
    v = jnp.var(x, axis=axis, keepdims=True)
    return (x - m) / jnp.sqrt(v + eps)
def _scatter_add(tgt, idx, src, axis=0):
    return tgt.at[idx].add(src)
def _segment_sum(src, seg, n):
    return jax.ops.segment_sum(src, seg, n)

kernel_name = 'mk_conv_attn_hybrid_d2_conv_nchw256_6c8dd8'

def setup_inputs(seed: int = 0):
    np.random.seed(seed)
    _w = jnp.asarray
    def _rec_inputs():
        import jax
        import jax.numpy as jnp
        _gk = jax.random.key(seed)
        x = -0.000929 + 1 * jax.random.normal(jax.random.fold_in(_gk, 1), (1, 256, 64, 64), jnp.float32)
        return x
    x = _rec_inputs()
    def _L0_conv_setup():
        import jax, jax.numpy as jnp
        import numpy as np
        N_FEAT = 256
        NUM_HEADS = 8
        EPS = 1e-12

        def _l2norm(t):
            n = jnp.linalg.norm(t, axis=-1, keepdims=True)
            return t / jnp.maximum(n, EPS)
        key = jax.random.key(seed)
        k1, k2, k3 = jax.random.split(key, 3)
        b, c, h, w = (1, N_FEAT, 64, 64)
        x = jax.random.normal(k1, (b, c, h, w), dtype=jnp.float32)
        w_qkv = jax.random.normal(k2, (3 * c, c), dtype=jnp.float32) * (1.0 / np.sqrt(c))
        w_proj = jax.random.normal(k3, (c, c), dtype=jnp.float32) * (1.0 / np.sqrt(c))
        temperature = jnp.ones((NUM_HEADS, 1, 1), dtype=jnp.float32)
        return {'x': x, 'w_qkv': w_qkv, 'w_proj': w_proj, 'temperature': temperature}
    _L0_conv_all = _L0_conv_setup()
    _L0_conv_in = {k: v for k, v in _L0_conv_all.items() if k in ('w_qkv', 'w_proj', 'temperature', )}
    del _L0_conv_all

    def _L1_attn_setup():
        import jax, jax.numpy as jnp
        import numpy as np
        TOPK = 32
        key = jax.random.key(seed)
        ks = jax.random.split(key, 7)
        B, S, D = (4, 4096, 256)
        sc = 1.0 / np.sqrt(D)
        return {'x': jax.random.normal(ks[0], (B, S, D), dtype=jnp.float32), 'Wq': jax.random.normal(ks[1], (D, D), dtype=jnp.float32) * sc, 'bq': jnp.zeros((D,), dtype=jnp.float32), 'Wk': jax.random.normal(ks[2], (D, D), dtype=jnp.float32) * sc, 'bk': jnp.zeros((D,), dtype=jnp.float32), 'Wv': jax.random.normal(ks[3], (D, D), dtype=jnp.float32) * sc, 'bv': jnp.zeros((D,), dtype=jnp.float32)}
    _L1_attn_all = _L1_attn_setup()
    _L1_attn_in = {k: v for k, v in _L1_attn_all.items() if k in ('Wq', 'bq', 'Wk', 'bk', 'Wv', 'bv', )}
    del _L1_attn_all

    def _L1_ffn_setup():
        import jax, jax.numpy as jnp
        import numpy as np
        TOP_K = 2
        key = jax.random.key(seed)
        ks = jax.random.split(key, 4)
        B, L, D, H, E = (8, 4096, 256, 1024, 8)
        s = 0.02
        return {'x': jax.random.normal(ks[0], (B, L, D), jnp.float32), 'Wg': jax.random.normal(ks[1], (D, E), jnp.float32) * s, 'bg': jnp.zeros((E,), jnp.float32), 'W1': jax.random.normal(ks[2], (E, D, H), jnp.float32) * s, 'b1': jnp.zeros((E, H), jnp.float32), 'W2': jax.random.normal(ks[3], (E, H, D), jnp.float32) * s, 'b2': jnp.zeros((E, D), jnp.float32)}
    _L1_ffn_all = _L1_ffn_setup()
    _L1_ffn_in = {k: v for k, v in _L1_ffn_all.items() if k in ('Wg', 'bg', 'W1', 'b1', 'W2', 'b2', )}
    del _L1_ffn_all

    return {
        "x": x,
        "L0_conv_w_qkv": _L0_conv_in["w_qkv"],
        "L0_conv_w_proj": _L0_conv_in["w_proj"],
        "L0_conv_temperature": _L0_conv_in["temperature"],
        "L1_attn_Wq": _L1_attn_in["Wq"],
        "L1_attn_bq": _L1_attn_in["bq"],
        "L1_attn_Wk": _L1_attn_in["Wk"],
        "L1_attn_bk": _L1_attn_in["bk"],
        "L1_attn_Wv": _L1_attn_in["Wv"],
        "L1_attn_bv": _L1_attn_in["bv"],
        "L1_ffn_Wg": _L1_ffn_in["Wg"],
        "L1_ffn_bg": _L1_ffn_in["bg"],
        "L1_ffn_W1": _L1_ffn_in["W1"],
        "L1_ffn_b1": _L1_ffn_in["b1"],
        "L1_ffn_W2": _L1_ffn_in["W2"],
        "L1_ffn_b2": _L1_ffn_in["b2"],
    }

def reference(x, L0_conv_w_qkv, L0_conv_w_proj, L0_conv_temperature, L1_attn_Wq, L1_attn_bq, L1_attn_Wk, L1_attn_bk, L1_attn_Wv, L1_attn_bv, L1_ffn_Wg, L1_ffn_bg, L1_ffn_W1, L1_ffn_b1, L1_ffn_W2, L1_ffn_b2):
    import jax
    import jax.numpy as jnp
    def _L0_conv_ref(x, w_qkv, w_proj, temperature):
        import jax, jax.numpy as jnp
        import numpy as np
        N_FEAT = 256
        NUM_HEADS = 8
        EPS = 1e-12

        def _l2norm(t):
            n = jnp.linalg.norm(t, axis=-1, keepdims=True)
            return t / jnp.maximum(n, EPS)
        b, c, h, w = x.shape
        heads = temperature.shape[0]
        d = c // heads
        hw = h * w
        xf = x.reshape(b, c, hw)
        qkv = jnp.einsum('oc,bcs->bos', w_qkv, xf)
        qkv = qkv.reshape(b, 3, heads, d, hw)
        q, k, v = (qkv[:, 0], qkv[:, 1], qkv[:, 2])
        q = jnp.swapaxes(q, -2, -1)
        k = jnp.swapaxes(k, -2, -1)
        v = jnp.swapaxes(v, -2, -1)
        q = _l2norm(q)
        k = _l2norm(k)
        attn = jnp.einsum('bhsd,bhtd->bhst', q, k) * temperature[None]
        attn = jax.nn.softmax(attn, axis=-1)
        out = jnp.einsum('bhst,bhtd->bhsd', attn, v)
        out = out.transpose(0, 2, 1, 3).reshape(b, c, h, w)
        out = jnp.einsum('oc,bchw->bohw', w_proj, out)
        return out

    def _L1_attn_ref(x, Wq, bq, Wk, bk, Wv, bv):
        import jax, jax.numpy as jnp
        import numpy as np
        TOPK = 32
        q = x @ Wq + bq
        k = x @ Wk + bk
        v = x @ Wv + bv
        sim = jnp.einsum('bsd,btd->bst', q, k)
        topk_vals, topk_idx = jax.lax.top_k(sim, TOPK)
        probs = jax.nn.softmax(topk_vals, axis=-1)
        v_sel = jnp.take_along_axis(v[:, None, :, :], topk_idx[..., None], axis=2)
        out = jnp.einsum('bsk,bskd->bsd', probs, v_sel)
        return out

    def _L1_ffn_ref(x, Wg, bg, W1, b1, W2, b2):
        import jax, jax.numpy as jnp
        import numpy as np
        TOP_K = 2
        B, L, D = x.shape
        E = W1.shape[0]
        xf = x.reshape(-1, D)
        gate_logits = xf @ Wg + bg
        top_w, top_i = jax.lax.top_k(gate_logits, TOP_K)
        top_w = jax.nn.softmax(top_w, axis=-1)
        w_dense = jnp.sum(jax.nn.one_hot(top_i, E, dtype=xf.dtype) * top_w[..., None], axis=1)
        out = jnp.zeros_like(xf)
        for e in range(E):
            h = jax.nn.gelu(xf @ W1[e] + b1[e], approximate=False)
            out = out + w_dense[:, e:e + 1] * (h @ W2[e] + b2[e])
        return out.reshape(B, L, D)

    def _gn(v, G=32, eps=1e-5):
        B_, C_, H_, W_ = v.shape
        g = v.reshape(B_, G, C_ // G, H_, W_)
        m = jnp.mean(g, axis=(2, 3, 4), keepdims=True)
        s = jnp.var(g, axis=(2, 3, 4), keepdims=True)
        return ((g - m) / jnp.sqrt(s + eps)).reshape(v.shape)

    def _ln_c(v, eps=1e-6):
        m = jnp.mean(v, axis=1, keepdims=True)
        s = jnp.var(v, axis=1, keepdims=True)
        return (v - m) / jnp.sqrt(s + eps)

    def _ln_t(v, eps=1e-5):
        m = jnp.mean(v, axis=-1, keepdims=True)
        s = jnp.var(v, axis=-1, keepdims=True)
        return (v - m) / jnp.sqrt(s + eps)

    def _to_tokens(v):
        B_, C_, H_, W_ = v.shape
        return v.reshape(B_, C_, H_ * W_).transpose(0, 2, 1)
    def _from_tokens(t, like):
        B_, C_, H_, W_ = like.shape
        return t.transpose(0, 2, 1).reshape(B_, C_, H_, W_)

    x = x + _L0_conv_ref(_gn(x), L0_conv_w_qkv, L0_conv_w_proj, L0_conv_temperature)
    t = _to_tokens(x)
    t = t + _L1_attn_ref(_ln_t(t), L1_attn_Wq, L1_attn_bq, L1_attn_Wk, L1_attn_bk, L1_attn_Wv, L1_attn_bv)
    t = t + _L1_ffn_ref(_ln_t(t), L1_ffn_Wg, L1_ffn_bg, L1_ffn_W1, L1_ffn_b1, L1_ffn_W2, L1_ffn_b2)
    x = _from_tokens(t, x)
    return x


_drawn_inputs = setup_inputs


def setup_inputs(seed=0):
    import zlib

    import numpy as np

    out = dict(_drawn_inputs(seed))
    spreads = {'L0_conv_temperature': (1.0, 0.6),
     'L1_attn_bq': (0.0, 0.1),
     'L1_attn_bk': (0.0, 0.8),
     'L1_attn_bv': (0.0, 0.1),
     'L1_ffn_bg': (0.0, 0.1),
     'L1_ffn_b1': (0.0, 0.418),
     'L1_ffn_b2': (0.0, 0.1)}
    factors = {}
    for name, (base, spread) in spreads.items():
        noise = np.random.default_rng([zlib.crc32(name.encode()), seed]).standard_normal(out[name].shape)
        drawn = base * np.exp(spread * noise) if base else spread * noise
        out[name] = jnp.asarray(drawn.astype(out[name].dtype))
    for name, factor in factors.items():
        out[name] = (out[name] * factor).astype(out[name].dtype)
    return out
```

```python
from contextlib import ExitStack

import numpy as np

import concourse.bass as bass
from concourse import mybir

P = 128
F32 = mybir.dt.float32
F16 = mybir.dt.float16
U32 = mybir.dt.uint32
ALU = mybir.AluOpType
ACT = mybir.ActivationFunctionType
AX_X = mybir.AxisListType.X

C = 256
S = 4096
HEADS = 8
D = C // HEADS
KC = C // P
TT = S // P
ST = S // 512
SUB = S // C
NE = 8
HID = 1024
HC = HID // P
TOPK = 32
GN_EPS = 1e-5
LN_EPS = 1e-5
NORM_EPS = 1e-12
TAKEN = -3.0e38

C_ID, C_GROUP, C_HEAD, C_FOLD, C_ONE, C_SEL, C_IOTA = 0, 128, 256, 384, 416, 417, 418
C_N = C_IOTA + NE


class Chain:

    def __init__(self, eng, sem, base=0):
        self.eng, self.sem, self.base, self.n = eng, sem, base, 0

    def step(self, ins):
        ins.then_inc(self.sem, 1)
        self.n += 1

    def wait(self):
        self.eng.wait_ge(self.sem, self.base + self.n)

    def link(self, ins):
        self.step(ins)
        self.wait()


def build(nc, x, xT, wqkvT, wprojT, t_col, t_row, wq, wk, wv, bq, bk, bv, wg, bg, w1, b1, w2, b2, consts, out):
    qk_scr = nc.dram_tensor("qk_scr", (2, 2, C, S), F16, kind="Internal").ap()
    q1_scr = nc.dram_tensor("q1_scr", (TT, P, KC, P), F32, kind="Internal").ap()
    with ExitStack() as ctx:
        def sb(name, shape, dt=F32):
            return ctx.enter_context(nc.sbuf_tensor(name, shape, dt))

        big = [sb(f"big{i}", [P, 8192]) for i in range(6)]
        cst = sb("cst", [P, C_N])
        ident = cst[:, C_ID:C_ID + P]
        negt = sb("negt", [P, HEADS])
        eps = sb("eps", [P, 2])
        gate = sb("gate", [P, TT, NE])
        ps = ctx.enter_context(nc.psum_tensor("ps", [P, 8, 512], F32))
        group_norm_and_qkv(nc, ctx, ps, big, cst, eps, negt, x, wqkvT, t_col, t_row, consts, qk_scr)
        attention_0(nc, ctx, ps, big, cst, negt, qk_scr)
        project_and_norm(nc, ctx, ps, big, cst, eps, xT, wprojT)
        qkv_1(nc, ctx, ps, big, wq, wk, wv, bq, bk, bv, q1_scr)
        attention_1(nc, ctx, ps, big, ident, q1_scr)
        norm_and_gate(nc, ctx, ps, big, cst, eps, gate, wg, bg, b2)
        experts(nc, ctx, ps, big, gate, w1, b1, w2, out)


def group_norm_and_qkv(nc, ctx, ps, big, cst, eps, negt, x, wqkvT, t_col, t_row, consts, qk_scr):
    v0 = big[0].rearrange("p (t c) -> p t c", c=C)
    xn = big[2].rearrange("p (k s) -> p k s", k=KC)
    w = big[3][:, 0:KC * 3 * C].rearrange("p (k o) -> p k o", k=KC)
    stage = big[4]
    sq = [stage[:, 512 * b:512 * b + 512] for b in range(2)]
    nrm = [stage[:, 1024 + 512 * b:1536 + 512 * b] for b in range(2)]
    y = [stage[:, 2048 + 512 * b:2560 + 512 * b] for b in range(2)]
    hi = [stage[:, 3072 + 512 * b:3328 + 512 * b].bitcast(F16) for b in range(2)]
    lo = [stage[:, 4096 + 512 * b:4352 + 512 * b].bitcast(F16) for b in range(2)]
    small = big[5]
    stats = small[:, 0:96].rearrange("p (k g n) -> p k g n", k=KC, n=6)
    mv = small[:, 96:100].rearrange("p (k n) -> p k n", k=KC)
    dev = small[:, 100:102]
    var = small[:, 102:104]
    rstd = small[:, 104:106]
    shift = small[:, 106:108]
    gmean = small[:, 108:112].rearrange("p (k n) -> p k n", k=KC)
    tcol = small[:, 112:114]
    trow = small[:, 114:122]

    def sem(name):
        return ctx.enter_context(nc.semaphore(name))

    loaded_x = [sem("loaded_x0"), sem("loaded_x1")]
    loaded_w, loaded_c = sem("loaded_w"), sem("loaded_c")
    gn_step = sem("gn_step")
    stats_ready, gmean_ready, dev_ready, gvar_ready = sem("stats_ready"), sem("gmean_ready"), sem("dev_ready"), sem("gvar_ready")
    var_ready, std_ready, xn_ready = sem("var_ready"), sem("std_ready"), sem("xn_ready")
    qk_ready, sq_ready, ss_ready, nrm_ready = sem("qk_ready"), sem("sq_ready"), sem("ss_ready"), sem("nrm_ready")
    hi_ready = sem("hi_ready")
    y_step, split_ready, split_stored = sem("y_step"), sem("split_ready"), [sem("split_stored_even"), sem("split_stored_odd")]
    v_ready, v_copied = sem("v_ready"), sem("v_copied")

    with nc.Block() as block:
        @block.sync
        def _(sp):
            for k in range(KC):
                sp.dma_start(xn[:, k, :], x[P * k:P * k + P, :]).then_inc(loaded_x[k], 16)
            sp.dma_start(w[:, :, :], wqkvT.rearrange("(k p) o -> p k o", p=P)).then_inc(loaded_w, 16)
            for b in range(2):
                sp.sem_inc(split_stored[b], 16)
            for ot in range(4):
                with sp.Fori(0, ST // 2) as i:
                    for b in range(2):
                        sp.wait_ge(split_ready, (i * 2 + b) + (ot * ST + 1))
                        for part, src in ((0, hi[b]), (1, lo[b])):
                            sp.dma_start(qk_scr[ot // 2, part, P * (ot % 2):P * (ot % 2) + P,
                                                bass.ds(i * 1024 + b * 512, 512)], src).then_inc(split_stored[b], 16)
            for b in range(2):
                sp.wait_ge(split_stored[b], 16 + 32 * 4 * ST // 2)

        @block.gpsimd
        def _(pool):
            pool.dma_start(cst[:, :], consts).then_inc(loaded_c, 16)
            pool.dma_start(tcol, t_col).then_inc(loaded_c, 16)
            pool.dma_start(trow, t_row).then_inc(loaded_c, 16)

        @block.vector
        def _(dve):
            dve.sem_inc(y_step, 4)
            ch = Chain(dve, gn_step)
            ch.step(nc.vector.memset(eps[:, 0:1], GN_EPS))
            ch.step(nc.vector.memset(eps[:, 1:2], LN_EPS))
            dve.wait_ge(loaded_c, 48)
            ch.link(nc.vector.tensor_scalar(negt[:, :], trow, -1.0, None, op0=ALU.mult))
            ch.step(nc.vector.tensor_tensor(out=negt[:, :], in0=negt[:, :], in1=trow, op=ALU.min))
            for k in range(KC):
                dve.wait_ge(loaded_x[k], 16)
                for g in range(ST):
                    ch.step(nc.vector.bn_stats(stats[:, k, g, :], xn[:, k, 512 * g:512 * g + 512]))
            ch.wait()
            for k in range(KC):
                nc.vector.bn_aggr(mv[:, k, :], stats[:, k, :, :]).then_inc(stats_ready, 1)
            dve.wait_ge(gmean_ready, 1)
            dve.wait_ge(stats_ready, KC)
            ch.link(nc.vector.tensor_copy(gmean[:, :, :], ps[:, 0, 0:4].rearrange("p (k n) -> p k n", k=KC)))
            ch.link(nc.vector.tensor_tensor(out=dev, in0=mv[:, :, 0], in1=gmean[:, :, 0], op=ALU.subtract))
            nc.vector.tensor_tensor(out=dev, in0=dev, in1=dev, op=ALU.mult).then_inc(dev_ready, 1)
            dve.wait_ge(gvar_ready, 1)
            nc.vector.tensor_tensor(out=var, in0=gmean[:, :, 1], in1=ps[:, 1, 0:2], op=ALU.add).then_inc(var_ready, 1)
            dve.wait_ge(std_ready, 1)
            ch.link(nc.vector.reciprocal(rstd, var))
            for k in range(KC):
                nc.vector.tensor_scalar(xn[:, k, :], xn[:, k, :], gmean[:, k, 0:1], rstd[:, k:k + 1],
                                        op0=ALU.subtract, op1=ALU.mult).then_inc(xn_ready, 1)
            for ot in range(4):
                with dve.Fori(0, ST // 2) as i:
                    for b in range(2):
                        n = i * 2 + (b + ot * ST)
                        yc = Chain(dve, y_step, n * 3 + 4)
                        dve.wait_ge(nrm_ready, n + 1)
                        yc.link(nc.vector.tensor_scalar(nrm[b], nrm[b], NORM_EPS, None, op0=ALU.max))
                        yc.link(nc.vector.reciprocal(nrm[b], nrm[b]))
                        dve.wait_ge(split_stored[b], i * 32 + (16 + 32 * (ot * ST // 2)))
                        yc.link(nc.vector.scalar_tensor_tensor(
                            out=y[b], in0=ps[:, 2 + b, :], scalar=tcol[:, ot:ot + 1] if ot < 2 else 1.0,
                            in1=nrm[b], op0=ALU.mult, op1=ALU.mult))
                        nc.vector.tensor_copy(hi[b], y[b]).then_inc(hi_ready, 1)
                        dve.wait_ge(hi_ready, n + 1)
                        nc.vector.tensor_tensor(out=lo[b], in0=y[b], in1=hi[b], op=ALU.subtract).then_inc(split_ready, 1)

        @block.scalar
        def _(act):
            act.wait_ge(var_ready, 1)
            act.wait_ge(gn_step, 1)
            nc.scalar.activation(var, var, ACT.Sqrt, bias=eps[:, 0:1]).then_inc(std_ready, 1)
            for ot in range(4):
                with act.Fori(0, ST // 2) as i:
                    for b in range(2):
                        n = i * 2 + (b + ot * ST)
                        act.wait_ge(qk_ready, n + 1)
                        nc.scalar.activation(sq[b], ps[:, 2 + b, :], ACT.Square).then_inc(sq_ready, 1)
                    for b in range(2):
                        n = i * 2 + (b + ot * ST)
                        act.wait_ge(ss_ready, n + 1)
                        nc.scalar.activation(nrm[b], ps[:, 4 + b, :], ACT.Sqrt).then_inc(nrm_ready, 1)
            for t in range(TT // 2):
                act.wait_ge(v_ready, t + 1)
                nc.scalar.activation(big[0][:, 512 * t:512 * t + 512], ps[:, 6 + t % 2, :], ACT.Copy).then_inc(v_copied, 1)

        @block.tensor
        def _(pe):
            pe.wait_ge(loaded_c, 48)
            pe.wait_ge(stats_ready, KC)
            nc.tensor.matmul(ps[:, 0, 0:4], cst[:, C_GROUP:C_GROUP + P], mv[:, :, :].rearrange("p k n -> p (k n)"),
                             start=True, stop=True).then_inc(gmean_ready, 1)
            pe.wait_ge(dev_ready, 1)
            nc.tensor.matmul(ps[:, 1, 0:2], cst[:, C_GROUP:C_GROUP + P], dev, start=True, stop=True).then_inc(gvar_ready, 1)
            pe.wait_ge(loaded_w, 16)
            pe.wait_ge(xn_ready, KC)
            for ot in range(4):
                with pe.Fori(0, ST // 2) as i:
                    for b in range(2):
                        n = i * 2 + (b + ot * ST)
                        pe.wait_ge(y_step, n * 3 + 1)
                        for k in range(KC):
                            last = nc.tensor.matmul(ps[:, 2 + b, :], w[:, k, P * ot:P * ot + P],
                                                    xn[:, k, bass.ds(i * 1024 + b * 512, 512)],
                                                    start=(k == 0), stop=(k == KC - 1))
                        last.then_inc(qk_ready, 1)
                    for b in range(2):
                        n = i * 2 + (b + ot * ST)
                        pe.wait_ge(sq_ready, n + 1)
                        nc.tensor.matmul(ps[:, 4 + b, :], cst[:, C_HEAD:C_HEAD + P], sq[b],
                                         start=True, stop=True).then_inc(ss_ready, 1)
            for t in range(TT // 2):
                if t >= 2:
                    pe.wait_ge(v_copied, t - 1)
                for u in range(2):
                    for k in range(KC):
                        last = nc.tensor.matmul(ps[:, 6 + t % 2, 256 * u:256 * u + 256],
                                                xn[:, k, P * (2 * t + u):P * (2 * t + u) + P], w[:, k, 2 * C:3 * C],
                                                start=(k == 0), stop=(k == KC - 1))
                last.then_inc(v_ready, 1)


def attention_0(nc, ctx, ps, big, cst, negt, qk_scr):
    HALF_ST = ST // 2
    GROUPS = TT // 4
    NG = HALF_ST * GROUPS
    RING_S, RING_P = 3, 4
    v0 = big[0].rearrange("p (t c) -> p t c", c=C)
    image = big[1].rearrange("p (f j c) -> p f j c", f=2, j=SUB)
    kst = [big[2][:, 2048 * b:2048 * b + 2048].bitcast(F16) for b in range(2)]
    qst = [big[2][:, 4096 + 2048 * b:6144 + 2048 * b].bitcast(F16) for b in range(2)]
    probs = big[3].rearrange("p (r t s) -> p r t s", r=RING_P, t=4)
    vh = [big[4][:, 1024 * b:1024 * b + 1024].rearrange("p (t d) -> p t d", d=D) for b in range(2)]
    outT = big[4][:, 2048:4096]
    denV = big[4][:, 4096:6144]
    denP = big[4][:, 6144:8192]
    tmp = [big[5][:, 1024 * b:1024 * b + 1024] for b in range(2)]
    acc = big[5][:, 2048:3072]
    ones = big[5][:, 3072:3104]
    rden = big[5][:, 3104:3120]
    bound = [big[5][:, 3120 + b:3121 + b] for b in range(2)]
    PS_O, PS_D = 6, 7

    def by_pe(g):
        return g % 4 == 3

    upto = [sum(not by_pe(a) for a in range(g + 1)) for g in range(NG)]
    NDV = upto[-1]

    def sem(name):
        return ctx.enter_context(nc.semaphore(name))

    heads_loaded = [sem("heads_loaded_even"), sem("heads_loaded_odd")]
    vh_ready = sem("vh_ready")
    s_ready, exp_done, pv_done, sum_done = sem("s_ready"), sem("exp_done"), sem("pv_done"), sem("sum_done")
    sum_step, ones_ready = sem("sum_step"), sem("ones_ready")
    o_copied, d_copied, acc_done = sem("o_copied"), sem("d_copied"), sem("acc_done")
    fold_done, image_done, rden_done = sem("fold_done"), sem("image_done"), sem("rden_done")

    with nc.Block() as block:
        @block.sync
        def _(sp):
            def load(hb, rows):
                for a in range(2):
                    for part in range(2):
                        at = 64 * a + 32 * part
                        sp.dma_start(qst[hb][at:at + D, :], qk_scr[0, part, rows, :]).then_inc(heads_loaded[hb], 16)
                        sp.dma_start(kst[hb][at:at + D, :], qk_scr[1, a, rows, :]).then_inc(heads_loaded[hb], 16)

            for hb in range(2):
                load(hb, bass.ds(hb * D, D))
            with sp.Fori(0, HEADS // 2 - 1) as hp:
                for hb in range(2):
                    sp.wait_ge(fold_done, hp * 4 + (1 + 2 * (hb + 1)))
                    load(hb, bass.ds(hp * 2 * D + (hb + 2) * D, D))

        @block.gpsimd
        def _(pool):
            def load(hb, head, cols):
                nc.gpsimd.tensor_copy(bound[hb], negt[:, head]).then_inc(vh_ready, 1)
                nc.gpsimd.tensor_copy(vh[hb], v0[:, :, cols]).then_inc(vh_ready, 1)

            for hb in range(2):
                load(hb, bass.ds(hb, 1), bass.ds(hb * D, D))
            with pool.Fori(0, HEADS // 2 - 1) as hp:
                for hb in range(2):
                    pool.wait_ge(fold_done, hp * 4 + (1 + 2 * (hb + 1)))
                    load(hb, bass.ds(hp * 2 + (hb + 2), 1), bass.ds(hp * 2 * D + (hb + 2) * D, D))

        def copy_out(act, it, st):
            act.wait_ge(pv_done, it * NG + (RING_P + GROUPS * (st + 1)))
            if st == 0:
                act.wait_ge(fold_done, it + 1)
            nc.scalar.activation(outT[:, 512 * st:512 * st + 512], ps[:, PS_O, :], ACT.Copy).then_inc(o_copied, 1)

        @block.scalar
        def _(act):
            act.sem_inc(exp_done, RING_S)
            with act.Fori(0, HEADS // 2) as hp:
                for hb in range(2):
                    with act.Fori(0, 2) as half:
                        it = hp * 4 + hb * 2 + half
                        act.wait_ge(vh_ready, hp * 4 + 2 * (hb + 1))
                        for g in range(NG):
                            act.wait_ge(pv_done, it * NG + (g + 1))
                            p = g - RING_P
                            if not by_pe(p % NG):
                                act.wait_ge(sum_done, it * NDV + (3 + (upto[p] if p >= 0 else upto[p + NG] - NDV)))
                            for u in (2 * g, 2 * g + 1):
                                act.wait_ge(s_ready, it * (2 * NG) + (u + 1))
                                sl = 2 * (u % RING_S)
                                nc.scalar.activation(probs[:, g % RING_P, 2 * (u % 2):2 * (u % 2) + 2, :], ps[:, sl:sl + 2, :],
                                                     ACT.Exp, bias=bound[hb]).then_inc(exp_done, 1)
                            if g % GROUPS == 0 and g >= GROUPS:
                                copy_out(act, it, g // GROUPS - 1)
                        copy_out(act, it, HALF_ST - 1)

        @block.vector
        def _(dve):
            nc.vector.memset(ones, 1.0).then_inc(ones_ready, 1)
            dve.sem_inc(sum_done, 3)
            with dve.Fori(0, HEADS // 2) as hp:
                for hb in range(2):
                    with dve.Fori(0, 2) as half:
                        it = hp * 4 + hb * 2 + half
                        ch = Chain(dve, sum_step, it * (NDV - HALF_ST))
                        for st in range(HALF_ST):
                            first = True
                            for g in range(GROUPS * st, GROUPS * (st + 1)):
                                if by_pe(g):
                                    continue
                                dve.wait_ge(exp_done, it * (2 * NG) + (RING_S + 2 * g + 2))
                                a, b = probs[:, g % RING_P, 0:2, :], probs[:, g % RING_P, 2:4, :]
                                if first:
                                    if st == 0:
                                        dve.wait_ge(fold_done, it + 1)
                                    nc.vector.tensor_tensor(out=acc, in0=a, in1=b, op=ALU.add).then_inc(sum_done, 1)
                                else:
                                    t = tmp[g % 2]
                                    nc.vector.tensor_tensor(out=t, in0=a, in1=b, op=ALU.add).then_inc(sum_done, 1)
                                    dve.wait_ge(sum_done, it * NDV + (3 + upto[g]))
                                    ch.link(nc.vector.tensor_tensor(out=acc, in0=acc, in1=t, op=ALU.add))
                                first = False
                            nc.vector.tensor_tensor(out=denV[:, 512 * st:512 * st + 512], in0=acc[:, 0:512],
                                                    in1=acc[:, 512:1024], op=ALU.add).then_inc(acc_done, 1)
                            dve.wait_ge(acc_done, it * HALF_ST + (st + 1))
                            dve.wait_ge(pv_done, it * NG + (RING_P + GROUPS * (st + 1)))
                            nc.vector.tensor_copy(denP[:, 512 * st:512 * st + 512], ps[:, PS_D, :]).then_inc(d_copied, 1)
                        dve.wait_ge(fold_done, it + 2)
                        nc.vector.reciprocal(rden, ps[:, 3, 0:SUB]).then_inc(rden_done, 1)
                        dve.wait_ge(rden_done, it + 1)
                        nc.vector.tensor_tensor(
                            out=image[:, bass.ds(half, 1), :, bass.ds(hp * 2 * D + hb * D, D)].rearrange("p f j d -> p (f j) d"),
                            in0=ps[:, 2, :].rearrange("p (j d) -> p j d", d=D),
                            in1=rden.unsqueeze(2).to_broadcast([P, SUB, D]), op=ALU.mult).then_inc(image_done, 1)

        @block.tensor
        def _(pe):
            pe.sem_inc(fold_done, 1)
            pe.sem_inc(image_done, 1)
            pe.sem_inc(o_copied, 1)
            pe.sem_inc(d_copied, 1)
            pe.sem_inc(pv_done, RING_P)
            pe.wait_ge(ones_ready, 1)

            def scores(it, hb, half, g):
                for u in (2 * g, 2 * g + 1):
                    pe.wait_ge(exp_done, it * (2 * NG) + (u + 1))
                    if u == 1:
                        pe.wait_ge(image_done, it + 1)
                    for a in range(2):
                        t = 2 * (u % (2 * GROUPS)) + a
                        last = nc.tensor.matmul(ps[:, 2 * (u % RING_S) + a, :], kst[hb][:, P * t:P * t + P],
                                                qst[hb][:, bass.ds(half * 2048 + 512 * (g // GROUPS), 512)],
                                                start=True, stop=True)
                    last.then_inc(s_ready, 1)

            def weighted(it, hb, g):
                st, r = g // GROUPS, g % GROUPS
                pe.wait_ge(exp_done, it * (2 * NG) + (RING_S + 2 * g + 2))
                if r == 0:
                    pe.wait_ge(o_copied, it * HALF_ST + (st + 1))
                for j in range(4):
                    last = nc.tensor.matmul(ps[32 * j:32 * j + 32, PS_O, :], vh[hb][:, 4 * r + j, :],
                                            probs[:, g % RING_P, j, :], start=(r == 0), stop=(r == GROUPS - 1),
                                            tile_position=(0, 32 * j))
                if by_pe(g):
                    if r == 3:
                        pe.wait_ge(d_copied, it * HALF_ST + (st + 1))
                    for j in range(4):
                        last = nc.tensor.matmul(ps[32 * j:32 * j + 32, PS_D, :], ones, probs[:, g % RING_P, j, :],
                                                start=(r == 3), stop=(r == GROUPS - 1), tile_position=(0, 32 * j))
                last.then_inc(pv_done, 1)

            with pe.Fori(0, HEADS // 2) as hp:
                for hb in range(2):
                    with pe.Fori(0, 2) as half:
                        it = hp * 4 + hb * 2 + half
                        pe.wait_ge(heads_loaded[hb], hp * 128 + 128)
                        pe.wait_ge(vh_ready, hp * 4 + 2 * (hb + 1))
                        LAG = 1
                        for g in range(NG + LAG):
                            if g < NG:
                                scores(it, hb, half, g)
                            if g >= LAG:
                                weighted(it, hb, g - LAG)
                        pe.wait_ge(o_copied, it * HALF_ST + (HALF_ST + 1))
                        pe.wait_ge(acc_done, it * HALF_ST + HALF_ST)
                        pe.wait_ge(d_copied, it * HALF_ST + (HALF_ST + 1))
                        for j in range(SUB):
                            def rows(a):
                                return a.rearrange("p (c j) -> p j c", j=SUB)[:, j, :]
                            nc.tensor.matmul(ps[:, 2, D * j:D * j + D], rows(outT), cst[:, C_FOLD:C_FOLD + D], start=True, stop=True)
                            nc.tensor.matmul(ps[:, 3, j:j + 1], rows(denV), cst[:, C_ONE:C_ONE + 1], start=True, stop=False)
                            last = nc.tensor.matmul(ps[:, 3, j:j + 1], rows(denP), cst[:, C_SEL:C_SEL + 1], start=False, stop=True)
                        last.then_inc(fold_done, 1)


def layer_norm_tiles(nc, block, ctx, name, tok, normT, eps, cst, ps, stage, small, add, loaded):
    NB = TT // 4

    def sem(n):
        return ctx.enter_context(nc.semaphore(name + n))

    step, var_ready, std_ready, norm_ready = sem("step"), sem("var_ready"), sem("std_ready"), sem("norm_ready")
    turned, turned_copied, add_ready, added = sem("turned"), sem("turned_copied"), sem("add_ready"), sem("added")
    norm = [stage[:, 1024 * b:1024 * b + 1024].rearrange("p (t c) -> p t c", t=4) for b in range(2)]
    stats = small[:, 0:24].rearrange("p (t n) -> p t n", n=6)
    mv = [small[:, 24 + 8 * b:32 + 8 * b].rearrange("p (t n) -> p t n", n=2) for b in range(2)]
    std = [small[:, 40 + 4 * b:44 + 4 * b] for b in range(2)]

    @block.vector
    def _(dve):
        ch = Chain(dve, step)
        if loaded is not None:
            dve.wait_ge(loaded, 16)
        for n in range(NB):
            b = n % 2
            if n >= 2:
                dve.wait_ge(norm_ready, 4 * (n - 1))
            t4 = tok[:, 4 * n:4 * n + 4, :]
            if add is not None:
                dve.wait_ge(add_ready, n + 1)
                nc.vector.tensor_tensor(out=t4, in0=t4, in1=ps[:, 2 * b:2 * b + 2, :].rearrange("p b (t c) -> p (b t) c", c=C),
                                        op=ALU.add).then_inc(added, 1)
                dve.wait_ge(added, n + 1)
            ch.wait()
            for t in range(4):
                ch.step(nc.vector.bn_stats(stats[:, t, :], t4[:, t, :]))
            ch.wait()
            for t in range(4):
                last = nc.vector.bn_aggr(mv[b][:, t, :], stats[:, t, :])
                ch.step(last)
            ch.wait()
            nc.vector.tensor_copy(std[b], mv[b][:, :, 1]).then_inc(var_ready, 1)
            dve.wait_ge(std_ready, n + 1)
            ch.link(nc.vector.reciprocal(std[b], std[b]))
            if n >= 2:
                dve.wait_ge(turned, n - 1)
            for t in range(4):
                last = nc.vector.tensor_scalar(norm[b][:, t, :], t4[:, t, :], mv[b][:, t, 0:1], std[b][:, t:t + 1],
                                               op0=ALU.subtract, op1=ALU.mult)
                last.then_inc(norm_ready, 1)

    @block.scalar
    def _(act):
        for n in range(NB):
            b = n % 2
            act.wait_ge(var_ready, n + 1)
            nc.scalar.activation(std[b], std[b], ACT.Sqrt, bias=eps[:, 1:2]).then_inc(std_ready, 1)
            act.wait_ge(turned, n + 1)
            for k in range(KC):
                nc.scalar.activation(normT[:, k, 512 * n:512 * n + 512], ps[:, 4 + 2 * b + k, :], ACT.Copy).then_inc(turned_copied, 1)

    @block.tensor
    def _(pe):
        for n in range(NB + 1):
            if n < NB and add is not None:
                if n >= 2:
                    pe.wait_ge(added, n - 1)
                add(pe, n, 2 * (n % 2)).then_inc(add_ready, 1)
            if n >= 1:
                m, b = n - 1, (n - 1) % 2
                pe.wait_ge(norm_ready, 4 * (m + 1))
                if m >= 2:
                    pe.wait_ge(turned_copied, KC * (m - 1))
                for t in range(4):
                    for k in range(KC):
                        last = nc.tensor.transpose(ps[:, 4 + 2 * b + k, P * t:P * t + P], norm[b][:, t, P * k:P * k + P],
                                                   cst[:, C_ID:C_ID + P])
                last.then_inc(turned, 1)


def project_and_norm(nc, ctx, ps, big, cst, eps, xT, wprojT):
    image = big[1].rearrange("p (f j c) -> p f j c", f=2, j=SUB)
    tok = big[5].rearrange("p (t c) -> p t c", c=C)
    normT = big[2].rearrange("p (k s) -> p k s", k=KC)
    wp = big[4][:, 0:KC * C].rearrange("p (k c) -> p k c", k=KC)
    wp_loaded = ctx.enter_context(nc.semaphore("wp_loaded"))

    def add(pe, n, bank):
        if n == 0:
            pe.wait_ge(wp_loaded, 16)
        for t in range(4):
            i = 4 * n + t
            for f in range(2):
                last = nc.tensor.matmul(ps[:, bank + t // 2, C * (t % 2):C * (t % 2) + C],
                                        image[:, f, i // 2, P * (i % 2):P * (i % 2) + P], wp[:, f, :],
                                        start=(f == 0), stop=(f == 1))
        return last

    loaded = ctx.enter_context(nc.semaphore("xT_loaded"))
    with nc.Block() as block:
        layer_norm_tiles(nc, block, ctx, "ln1_", tok, normT, eps, cst, ps, big[3], big[4][:, 4096:4160], add, loaded)

        @block.sync
        def _(sp):
            sp.dma_start(tok[:, :, :], xT.rearrange("(t p) c -> p t c", p=P)).then_inc(loaded, 16)
            sp.dma_start(wp[:, :, :], wprojT.rearrange("(k p) c -> p k c", p=P)).then_inc(wp_loaded, 16)


def qkv_1(nc, ctx, ps, big, wq, wk, wv, bq, bk, bv, q1_scr):
    normT = big[2].rearrange("p (k s) -> p k s", k=KC)
    kT = big[1].rearrange("p (k s) -> p k s", k=KC)
    v1 = big[3].rearrange("p (t c) -> p t c", c=C)
    wts = [big[4][:, 512 * n:512 * n + 512].rearrange("p (k c) -> p k c", k=KC) for n in range(3)]
    bvb = big[4][:, 1536:2048]
    bcol = big[4][:, 2048:2052]
    qst = [big[4][:, 2560 + 512 * n:3072 + 512 * n] for n in range(4)]

    def sem(n):
        return ctx.enter_context(nc.semaphore("qkv1_" + n))

    loaded, ready, moved, stored = sem("loaded"), sem("ready"), sem("moved"), [sem(f"stored{n}") for n in range(4)]
    NQ = KC * ST
    NV = TT // 2

    def bank(n):
        return n % 8

    def product(n):
        for k in range(KC):
            if n < 2 * NQ:
                o, st = (n % NQ) // ST, n % ST
                yield (ps[:, bank(n), :], wts[n // NQ][:, k, P * o:P * o + P], normT[:, k, 512 * st:512 * st + 512], k)

    with nc.Block() as block:
        @block.sync
        def _(sp):
            for w, t in ((wq, wts[0]), (wk, wts[1]), (wv, wts[2])):
                sp.dma_start(t[:, :, :], w.rearrange("(k p) c -> p k c", p=P)).then_inc(loaded, 16)
            for n, b in enumerate((bq, bk)):
                sp.dma_start(bcol[:, 2 * n:2 * n + 2], b).then_inc(loaded, 16)
            sp.dma_start(bvb, bv).then_inc(loaded, 16)
            for n in range(NQ):
                o, st = n // ST, n % ST
                sp.wait_ge(moved, n + 1)
                sp.dma_start(q1_scr[4 * st:4 * st + 4, :, o, :].rearrange("t p s -> p t s"),
                             qst[n % 4].rearrange("p (t s) -> p t s", t=4)).then_inc(stored[n % 4], 16)
            for n in range(4):
                sp.wait_ge(stored[n], 16 * NQ // 4)

        @block.tensor
        def _(pe):
            pe.wait_ge(loaded, 96)
            for n in range(2 * NQ):
                if n >= 8:
                    pe.wait_ge(moved, n - 7)
                for o, l, r, k in product(n):
                    last = nc.tensor.matmul(o, l, r, start=(k == 0), stop=(k == KC - 1))
                last.then_inc(ready, 1)
            for m in range(NV):
                n = 2 * NQ + m
                pe.wait_ge(moved, n - 7)
                for u in range(2):
                    t = 2 * m + u
                    for k in range(KC):
                        last = nc.tensor.matmul(ps[:, bank(n), C * u:C * u + C], normT[:, k, P * t:P * t + P],
                                                wts[2][:, k, :], start=(k == 0), stop=(k == KC - 1))
                last.then_inc(ready, 1)

        @block.vector
        def _(dve):
            dve.wait_ge(loaded, 96)
            for n in range(2 * NQ + NV):
                dve.wait_ge(ready, n + 1)
                if n < 2 * NQ:
                    o, st = (n % NQ) // ST, n % ST
                    if n < NQ and n >= 4:
                        dve.wait_ge(stored[n % 4], 16 * (n // 4))
                    dst = qst[n % 4] if n < NQ else kT[:, o, 512 * st:512 * st + 512]
                    c = 2 * (n // NQ) + o
                    nc.vector.tensor_scalar(dst, ps[:, bank(n), :], bcol[:, c:c + 1], None, op0=ALU.add).then_inc(moved, 1)
                else:
                    m = n - 2 * NQ
                    nc.vector.tensor_tensor(out=big[3][:, 512 * m:512 * m + 512], in0=ps[:, bank(n), :], in1=bvb,
                                            op=ALU.add).then_inc(moved, 1)


def attention_1(nc, ctx, ps, big, ident, q1_scr):
    kT = big[1].rearrange("p (k s) -> p k s", k=KC)
    v1 = big[3].rearrange("p (t c) -> p t c", c=C)
    tok = big[5].rearrange("p (t c) -> p t c", c=C)
    score = [big[0][:, S * b:S * b + S] for b in range(2)]
    work = [big[2][:, S * b:S * b + S] for b in range(2)]
    wT = big[4][:, 0:S].rearrange("p (t s) -> p t s", t=TT)
    qT = [big[4][:, S + 256 * b:S + 256 * b + 256].rearrange("p (k s) -> p k s", k=KC) for b in range(2)]
    sm = big[4][:, S + 512:S + 640]
    top = [sm[:, 32 * b:32 * b + 32] for b in range(2)]
    negmax = [sm[:, 64 + b:65 + b] for b in range(2)]
    total = [sm[:, 66 + b:67 + b] for b in range(2)]
    CH = S // 512
    RING_S, RING_T = 4, 2
    PS_T, PS_A = 4, 6
    PAIRS = TT // 2 - 1

    def sem(n):
        return ctx.enter_context(nc.semaphore("a1_" + n))

    q_loaded = [sem("q_loaded_even"), sem("q_loaded_odd")]
    passed, s_ready, s_copied, top_step = sem("passed"), sem("s_ready"), sem("s_copied"), sem("top_step")
    exp_may, exp_done, w_ready = sem("exp_may"), sem("exp_done"), sem("w_ready")
    max_step, inv_step = sem("max_step"), sem("inv_step")
    t_ready, t_copied, o_ready, o_done = sem("t_ready"), sem("t_copied"), sem("o_ready"), sem("o_done")

    with nc.Block() as block:
        @block.sync
        def _(sp):
            for b in range(2):
                sp.dma_start(qT[b], q1_scr[b, :, :, :]).then_inc(q_loaded[b], 16)
            with sp.Fori(0, PAIRS) as r:
                for b in range(2):
                    sp.wait_ge(s_ready, r * (2 * CH) + CH * (b + 1))
                    sp.dma_start(qT[b], q1_scr[bass.ds(r * 2 + (b + 2), 1), :, :, :].rearrange("t p k s -> (t p) k s")
                                 ).then_inc(q_loaded[b], 16)

        @block.tensor
        def _(pe):
            pe.sem_inc(t_ready, CH + 1)
            pe.sem_inc(o_ready, 1)

            def scores(n, b, q_count):
                pe.wait_ge(q_loaded[b], q_count)
                for c in range(CH):
                    pe.wait_ge(s_copied, n * CH + (c + 1))
                    for k in range(KC):
                        last = nc.tensor.matmul(ps[:, c % RING_S, :], qT[b][:, k, :], kT[:, k, 512 * c:512 * c + 512],
                                                start=(k == 0), stop=(k == KC - 1))
                    last.then_inc(s_ready, 1)

            def values(n, b, c):
                pe.wait_ge(t_copied, n * CH + (RING_T + c + 1))
                if c == 0:
                    pe.wait_ge(o_done, n + 1)
                for t in range(4 * c, 4 * c + 4):
                    last = nc.tensor.matmul(ps[:, PS_A + b, 0:C], wT[:, t, :], v1[:, t, :], start=(t == 0), stop=(t == TT - 1))
                if c == CH - 1:
                    last.then_inc(o_ready, 1)

            def outputs(n, b):
                pe.wait_ge(w_ready, n + 1)
                for c in range(CH + 1):
                    if c < CH:
                        pe.wait_ge(t_copied, n * CH + (c + 1))
                        for u in range(4):
                            t = 4 * c + u
                            last = nc.tensor.transpose(ps[:, PS_T + c % RING_T, P * u:P * u + P],
                                                       work[b][:, P * t:P * t + P], ident)
                        last.then_inc(t_ready, 1)
                    if c >= 1:
                        values(n, b, c - 1)

            for b in range(2):
                scores(b, b, 16)
            with pe.Fori(0, PAIRS) as r:
                for b in range(2):
                    outputs(r * 2 + b, b)
                    scores(r * 2 + (b + 2), b, r * 16 + 32)
            for b in range(2):
                outputs(TT - 2 + b, b)

        @block.scalar
        def _(act):
            act.sem_inc(s_copied, RING_S)
            act.sem_inc(t_copied, RING_T)

            def copy_scores(n, b):
                for c in range(CH):
                    act.wait_ge(s_ready, n * CH + (c + 1))
                    nc.scalar.activation(score[b][:, 512 * c:512 * c + 512], ps[:, c % RING_S, :], ACT.Copy).then_inc(s_copied, 1)

            def exponentials(n, b):
                act.wait_ge(exp_may, n + 1)
                nc.scalar.activation(score[b], score[b], ACT.Exp, bias=negmax[b]).then_inc(exp_done, 1)

            def copy_weights(n, b):
                act.wait_ge(o_ready, n + 1)
                for c in range(CH):
                    act.wait_ge(t_ready, n * CH + (CH + c + 2))
                    nc.scalar.activation(big[4][:, 512 * c:512 * c + 512], ps[:, PS_T + c % RING_T, :], ACT.Copy).then_inc(t_copied, 1)

            copy_scores(0, 0)
            exponentials(0, 0)
            copy_scores(1, 1)
            with act.Fori(0, PAIRS) as r:
                for b in range(2):
                    n = r * 2 + b
                    copy_weights(n, b)
                    copy_scores(n + 2, b)
                    exponentials(n + 1, 1 - b)
            copy_weights(TT - 2, 0)
            exponentials(TT - 1, 1)
            copy_weights(TT - 1, 1)

        @block.vector
        def _(dve):
            dve.sem_inc(o_done, 2)
            STEPS = 7

            def pass_waits():
                dve.sem_inc(passed, 1)

            def take_top(n, b):
                ch = Chain(dve, top_step, n * STEPS)
                dve.wait_ge(s_copied, n * CH + (RING_S + CH))
                dve.wait_ge(t_ready, n * CH + 1)
                for a in range(TOPK // 8):
                    src = score[b] if a == 0 else work[b]
                    pass_waits()
                    ch.link(nc.vector.max(top[b][:, 8 * a:8 * a + 8], src))
                    if a == 0:
                        nc.vector.tensor_scalar(negmax[b], top[b][:, 0:1], -1.0, None, op0=ALU.mult).then_inc(max_step, 1)
                        dve.wait_ge(max_step, n + 1)
                    pass_waits()
                    ins = nc.vector.match_replace(work[b], top[b][:, 8 * a:8 * a + 8], src, TAKEN)
                    if a == 0:
                        ins.then_inc(exp_may, 1)
                        dve.wait_ge(exp_may, n + 1)
                    else:
                        ch.link(ins)
                assert ch.n == STEPS
                dve.wait_ge(exp_done, n + 1)
                dve.wait_ge(o_done, n + 1)
                nc.vector.scalar_tensor_tensor(out=work[b], in0=work[b], scalar=TAKEN, in1=score[b],
                                               op0=ALU.is_equal, op1=ALU.mult, accum_out=total[b]).then_inc(w_ready, 1)

            def add_output(n, b):
                dve.wait_ge(w_ready, n + 1)
                nc.vector.reciprocal(total[b], total[b]).then_inc(inv_step, 1)
                dve.wait_ge(inv_step, n + 1)
                dve.wait_ge(o_ready, n + 2)
                t = tok[:, bass.ds(n, 1), :].rearrange("p t c -> p (t c)")
                nc.vector.scalar_tensor_tensor(out=t, in0=ps[:, PS_A + b, 0:C], scalar=total[b], in1=t,
                                               op0=ALU.mult, op1=ALU.add).then_inc(o_done, 1)

            take_top(0, 0)
            with dve.Fori(0, PAIRS) as r:
                for b in range(2):
                    take_top(r * 2 + (b + 1), 1 - b)
                    add_output(r * 2 + b, b)
            take_top(TT - 1, 1)
            add_output(TT - 2, 0)
            add_output(TT - 1, 1)


def norm_and_gate(nc, ctx, ps, big, cst, eps, gate, wg, bg, b2):
    tok = big[5].rearrange("p (t c) -> p t c", c=C)
    normT = big[2].rearrange("p (k s) -> p k s", k=KC)
    with nc.Block() as block:
        layer_norm_tiles(nc, block, ctx, "ln2_", tok, normT, eps, cst, ps, big[3], big[4][:, 0:64], None, None)

    area = big[4]
    wg_t = area[:, 64:64 + KC * NE].rearrange("p (k e) -> p k e", k=KC)
    bg_t = area[:, 80:80 + NE]
    b2_t = area[0:NE, 128:128 + C]
    logit = area[:, 512:768].rearrange("p (t e) -> p t e", e=NE)
    best = area[:, 768:1024].rearrange("p (t e) -> p t e", e=NE)
    where = area[:, 1024:1280].bitcast(U32).rearrange("p (t e) -> p t e", e=NE)
    wheref = area[:, 1280:1344].rearrange("p (t e) -> p t e", e=2)
    pair = area[:, 1344:1408].rearrange("p (t e) -> p t e", e=2)
    hit = area[:, 1408:1664].rearrange("p (t e) -> p t e", e=NE)
    gateT = big[3][0:NE, 0:S]
    iota = cst[:, C_IOTA:C_IOTA + NE]

    def sem(n):
        return ctx.enter_context(nc.semaphore("gate_" + n))

    loaded, logits, step, diff, ratio, gates = sem("loaded"), sem("logits"), sem("step"), sem("diff"), sem("ratio"), sem("gates")
    turned, turned_copied, b2_ready, b2_added = sem("turned"), sem("turned_copied"), sem("b2_ready"), sem("b2_added")

    with nc.Block() as block:
        @block.sync
        def _(sp):
            sp.dma_start(wg_t[:, :, :], wg.rearrange("(k p) e -> p k e", p=P)).then_inc(loaded, 16)
            sp.dma_start(bg_t, bg).then_inc(loaded, 16)
            sp.dma_start(b2_t, b2).then_inc(loaded, 16)

        @block.tensor
        def _(pe):
            pe.wait_ge(loaded, 48)
            for t in range(TT):
                for k in range(KC):
                    last = nc.tensor.matmul(ps[:, 0, NE * t:NE * t + NE], normT[:, k, P * t:P * t + P], wg_t[:, k, :],
                                            start=(k == 0), stop=(k == KC - 1))
            last.then_inc(logits, 1)
            pe.wait_ge(gates, 1)
            for n in range(TT // 4):
                if n >= 2:
                    pe.wait_ge(turned_copied, n - 1)
                for u in range(4):
                    last = nc.tensor.transpose(ps[0:NE, 1 + n % 2, P * u:P * u + P], gate[:, 4 * n + u, :], cst[:, C_ID:C_ID + P])
                last.then_inc(turned, 1)
            for n in range(TT // 2):
                pe.wait_ge(turned_copied, n // 2 + 1)
                if n >= 4:
                    pe.wait_ge(b2_added, n - 3)
                for u in range(2):
                    t = 2 * n + u
                    last = nc.tensor.matmul(ps[:, 4 + n % 4, C * u:C * u + C], gateT[:, P * t:P * t + P], b2_t,
                                            start=True, stop=True)
                last.then_inc(b2_ready, 1)

        @block.scalar
        def _(act):
            act.wait_ge(diff, 1)
            nc.scalar.activation(pair[:, :, 1], pair[:, :, 1], ACT.Exp).then_inc(ratio, 1)
            for n in range(TT // 4):
                act.wait_ge(turned, n + 1)
                nc.scalar.activation(gateT[:, 512 * n:512 * n + 512], ps[0:NE, 1 + n % 2, :], ACT.Copy).then_inc(turned_copied, 1)

        @block.vector
        def _(dve):
            ch = Chain(dve, step)
            dve.wait_ge(loaded, 48)
            dve.wait_ge(logits, 1)
            ch.link(nc.vector.tensor_tensor(out=logit[:, :, :], in0=ps[:, 0, 0:TT * NE].rearrange("p (t e) -> p t e", e=NE),
                                            in1=bg_t.unsqueeze(1).to_broadcast([P, TT, NE]), op=ALU.add))
            for t in range(TT):
                ch.step(nc.vector.max(best[:, t, :], logit[:, t, :]))
            ch.wait()
            for t in range(TT):
                ch.step(nc.vector.max_index(where[:, t, :], best[:, t, :], logit[:, t, :]))
            ch.wait()
            ch.step(nc.vector.tensor_copy(wheref[:, :, :], where[:, :, 0:2]))
            nc.vector.tensor_tensor(out=pair[:, :, 1], in0=best[:, :, 1], in1=best[:, :, 0], op=ALU.subtract).then_inc(diff, 1)
            dve.wait_ge(ratio, 1)
            ch.link(nc.vector.tensor_scalar(pair[:, :, 0], pair[:, :, 1], 1.0, None, op0=ALU.add))
            ch.link(nc.vector.reciprocal(pair[:, :, 0], pair[:, :, 0]))
            ch.link(nc.vector.tensor_tensor(out=pair[:, :, 1], in0=pair[:, :, 1], in1=pair[:, :, 0], op=ALU.mult))
            for a, dst in ((0, gate), (1, hit)):
                ch.link(nc.vector.tensor_tensor(out=dst[:, :, :], in0=iota.unsqueeze(1).to_broadcast([P, TT, NE]),
                                                in1=wheref[:, :, a:a + 1].to_broadcast([P, TT, NE]), op=ALU.is_equal))
                ch.link(nc.vector.tensor_tensor(out=dst[:, :, :], in0=dst[:, :, :],
                                                in1=pair[:, :, a:a + 1].to_broadcast([P, TT, NE]), op=ALU.mult))
            nc.vector.tensor_tensor(out=gate[:, :, :], in0=gate[:, :, :], in1=hit[:, :, :], op=ALU.add).then_inc(gates, 1)
            for n in range(TT // 2):
                dve.wait_ge(b2_ready, n + 1)
                two = big[5][:, 512 * n:512 * n + 512]
                nc.vector.tensor_tensor(out=two, in0=two, in1=ps[:, 4 + n % 4, :], op=ALU.add).then_inc(b2_added, 1)


def experts(nc, ctx, ps, big, gate, w1, b1, w2, out):
    tok = big[5].rearrange("p (t c) -> p t c", c=C)
    normT = big[2].rearrange("p (k s) -> p k s", k=KC)
    w1_t = [big[0][:, 2048 * b:2048 * b + 2048].rearrange("p (k h) -> p k h", k=KC) for b in range(2)]
    w2_t = [big[0][:, 4096 + 2048 * b:6144 + 2048 * b].rearrange("p (h c) -> p h c", h=HC) for b in range(2)]
    b1_t = [big[4][:, HC * b:HC * b + HC] for b in range(2)]
    hT = [big[1][:, 4096 * b:4096 * b + 4096].rearrange("p (h s) -> p h s", h=HC) for b in range(2)]
    RING_H, PS_O = 4, 4

    def sem(n):
        return ctx.enter_context(nc.semaphore("ffn_" + n))

    w_loaded = [sem("w_loaded_even"), sem("w_loaded_odd")]
    h_ready, h_done, o_ready, o_added, stored = sem("h_ready"), sem("h_done"), sem("o_ready"), sem("o_added"), sem("stored")

    with nc.Block() as block:
        @block.sync
        def _(sp):
            def load(eb, expert, chunks):
                sp.dma_start(w1_t[eb][:, :, :], w1[expert, :, :].rearrange("e (k p) h -> p (e k) h", p=P)).then_inc(w_loaded[eb], 16)
                sp.dma_start(b1_t[eb], b1[:, chunks]).then_inc(w_loaded[eb], 16)
                sp.dma_start(w2_t[eb][:, :, :], w2[expert, :, :].rearrange("e (h p) c -> p (e h) c", p=P)).then_inc(w_loaded[eb], 16)

            for eb in range(2):
                load(eb, bass.ds(eb, 1), bass.ds(eb * HC, HC))
            with sp.Fori(0, NE // 2 - 1) as ep:
                for eb in range(2):
                    sp.wait_ge(o_ready, ep * (2 * ST) + (2 + ST * (eb + 1)))
                    load(eb, bass.ds(ep * 2 + (eb + 2), 1), bass.ds(ep * (2 * HC) + (eb + 2) * HC, HC))
            sp.wait_ge(o_added, 8 + NE * TT)
            sp.dma_start(out.rearrange("(t p) c -> p t c", p=P), tok[:, :, :]).then_inc(stored, 16)
            sp.wait_ge(stored, 16)

        @block.tensor
        def _(pe):
            pe.sem_inc(o_ready, 2)
            with pe.Fori(0, NE // 2) as ep:
                for eb in range(2):
                    with pe.Fori(0, ST // 2) as tp:
                        pe.wait_ge(w_loaded[eb], ep * 48 + 48)
                        base = ep * (2 * ST) + tp * 2 + ST * eb
                        for b in range(2):
                            m = base + b
                            for h in range(HC):
                                pe.wait_ge(h_done, m * HC + (h + 1))
                                for k in range(KC):
                                    last = nc.tensor.matmul(ps[:, h % RING_H, :], w1_t[eb][:, k, P * h:P * h + P],
                                                            normT[:, k, bass.ds(tp * 1024 + 512 * b, 512)],
                                                            start=(k == 0), stop=(k == KC - 1))
                                last.then_inc(h_ready, 1)
                        for b in range(2):
                            m = base + b
                            pe.wait_ge(h_done, m * HC + (RING_H + HC))
                            pe.wait_ge(o_added, m * 4 + 4)
                            for t in range(4):
                                for h in range(HC):
                                    last = nc.tensor.matmul(ps[:, PS_O + 2 * b + t // 2, C * (t % 2):C * (t % 2) + C],
                                                            hT[b][:, h, P * t:P * t + P], w2_t[eb][:, h, :],
                                                            start=(h == 0), stop=(h == HC - 1))
                            last.then_inc(o_ready, 1)

        @block.scalar
        def _(act):
            act.sem_inc(h_done, RING_H)
            with act.Fori(0, NE // 2) as ep:
                for eb in range(2):
                    with act.Fori(0, ST // 2) as tp:
                        for b in range(2):
                            m = ep * (2 * ST) + tp * 2 + (ST * eb + b)
                            act.wait_ge(o_ready, m + 1)
                            act.wait_ge(w_loaded[eb], ep * 48 + 48)
                            for h in range(HC):
                                act.wait_ge(h_ready, m * HC + (h + 1))
                                nc.scalar.activation(hT[b][:, h, :], ps[:, h % RING_H, :], ACT.Gelu,
                                                     bias=b1_t[eb][:, h:h + 1]).then_inc(h_done, 1)

        @block.vector
        def _(dve):
            dve.sem_inc(o_added, 8)
            with dve.Fori(0, NE // 2) as ep:
                for eb in range(2):
                    with dve.Fori(0, ST // 2) as tp:
                        for b in range(2):
                            m = ep * (2 * ST) + tp * 2 + (ST * eb + b)
                            dve.wait_ge(o_ready, m + 3)
                            dve.wait_ge(o_added, m * 4 + 8)
                            for t in range(4):
                                i = tp * 8 + (4 * b + t)
                                o = tok[:, bass.ds(i, 1), :].rearrange("p t c -> p (t c)")
                                g = gate[:, bass.ds(i, 1), bass.ds(ep * 2 + eb, 1)].rearrange("p t e -> p (t e)")
                                nc.vector.scalar_tensor_tensor(
                                    out=o, in0=ps[:, PS_O + 2 * b + t // 2, C * (t % 2):C * (t % 2) + C], scalar=g, in1=o,
                                    op0=ALU.mult, op1=ALU.add).then_inc(o_added, 1)


def constants():
    c = np.zeros((P, C_N), np.float32)
    i = np.arange(P)
    c[:, C_ID:C_ID + P] = np.eye(P)
    c[:, C_GROUP:C_GROUP + P] = (i[:, None] // 8 == i[None, :] // 8) / 8.0
    c[:, C_HEAD:C_HEAD + P] = i[:, None] // D == i[None, :] // D
    c[:, C_FOLD:C_FOLD + D] = i[:, None] % D == np.arange(D)[None, :]
    c[:, C_ONE] = 1.0
    c[:, C_SEL] = i % 32 == 0
    c[:, C_IOTA:C_IOTA + NE] = np.arange(NE)
    return c


def kernel(**inputs):
    import concourse.bacc as bacc
    from concourse.bass_utils import run_bass_kernel_spmd

    a = {k: np.asarray(v) for k, v in inputs.items()}
    x = a["x"].reshape(C, S)
    t = a["L0_conv_temperature"].reshape(HEADS)

    def columns(v):
        return v.reshape(-1, P).T

    def rows(v):
        return np.broadcast_to(v.reshape(1, -1), (P, v.size))

    arrays = {
        "x": x, "xT": x.T, "wqkvT": a["L0_conv_w_qkv"].T, "wprojT": a["L0_conv_w_proj"].T,
        "t_col": columns(np.repeat(t, D)), "t_row": rows(t),
        "wq": a["L1_attn_Wq"], "wk": a["L1_attn_Wk"], "wv": a["L1_attn_Wv"],
        "bq": columns(a["L1_attn_bq"]), "bk": columns(a["L1_attn_bk"]),
        "bv": np.concatenate([rows(a["L1_attn_bv"])] * 2, axis=1),
        "wg": a["L1_ffn_Wg"], "bg": rows(a["L1_ffn_bg"]),
        "w1": a["L1_ffn_W1"], "b1": columns(a["L1_ffn_b1"]), "w2": a["L1_ffn_W2"], "b2": a["L1_ffn_b2"],
        "consts": constants(),
    }
    arrays = {k + "_in": np.ascontiguousarray(v) for k, v in arrays.items()}
    nc = bacc.Bacc("TRN2", target_bir_lowering=False, num_devices=1)
    args = [nc.dram_tensor(k, v.shape, mybir.dt.from_np(v.dtype), kind="ExternalInput").ap() for k, v in arrays.items()]
    out = nc.dram_tensor("out", (S, C), F32, kind="ExternalOutput").ap()
    build(nc, *args, out)
    r = run_bass_kernel_spmd(nc, [arrays], core_ids=[0])
    return r.results[0]["out"].T.reshape(1, C, 64, 64)
```

```python
from contextlib import ExitStack

import numpy as np

import concourse.bass as bass
from concourse import mybir

P = 128
F32 = mybir.dt.float32
F16 = mybir.dt.float16
U32 = mybir.dt.uint32
I32 = mybir.dt.int32
ALU = mybir.AluOpType
ACT = mybir.ActivationFunctionType
AX_X = mybir.AxisListType.X

C = 256
S = 4096
HEADS = 8
D = C // HEADS
KC = C // P
TT = S // P
ST = S // 512
SUB = S // C
NE = 8
HID = 1024
HC = HID // P
TOPK = 32
GN_EPS = 1e-5
LN_EPS = 1e-5
NORM_EPS = 1e-12
SQ = 4
SLOT = SQ * P
NS = (2 * S + NE * (SLOT - 1)) // SLOT
NK = -(-S // SLOT)
TAKEN = -3.0e38

C_ID, C_GROUP, C_HEAD, C_FOLD, C_IOTA = 0, 128, 256, 384, 416
C_BEFORE, C_ALL = 424, 552
C_STEP = C_ALL + P
C_SLOT = C_STEP + NK
C_N = C_SLOT + NS
assert NS % 2 == 1


class Chain:

    def __init__(self, eng, sem, base=0):
        self.eng, self.sem, self.base, self.n = eng, sem, base, 0

    def step(self, ins):
        ins.then_inc(self.sem, 1)
        self.n += 1

    def wait(self):
        self.eng.wait_ge(self.sem, self.base + self.n)

    def link(self, ins):
        self.step(ins)
        self.wait()


def build(nc, x, xT, wqkvT, wprojT, t_col, t_row, wq, wk, wv, bq, bk, bv, wg, bg, w1, b1, w2, b2, consts, out):
    qk_scr = nc.dram_tensor("qk_scr", (2, 2, C, S), F16, kind="Internal").ap()
    q1_scr = nc.dram_tensor("q1_scr", (TT, P, KC, P), F32, kind="Internal").ap()
    x_slots = nc.dram_tensor("x_slots", (NS * SLOT, C), F32, kind="Internal").ap()
    y_slots = nc.dram_tensor("y_slots", (NS * SLOT, C), F32, kind="Internal").ap()
    with ExitStack() as ctx:
        def sb(name, shape, dt=F32):
            return ctx.enter_context(nc.sbuf_tensor(name, shape, dt))

        big = [sb(f"big{i}", [P, 8192]) for i in range(6)]
        cst = sb("cst", [P, C_N])
        ident = cst[:, C_ID:C_ID + P]
        negt = sb("negt", [P, HEADS])
        eps = sb("eps", [P, 2])
        weight = sb("weight", [P, TT, 2])
        position = [sb(f"position{a}", [P, TT], U32) for a in range(2)]
        slot_expert = sb("slot_expert", [P, NS], I32)
        ps = ctx.enter_context(nc.psum_tensor("ps", [P, 8, 512], F32))
        group_norm_and_qkv(nc, ctx, ps, big, cst, eps, negt, x, wqkvT, t_col, t_row, consts, qk_scr)
        attention_0(nc, ctx, ps, big, cst, negt, qk_scr, x_slots)
        project_and_norm(nc, ctx, ps, big, cst, eps, xT, wprojT)
        qkv_1(nc, ctx, ps, big, wq, wk, wv, bq, bk, bv, q1_scr)
        attention_1(nc, ctx, ps, big, ident, q1_scr)
        norm_and_route(nc, ctx, ps, big, cst, eps, weight, position, slot_expert, wg, bg, b2, x_slots)
        experts(nc, ctx, ps, big, ident, slot_expert, w1, b1, w2, x_slots, y_slots)
        combine(nc, ctx, big, weight, position, y_slots, out)


def group_norm_and_qkv(nc, ctx, ps, big, cst, eps, negt, x, wqkvT, t_col, t_row, consts, qk_scr):
    RING = 4
    xn = big[2].rearrange("p (k s) -> p k s", k=KC)
    w = big[3][:, 0:KC * 3 * C].rearrange("p (k o) -> p k o", k=KC)
    stage = big[4]
    sq, y = ([stage[:, 1024 * a + 512 * b:1024 * a + 512 * b + 512] for b in range(2)] for a in range(2))
    hi, lo = ([stage[:, 2048 + 512 * a + 256 * b:2304 + 512 * a + 256 * b].bitcast(F16) for b in range(2)] for a in range(2))
    ssT = [stage[:, 3072 + 512 * b:3584 + 512 * b].rearrange("p (g d) -> p g d", d=D) for b in range(RING)]
    inv = [stage[:, 5120 + 512 * b:5632 + 512 * b].rearrange("p (g d) -> p g d", d=D) for b in range(2)]
    nrm = [big[5][:, 256 + 16 * b:272 + 16 * b] for b in range(RING)]
    small = big[5]
    stats = small[:, 0:96].rearrange("p (k g n) -> p k g n", k=KC, n=6)
    mv = small[:, 96:100].rearrange("p (k n) -> p k n", k=KC)
    dev = small[:, 100:102]
    var = small[:, 102:104]
    rstd = small[:, 104:106]
    shift = small[:, 106:108]
    gmean = small[:, 108:112].rearrange("p (k n) -> p k n", k=KC)
    tcol = small[:, 112:114]
    trow = small[:, 114:122]

    def sem(name):
        return ctx.enter_context(nc.semaphore(name))

    loaded_x = [sem("loaded_x0"), sem("loaded_x1")]
    loaded_w, loaded_c = sem("loaded_w"), sem("loaded_c")
    gn_step = sem("gn_step")
    stats_ready, gmean_ready, dev_ready, gvar_ready = sem("stats_ready"), sem("gmean_ready"), sem("dev_ready"), sem("gvar_ready")
    var_ready, std_ready, xn_ready = sem("var_ready"), sem("std_ready"), sem("xn_ready")
    qk_ready, sq_ready, ss_ready, nrm_ready = sem("qk_ready"), sem("sq_ready"), sem("ss_ready"), sem("nrm_ready")
    hi_ready, turned = sem("hi_ready"), sem("turned")
    y_step, split_ready, split_stored = sem("y_step"), sem("split_ready"), [sem("split_stored_even"), sem("split_stored_odd")]
    v_ready, v_copied = sem("v_ready"), sem("v_copied")

    with nc.Block() as block:
        @block.sync
        def _(sp):
            for k in range(KC):
                sp.dma_start(xn[:, k, :], x[P * k:P * k + P, :]).then_inc(loaded_x[k], 16)
            sp.dma_start(w[:, :, :], wqkvT.rearrange("(k p) o -> p k o", p=P)).then_inc(loaded_w, 16)
            for b in range(2):
                sp.sem_inc(split_stored[b], 16)
            for ot in range(4):
                with sp.Fori(0, ST // 2) as i:
                    for b in range(2):
                        sp.wait_ge(split_ready, (i * 2 + b) + (ot * ST + 1))
                        for part, src in ((0, hi[b]), (1, lo[b])):
                            sp.dma_start(qk_scr[ot // 2, part, P * (ot % 2):P * (ot % 2) + P,
                                                bass.ds(i * 1024 + b * 512, 512)], src).then_inc(split_stored[b], 16)
            for b in range(2):
                sp.wait_ge(split_stored[b], 16 + 32 * 4 * ST // 2)

        @block.gpsimd
        def _(pool):
            pool.dma_start(cst[:, :], consts).then_inc(loaded_c, 16)
            pool.dma_start(tcol, t_col).then_inc(loaded_c, 16)
            pool.dma_start(trow, t_row).then_inc(loaded_c, 16)
            for ot in range(4):
                with pool.Fori(0, ST // 2) as i:
                    for b in range(2):
                        pool.wait_ge(hi_ready, i * 2 + (b + ot * ST + 1))
                        nc.gpsimd.tensor_tensor(out=lo[b], in0=y[b], in1=hi[b], op=ALU.subtract).then_inc(split_ready, 1)

        @block.vector
        def _(dve):
            dve.sem_inc(y_step, 13)
            ch = Chain(dve, gn_step)
            ch.step(nc.vector.memset(eps[:, 0:1], GN_EPS))
            ch.step(nc.vector.memset(eps[:, 1:2], LN_EPS))
            dve.wait_ge(loaded_c, 48)
            ch.link(nc.vector.tensor_scalar(negt[:, :], trow, -1.0, None, op0=ALU.mult))
            ch.step(nc.vector.tensor_tensor(out=negt[:, :], in0=negt[:, :], in1=trow, op=ALU.min))
            for k in range(KC):
                dve.wait_ge(loaded_x[k], 16)
                for g in range(ST):
                    ch.step(nc.vector.bn_stats(stats[:, k, g, :], xn[:, k, 512 * g:512 * g + 512]))
            ch.wait()
            for k in range(KC):
                nc.vector.bn_aggr(mv[:, k, :], stats[:, k, :, :]).then_inc(stats_ready, 1)
            dve.wait_ge(gmean_ready, 1)
            dve.wait_ge(stats_ready, KC)
            ch.link(nc.vector.tensor_copy(gmean[:, :, :], ps[:, 0, 0:4].rearrange("p (k n) -> p k n", k=KC)))
            ch.link(nc.vector.tensor_tensor(out=dev, in0=mv[:, :, 0], in1=gmean[:, :, 0], op=ALU.subtract))
            nc.vector.tensor_tensor(out=dev, in0=dev, in1=dev, op=ALU.mult).then_inc(dev_ready, 1)
            dve.wait_ge(gvar_ready, 1)
            nc.vector.tensor_tensor(out=var, in0=gmean[:, :, 1], in1=ps[:, 1, 0:2], op=ALU.add).then_inc(var_ready, 1)
            dve.wait_ge(std_ready, 1)
            ch.link(nc.vector.reciprocal(rstd, var))
            for k in range(KC):
                nc.vector.tensor_scalar(xn[:, k, :], xn[:, k, :], gmean[:, k, 0:1], rstd[:, k:k + 1],
                                        op0=ALU.subtract, op1=ALU.mult).then_inc(xn_ready, 1)
            def turn(n, b):
                dve.wait_ge(ss_ready, n + 3)
                nc.vector.transpose(ssT[b], ps[:, RING + b % 2, :].rearrange("p (g d) -> p g d", d=D)).then_inc(turned, 1)

            def normalise(n, b, ot, stored):
                yc = Chain(dve, y_step, n * 4 + 13)
                dve.wait_ge(nrm_ready, n + 1)
                yc.link(nc.vector.tensor_scalar(nrm[b], nrm[b], NORM_EPS, None, op0=ALU.max))
                yc.link(nc.vector.reciprocal(nrm[b], nrm[b]))
                yc.link(nc.vector.transpose(inv[b % 2], nrm[b].unsqueeze(2).to_broadcast([P, 16, D])))
                dve.wait_ge(split_stored[b % 2], stored)
                yc.link(nc.vector.scalar_tensor_tensor(
                    out=y[b % 2], in0=ps[:, b, :], scalar=tcol[:, ot:ot + 1] if ot < 2 else 1.0,
                    in1=inv[b % 2].rearrange("p g d -> p (g d)"), op0=ALU.mult, op1=ALU.mult))
                nc.vector.tensor_copy(hi[b % 2], y[b % 2]).then_inc(hi_ready, 1)

            for ot in range(4):
                with dve.Fori(0, ST // RING) as i:
                    for b in range(RING + 1):
                        if b < RING:
                            turn(i * RING + (b + ot * ST), b)
                        if b > 0:
                            normalise(i * RING + (b - 1 + ot * ST), b - 1, ot, i * (16 * RING) + (16 + 16 * (ot * ST + (b - 1) // 2 * 2)))

        @block.scalar
        def _(act):
            act.wait_ge(var_ready, 1)
            act.wait_ge(gn_step, 1)
            nc.scalar.activation(var, var, ACT.Sqrt, bias=eps[:, 0:1]).then_inc(std_ready, 1)
            for ot in range(4):
                with act.Fori(0, ST // RING) as i:
                    for b in range(RING + 1):
                        n = i * RING + (b + ot * ST)
                        if b < RING:
                            act.wait_ge(qk_ready, n + 1)
                            act.wait_ge(ss_ready, n + 1)
                            nc.scalar.activation(sq[b % 2], ps[:, b, :], ACT.Square).then_inc(sq_ready, 1)
                        if b > 0:
                            act.wait_ge(turned, n + 2)
                            nc.scalar.activation(nrm[b - 1], ssT[b - 1][:, :, 0], ACT.Sqrt).then_inc(nrm_ready, 1)
            for t in range(TT // 2):
                act.wait_ge(v_ready, t + 1)
                nc.scalar.activation(big[0][:, 512 * t:512 * t + 512], ps[:, 6 + t % 2, :], ACT.Copy).then_inc(v_copied, 1)

        @block.tensor
        def _(pe):
            pe.sem_inc(ss_ready, 2)
            pe.sem_inc(turned, 2)
            pe.wait_ge(loaded_c, 48)
            pe.wait_ge(stats_ready, KC)
            nc.tensor.matmul(ps[:, 0, 0:4], cst[:, C_GROUP:C_GROUP + P], mv[:, :, :].rearrange("p k n -> p (k n)"),
                             start=True, stop=True).then_inc(gmean_ready, 1)
            pe.wait_ge(dev_ready, 1)
            nc.tensor.matmul(ps[:, 1, 0:2], cst[:, C_GROUP:C_GROUP + P], dev, start=True, stop=True).then_inc(gvar_ready, 1)
            pe.wait_ge(loaded_w, 16)
            pe.wait_ge(xn_ready, KC)
            for ot in range(4):
                with pe.Fori(0, ST // RING) as i:
                    for b in range(RING + 1):
                        n = i * RING + (b + ot * ST)
                        if b < RING:
                            pe.wait_ge(y_step, n * 4 + 1)
                            for k in range(KC):
                                last = nc.tensor.matmul(ps[:, b, :], w[:, k, P * ot:P * ot + P],
                                                        xn[:, k, bass.ds(i * (512 * RING) + b * 512, 512)],
                                                        start=(k == 0), stop=(k == KC - 1))
                            last.then_inc(qk_ready, 1)
                        if b > 0:
                            pe.wait_ge(sq_ready, n)
                            pe.wait_ge(turned, n)
                            nc.tensor.matmul(ps[:, RING + (b - 1) % 2, :], cst[:, C_HEAD:C_HEAD + P], sq[(b - 1) % 2],
                                             start=True, stop=True).then_inc(ss_ready, 1)
            for t in range(TT // 2):
                if t >= 2:
                    pe.wait_ge(v_copied, t - 1)
                for u in range(2):
                    for k in range(KC):
                        last = nc.tensor.matmul(ps[:, 6 + t % 2, 256 * u:256 * u + 256],
                                                xn[:, k, P * (2 * t + u):P * (2 * t + u) + P], w[:, k, 2 * C:3 * C],
                                                start=(k == 0), stop=(k == KC - 1))
                last.then_inc(v_ready, 1)


def attention_0(nc, ctx, ps, big, cst, negt, qk_scr, x_slots):
    TILES = ST // 2
    GROUPS = TT // 4
    NG = TILES * GROUPS
    NU = 2 * NG
    RUNS = 2 * HEADS
    RING_S, RING_P = 3, 4
    LAG = 2
    FOLD_AT = 4
    v0 = big[0].rearrange("p (t c) -> p t c", c=C)
    image = big[1].rearrange("p (f j c) -> p f j c", f=2, j=SUB)
    kst = [big[2][:, 2048 * b:2048 * b + 2048].bitcast(F16) for b in range(2)]
    qst = [big[2][:, 4096 + 2048 * b:6144 + 2048 * b].bitcast(F16) for b in range(2)]
    probs = big[3].rearrange("p (r t s) -> p r t s", r=RING_P, t=4)
    vh = [big[4][:, 1024 * b:1024 * b + 1024].rearrange("p (t d) -> p t d", d=D) for b in range(2)]
    outT = big[4][:, 2048:4096]
    den = big[4][:, 4096:6144]
    tmp = [big[5][:, 1024 * b:1024 * b + 1024] for b in range(2)]
    acc = big[5][:, 2048:3072]
    ones = big[5][:, 3072:3104]
    rden = big[5][:, 3136:3136 + SUB]
    numT, denT, quot = (big[5][:, 3648 + 512 * b:4160 + 512 * b] for b in range(3))
    bound = [big[5][:, 3104 + b:3105 + b] for b in range(2)]
    PS_O, PS_D = 6, 7
    FILLS = 8
    fill = NS * SLOT * C // P // FILLS
    zeros = big[5][:, 5184:5184 + fill]
    assert 5184 + fill <= 8192 and fill * FILLS * P == NS * SLOT * C

    def by_pe(g):
        return g % 4 == 3

    upto = [sum(not by_pe(a) for a in range(g + 1)) for g in range(NG)]
    NDV = upto[-1]
    upto = {g: upto[g] if g >= 0 else upto[g + NG] - NDV for g in range(-NG, NG)}

    FOLD_PLACE = 2 * FOLD_AT
    PLACES = NU + 2
    assert PLACES % RING_S == 0

    def place(u):
        return u if u < FOLD_PLACE else u + 1

    def holder_before(p):
        p -= RING_S
        while p == -1:
            p -= RING_S
        if p == FOLD_PLACE:
            return "fold"
        if p < 0:
            return p + PLACES - 1 - NU
        return p if p < FOLD_PLACE else p - 1

    def runs(eng, body):
        body(0, 0, 0, 0)
        with eng.Fori(0, RUNS // 4 - 1) as i:
            for k in (1, 2, 3, 4):
                body(i * 4 + k, i + k // 4, k // 2 % 2, k % 2)
        for n in range(RUNS - 3, RUNS):
            body(n, n // 4, n // 2 % 2, n % 2)

    def sem(name):
        return ctx.enter_context(nc.semaphore(name))

    heads_loaded = [sem("heads_loaded_even"), sem("heads_loaded_odd")]
    vh_ready, zeros_ready, filled = sem("vh_ready"), sem("zeros_ready"), sem("filled")
    s_ready, exp_done, pv_done, sum_done = sem("s_ready"), sem("exp_done"), sem("pv_done"), sem("sum_done")
    sum_step, ones_ready = sem("sum_step"), sem("ones_ready")
    o_copied, den_done, acc_done = sem("o_copied"), sem("den_done"), sem("acc_done")
    fold_done, image_done, rden_done = sem("fold_done"), sem("image_done"), sem("rden_done")
    quot_done, turn_done = sem("quot_done"), sem("turn_done")

    with nc.Block() as block:
        @block.sync
        def _(sp):
            def load(hb, rows):
                for a in range(2):
                    for part in range(2):
                        at = 64 * a + 32 * part
                        sp.dma_start(qst[hb][at:at + D, :], qk_scr[0, part, rows, :]).then_inc(heads_loaded[hb], 16)
                        sp.dma_start(kst[hb][at:at + D, :], qk_scr[1, a, rows, :]).then_inc(heads_loaded[hb], 16)

            for hb in range(2):
                load(hb, bass.ds(hb * D, D))
            sp.wait_ge(zeros_ready, 1)
            for f in range(FILLS):
                sp.dma_start(x_slots.rearrange("(p r) c -> p (r c)", p=P)[:, fill * f:fill * f + fill], zeros).then_inc(filled, 16)
            sp.wait_ge(filled, 16 * FILLS)
            with sp.Fori(0, HEADS // 2 - 1) as hp:
                for hb in range(2):
                    sp.wait_ge(fold_done, hp * 4 + (1 + 2 * (hb + 1)))
                    load(hb, bass.ds(hp * 2 * D + (hb + 2) * D, D))

        @block.gpsimd
        def _(pool):
            def load(hb, head, cols):
                nc.gpsimd.tensor_copy(bound[hb], negt[:, head]).then_inc(vh_ready, 1)
                nc.gpsimd.tensor_copy(vh[hb], v0[:, :, cols]).then_inc(vh_ready, 1)

            for hb in range(2):
                load(hb, bass.ds(hb, 1), bass.ds(hb * D, D))
            nc.gpsimd.memset(zeros, 0.0).then_inc(zeros_ready, 1)

            def rows(n, hp, hb, half):
                pool.wait_ge(quot_done, n + 1)
                nc.gpsimd.tensor_copy(image[:, half, :, bass.ds(hp * 2 * D + hb * D, D)],
                                      quot.rearrange("p (j d) -> p j d", d=D)).then_inc(image_done, 1)

            with pool.Fori(0, HEADS // 2 - 1) as hp:
                for hb in range(2):
                    for half in range(2):
                        rows(hp * 4 + (2 * hb + half), hp, hb, half)
                    load(hb, bass.ds(hp * 2 + (hb + 2), 1), bass.ds(hp * 2 * D + (hb + 2) * D, D))
            for n in range(RUNS - 4, RUNS):
                rows(n, n // 4, n // 2 % 2, n % 2)

        @block.scalar
        def _(act):
            act.sem_inc(exp_done, RING_S)

            def copy_out(n, t):
                act.wait_ge(pv_done, n * NG + (RING_P + GROUPS * (t + 1)))
                if t == 0:
                    act.wait_ge(fold_done, n + 1)
                nc.scalar.activation(outT[:, 512 * t:512 * t + 512], ps[:, PS_O, :], ACT.Copy).then_inc(o_copied, 1)

            def run(n, hp, hb, half):
                act.wait_ge(vh_ready, hp * 4 + 2 * (hb + 1))
                for g in range(NG):
                    act.wait_ge(pv_done, n * NG + (g + 1))
                    if not by_pe(g):
                        act.wait_ge(sum_done, n * NDV + (3 + upto[g - RING_P]))
                    for u in (2 * g, 2 * g + 1):
                        act.wait_ge(s_ready, n * NU + (u + 1))
                        at = 2 * (place(u) % RING_S)
                        nc.scalar.activation(probs[:, g % RING_P, 2 * (u % 2):2 * (u % 2) + 2, :], ps[:, at:at + 2, :],
                                             ACT.Exp, bias=bound[hb]).then_inc(exp_done, 1)
                    if g % GROUPS == LAG - 2:
                        if g >= GROUPS:
                            copy_out(n, g // GROUPS - 1)
                        elif not isinstance(n, int) or n > 0:
                            copy_out(n - 1, TILES - 1)

            runs(act, run)
            copy_out(RUNS - 1, TILES - 1)

        @block.vector
        def _(dve):
            nc.vector.memset(ones, 1.0).then_inc(ones_ready, 1)
            dve.sem_inc(sum_done, 3)

            def add_pe_sums(n, t):
                dve.wait_ge(pv_done, n * NG + (RING_P + GROUPS * (t + 1)))
                dve.wait_ge(acc_done, n * TILES + (t + 1))
                d = den[:, 512 * t:512 * t + 512]
                nc.vector.scalar_tensor_tensor(out=d, in0=ps[:, PS_D, :], scalar=1.0 / D, in1=d,
                                               op0=ALU.mult, op1=ALU.add).then_inc(den_done, 1)

            def fold(n):
                dve.wait_ge(fold_done, n + 2)
                at = 2 * (FOLD_PLACE % RING_S)
                nc.vector.transpose(numT.rearrange("p (j d) -> p j d", d=D),
                                    ps[:, at, :].rearrange("p (c j) -> p j c", j=SUB)).then_inc(turn_done, 1)
                nc.vector.transpose(denT.rearrange("p (j d) -> p j d", d=D),
                                    ps[:, at + 1, :].rearrange("p (c j) -> p j c", j=SUB)).then_inc(turn_done, 1)
                dve.wait_ge(turn_done, n * 2 + 3)
                nc.vector.reciprocal(rden, denT.rearrange("p (j d) -> p j d", d=D)[:, :, 0]).then_inc(rden_done, 1)
                dve.wait_ge(rden_done, n + 1)
                dve.wait_ge(image_done, n + 1)
                nc.vector.tensor_tensor(out=quot.rearrange("p (j d) -> p j d", d=D), in0=numT.rearrange("p (j d) -> p j d", d=D),
                                        in1=rden.unsqueeze(2).to_broadcast([P, SUB, D]), op=ALU.mult).then_inc(quot_done, 1)

            def run(n, hp, hb, half):
                first_run = isinstance(n, int) and n == 0
                ch = Chain(dve, sum_step, n * (NDV - TILES))
                for t in range(TILES):
                    first = True
                    for g in range(GROUPS * t, GROUPS * (t + 1)):
                        if not by_pe(g):
                            dve.wait_ge(exp_done, n * NU + (RING_S + 2 * g + 2))
                            a, b = probs[:, g % RING_P, 0:2, :], probs[:, g % RING_P, 2:4, :]
                            if first:
                                nc.vector.tensor_tensor(out=acc, in0=a, in1=b, op=ALU.add).then_inc(sum_done, 1)
                            else:
                                nc.vector.tensor_tensor(out=tmp[g % 2], in0=a, in1=b, op=ALU.add).then_inc(sum_done, 1)
                                dve.wait_ge(sum_done, n * NDV + (3 + upto[g]))
                                ch.link(nc.vector.tensor_tensor(out=acc, in0=acc, in1=tmp[g % 2], op=ALU.add))
                            first = False
                        if g % GROUPS == LAG - 1:
                            if t > 0:
                                add_pe_sums(n, t - 1)
                            elif not first_run:
                                add_pe_sums(n - 1, TILES - 1)
                        if g == FOLD_AT and not first_run:
                            fold(n - 1)
                    if t == 0:
                        dve.wait_ge(fold_done, n + 1)
                    nc.vector.tensor_tensor(out=den[:, 512 * t:512 * t + 512], in0=acc[:, 0:512],
                                            in1=acc[:, 512:1024], op=ALU.add).then_inc(acc_done, 1)
                    dve.wait_ge(acc_done, n * TILES + (t + 1))

            runs(dve, run)
            add_pe_sums(RUNS - 1, TILES - 1)
            fold(RUNS - 1)

        @block.tensor
        def _(pe):
            pe.sem_inc(fold_done, 1)
            pe.sem_inc(image_done, 1)
            pe.sem_inc(turn_done, 1)
            pe.sem_inc(o_copied, 1)
            pe.sem_inc(den_done, 1)
            pe.sem_inc(pv_done, RING_P)
            pe.wait_ge(ones_ready, 1)

            def ring_free(n, p):
                v = holder_before(p)
                if v == "fold":
                    pe.wait_ge(turn_done, n * 2 + 1)
                else:
                    pe.wait_ge(exp_done, n * NU + (RING_S + v + 1))

            def scores(n, hb, half, u):
                ring_free(n, place(u))
                at = 2 * (place(u) % RING_S)
                for a in range(2):
                    k = 2 * (u % (2 * GROUPS)) + a
                    last = nc.tensor.matmul(ps[:, at + a, :], kst[hb][:, P * k:P * k + P],
                                            qst[hb][:, 2048 * half + 512 * (u // (2 * GROUPS)):][:, 0:512],
                                            start=True, stop=True)
                last.then_inc(s_ready, 1)

            def weighted(n, hb, g):
                t, r = g // GROUPS, g % GROUPS
                pe.wait_ge(exp_done, n * NU + (RING_S + 2 * g + 2))
                if r == 0:
                    pe.wait_ge(o_copied, n * TILES + (t + 1))
                for j in range(4):
                    last = nc.tensor.matmul(ps[32 * j:32 * j + 32, PS_O, :], vh[hb][:, 4 * r + j, :],
                                            probs[:, g % RING_P, j, :], start=(r == 0), stop=(r == GROUPS - 1),
                                            tile_position=(0, 32 * j))
                if not by_pe(g):
                    last.then_inc(pv_done, 1)

            def summed(n, g):
                t, r = g // GROUPS, g % GROUPS
                if r == 3:
                    pe.wait_ge(den_done, n * TILES + (t + 1))
                for j in range(4):
                    last = nc.tensor.matmul(ps[32 * j:32 * j + 32, PS_D, :], ones, probs[:, g % RING_P, j, :],
                                            start=(r == 3), stop=(r == GROUPS - 1), tile_position=(0, 32 * j))
                last.then_inc(pv_done, 1)

            def fold(n):
                pe.wait_ge(o_copied, n * TILES + (TILES + 1))
                pe.wait_ge(den_done, n * TILES + (TILES + 1))
                at = 2 * (FOLD_PLACE % RING_S)
                for bank, w, a in ((at, cst[:, C_FOLD:C_FOLD + D], outT), (at + 1, ones, den)):
                    for t in range(TILES):
                        last = nc.tensor.matmul(ps[32 * t:32 * t + 32, bank, :], w, a[:, 512 * t:512 * t + 512],
                                                start=True, stop=True, tile_position=(0, 32 * t))
                last.then_inc(fold_done, 1)

            def run(n, hp, hb, half):
                first_run = isinstance(n, int) and n == 0
                pe.wait_ge(heads_loaded[hb], hp * 128 + 128)
                pe.wait_ge(vh_ready, hp * 4 + 2 * (hb + 1))
                for g in range(NG):
                    if g == FOLD_AT and not first_run:
                        ring_free(n, FOLD_PLACE)
                        fold(n - 1)
                    scores(n, hb, half, 2 * g)
                    if g >= LAG:
                        m, mb, w = n, hb, g - LAG
                    else:
                        m, mb, w = n - 1, hb if half else 1 - hb, NG + g - LAG
                    if g >= LAG or not first_run:
                        weighted(m, mb, w)
                    scores(n, hb, half, 2 * g + 1)
                    if by_pe(w) and (g >= LAG or not first_run):
                        summed(m, w)

            runs(pe, run)
            for g in range(NG - LAG, NG):
                weighted(RUNS - 1, 1, g)
                if by_pe(g):
                    summed(RUNS - 1, g)
            fold(RUNS - 1)


def layer_norm_tiles(nc, block, ctx, name, tok, normT, eps, cst, ps, stage, small, add, loaded):
    NB = TT // 4

    def sem(n):
        return ctx.enter_context(nc.semaphore(name + n))

    step, var_ready, std_ready, norm_ready = sem("step"), sem("var_ready"), sem("std_ready"), sem("norm_ready")
    turned, turned_copied, add_ready, added = sem("turned"), sem("turned_copied"), sem("add_ready"), sem("added")
    norm = [stage[:, 1024 * b:1024 * b + 1024].rearrange("p (t c) -> p t c", t=4) for b in range(stage.shape[1] // 1024)]
    RING_N = len(norm)
    stats = small[:, 0:24].rearrange("p (t n) -> p t n", n=6)
    mv = [small[:, 24 + 8 * b:32 + 8 * b].rearrange("p (t n) -> p t n", n=2) for b in range(2)]
    std = [small[:, 40 + 4 * b:44 + 4 * b] for b in range(2)]

    @block.vector
    def _(dve):
        ch = Chain(dve, step)
        if loaded is not None:
            dve.wait_ge(loaded, 16)
        for n in range(NB):
            b = n % 2
            if n >= 2:
                dve.wait_ge(norm_ready, 4 * (n - 1))
            t4 = tok[:, 4 * n:4 * n + 4, :]
            if add is not None:
                dve.wait_ge(add_ready, n + 1)
                nc.vector.tensor_tensor(out=t4, in0=t4, in1=ps[:, 2 * b:2 * b + 2, :].rearrange("p b (t c) -> p (b t) c", c=C),
                                        op=ALU.add).then_inc(added, 1)
                dve.wait_ge(added, n + 1)
            ch.wait()
            for t in range(4):
                ch.step(nc.vector.bn_stats(stats[:, t, :], t4[:, t, :]))
            ch.wait()
            for t in range(4):
                last = nc.vector.bn_aggr(mv[b][:, t, :], stats[:, t, :])
                ch.step(last)
            ch.wait()
            nc.vector.tensor_copy(std[b], mv[b][:, :, 1]).then_inc(var_ready, 1)
            dve.wait_ge(std_ready, n + 1)
            ch.link(nc.vector.reciprocal(std[b], std[b]))
            if n >= RING_N:
                dve.wait_ge(turned, n - RING_N + 1)
            for t in range(4):
                last = nc.vector.tensor_scalar(norm[n % RING_N][:, t, :], t4[:, t, :], mv[b][:, t, 0:1], std[b][:, t:t + 1],
                                               op0=ALU.subtract, op1=ALU.mult)
                last.then_inc(norm_ready, 1)

    @block.scalar
    def _(act):
        for n in range(NB):
            b = n % 2
            act.wait_ge(var_ready, n + 1)
            nc.scalar.activation(std[b], std[b], ACT.Sqrt, bias=eps[:, 1:2]).then_inc(std_ready, 1)
            act.wait_ge(turned, n + 1)
            for k in range(KC):
                nc.scalar.activation(normT[:, k, 512 * n:512 * n + 512], ps[:, 4 + 2 * b + k, :], ACT.Copy).then_inc(turned_copied, 1)

    @block.tensor
    def _(pe):
        for n in range(NB + 1):
            if n < NB and add is not None:
                if n >= 2:
                    pe.wait_ge(added, n - 1)
                add(pe, n, 2 * (n % 2)).then_inc(add_ready, 1)
            if n >= 1:
                m, b = n - 1, (n - 1) % 2
                pe.wait_ge(norm_ready, 4 * (m + 1))
                if m >= 2:
                    pe.wait_ge(turned_copied, KC * (m - 1))
                for t in range(4):
                    for k in range(KC):
                        last = nc.tensor.transpose(ps[:, 4 + 2 * b + k, P * t:P * t + P], norm[m % RING_N][:, t, P * k:P * k + P],
                                                   cst[:, C_ID:C_ID + P])
                last.then_inc(turned, 1)


def project_and_norm(nc, ctx, ps, big, cst, eps, xT, wprojT):
    image = big[1].rearrange("p (f j c) -> p f j c", f=2, j=SUB)
    tok = big[5].rearrange("p (t c) -> p t c", c=C)
    normT = big[2].rearrange("p (k s) -> p k s", k=KC)
    wp = big[4][:, 0:KC * C].rearrange("p (k c) -> p k c", k=KC)
    wp_loaded = ctx.enter_context(nc.semaphore("wp_loaded"))

    def add(pe, n, bank):
        if n == 0:
            pe.wait_ge(wp_loaded, 16)
        for t in range(4):
            i = 4 * n + t
            for f in range(2):
                last = nc.tensor.matmul(ps[:, bank + t // 2, C * (t % 2):C * (t % 2) + C],
                                        image[:, f, i // 2, P * (i % 2):P * (i % 2) + P], wp[:, f, :],
                                        start=(f == 0), stop=(f == 1))
        return last

    loaded = ctx.enter_context(nc.semaphore("xT_loaded"))
    with nc.Block() as block:
        layer_norm_tiles(nc, block, ctx, "ln1_", tok, normT, eps, cst, ps, big[3][:, 0:2048], big[4][:, 4096:4160], add, loaded)

        @block.sync
        def _(sp):
            sp.dma_start(tok[:, :, :], xT.rearrange("(t p) c -> p t c", p=P)).then_inc(loaded, 16)
            sp.dma_start(wp[:, :, :], wprojT.rearrange("(k p) c -> p k c", p=P)).then_inc(wp_loaded, 16)


def qkv_1(nc, ctx, ps, big, wq, wk, wv, bq, bk, bv, q1_scr):
    normT = big[2].rearrange("p (k s) -> p k s", k=KC)
    kT = big[1].rearrange("p (k s) -> p k s", k=KC)
    v1 = big[3].rearrange("p (t c) -> p t c", c=C)
    wts = [big[4][:, 512 * n:512 * n + 512].rearrange("p (k c) -> p k c", k=KC) for n in range(3)]
    bvb = big[4][:, 1536:2048]
    bcol = big[4][:, 2048:2052]
    qst = [big[4][:, 2560 + 512 * n:3072 + 512 * n] for n in range(4)]

    def sem(n):
        return ctx.enter_context(nc.semaphore("qkv1_" + n))

    loaded, ready, moved, stored = sem("loaded"), sem("ready"), sem("moved"), [sem(f"stored{n}") for n in range(4)]
    NQ = KC * ST
    NV = TT // 2

    def bank(n):
        return n % 8

    def product(n):
        for k in range(KC):
            if n < 2 * NQ:
                o, st = (n % NQ) // ST, n % ST
                yield (ps[:, bank(n), :], wts[n // NQ][:, k, P * o:P * o + P], normT[:, k, 512 * st:512 * st + 512], k)

    with nc.Block() as block:
        @block.sync
        def _(sp):
            for w, t in ((wq, wts[0]), (wk, wts[1]), (wv, wts[2])):
                sp.dma_start(t[:, :, :], w.rearrange("(k p) c -> p k c", p=P)).then_inc(loaded, 16)
            for n, b in enumerate((bq, bk)):
                sp.dma_start(bcol[:, 2 * n:2 * n + 2], b).then_inc(loaded, 16)
            sp.dma_start(bvb, bv).then_inc(loaded, 16)
            for n in range(NQ):
                o, st = n // ST, n % ST
                sp.wait_ge(moved, n + 1)
                sp.dma_start(q1_scr[4 * st:4 * st + 4, :, o, :].rearrange("t p s -> p t s"),
                             qst[n % 4].rearrange("p (t s) -> p t s", t=4)).then_inc(stored[n % 4], 16)
            for n in range(4):
                sp.wait_ge(stored[n], 16 * NQ // 4)

        @block.tensor
        def _(pe):
            pe.wait_ge(loaded, 96)
            for n in range(2 * NQ):
                if n >= 8:
                    pe.wait_ge(moved, n - 7)
                for o, l, r, k in product(n):
                    last = nc.tensor.matmul(o, l, r, start=(k == 0), stop=(k == KC - 1))
                last.then_inc(ready, 1)
            for m in range(NV):
                n = 2 * NQ + m
                pe.wait_ge(moved, n - 7)
                for u in range(2):
                    t = 2 * m + u
                    for k in range(KC):
                        last = nc.tensor.matmul(ps[:, bank(n), C * u:C * u + C], normT[:, k, P * t:P * t + P],
                                                wts[2][:, k, :], start=(k == 0), stop=(k == KC - 1))
                last.then_inc(ready, 1)

        @block.vector
        def _(dve):
            dve.wait_ge(loaded, 96)
            for n in range(2 * NQ + NV):
                dve.wait_ge(ready, n + 1)
                if n < 2 * NQ:
                    o, st = (n % NQ) // ST, n % ST
                    if n < NQ and n >= 4:
                        dve.wait_ge(stored[n % 4], 16 * (n // 4))
                    dst = qst[n % 4] if n < NQ else kT[:, o, 512 * st:512 * st + 512]
                    c = 2 * (n // NQ) + o
                    nc.vector.tensor_scalar(dst, ps[:, bank(n), :], bcol[:, c:c + 1], None, op0=ALU.add).then_inc(moved, 1)
                else:
                    m = n - 2 * NQ
                    nc.vector.tensor_tensor(out=big[3][:, 512 * m:512 * m + 512], in0=ps[:, bank(n), :], in1=bvb,
                                            op=ALU.add).then_inc(moved, 1)


def attention_1(nc, ctx, ps, big, ident, q1_scr):
    kT = big[1].rearrange("p (k s) -> p k s", k=KC)
    v1 = big[3].rearrange("p (t c) -> p t c", c=C)
    tok = big[5].rearrange("p (t c) -> p t c", c=C)
    score = [big[0][:, S * b:S * b + S] for b in range(2)]
    work = [big[2][:, S * b:S * b + S] for b in range(2)]
    wT = big[4][:, 0:S].rearrange("p (t s) -> p t s", t=TT)
    qT = [big[4][:, S + 256 * b:S + 256 * b + 256].rearrange("p (k s) -> p k s", k=KC) for b in range(2)]
    sm = big[4][:, S + 512:S + 640]
    top = [sm[:, 32 * b:32 * b + 32] for b in range(2)]
    negmax = [sm[:, 64 + b:65 + b] for b in range(2)]
    total = [sm[:, 66 + b:67 + b] for b in range(2)]
    CH = S // 512
    RING_S, RING_T = 4, 2
    PS_T, PS_A = 4, 6
    PAIRS = TT // 2 - 1

    def sem(n):
        return ctx.enter_context(nc.semaphore("a1_" + n))

    q_loaded = [sem("q_loaded_even"), sem("q_loaded_odd")]
    passed, s_ready, s_copied, top_step = sem("passed"), sem("s_ready"), sem("s_copied"), sem("top_step")
    exp_may, exp_done, w_ready = sem("exp_may"), sem("exp_done"), sem("w_ready")
    max_step, inv_step = sem("max_step"), sem("inv_step")
    t_ready, t_copied, o_ready, o_done = sem("t_ready"), sem("t_copied"), sem("o_ready"), sem("o_done")

    with nc.Block() as block:
        @block.sync
        def _(sp):
            for b in range(2):
                sp.dma_start(qT[b], q1_scr[b, :, :, :]).then_inc(q_loaded[b], 16)
            with sp.Fori(0, PAIRS) as r:
                for b in range(2):
                    sp.wait_ge(s_ready, r * (2 * CH) + CH * (b + 1))
                    sp.dma_start(qT[b], q1_scr[bass.ds(r * 2 + (b + 2), 1), :, :, :].rearrange("t p k s -> (t p) k s")
                                 ).then_inc(q_loaded[b], 16)

        @block.tensor
        def _(pe):
            pe.sem_inc(t_ready, CH + 1)
            pe.sem_inc(o_ready, 1)

            def scores(n, b, q_count):
                pe.wait_ge(q_loaded[b], q_count)
                for c in range(CH):
                    pe.wait_ge(s_copied, n * CH + (c + 1))
                    for k in range(KC):
                        last = nc.tensor.matmul(ps[:, c % RING_S, :], qT[b][:, k, :], kT[:, k, 512 * c:512 * c + 512],
                                                start=(k == 0), stop=(k == KC - 1))
                    last.then_inc(s_ready, 1)

            def values(n, b, c):
                pe.wait_ge(t_copied, n * CH + (RING_T + c + 1))
                if c == 0:
                    pe.wait_ge(o_done, n + 1)
                for t in range(4 * c, 4 * c + 4):
                    last = nc.tensor.matmul(ps[:, PS_A + b, 0:C], wT[:, t, :], v1[:, t, :], start=(t == 0), stop=(t == TT - 1))
                if c == CH - 1:
                    last.then_inc(o_ready, 1)

            def outputs(n, b):
                pe.wait_ge(w_ready, n + 1)
                for c in range(CH + 1):
                    if c < CH:
                        pe.wait_ge(t_copied, n * CH + (c + 1))
                        for u in range(4):
                            t = 4 * c + u
                            last = nc.tensor.transpose(ps[:, PS_T + c % RING_T, P * u:P * u + P],
                                                       work[b][:, P * t:P * t + P], ident)
                        last.then_inc(t_ready, 1)
                    if c >= 1:
                        values(n, b, c - 1)

            for b in range(2):
                scores(b, b, 16)
            with pe.Fori(0, PAIRS) as r:
                for b in range(2):
                    outputs(r * 2 + b, b)
                    scores(r * 2 + (b + 2), b, r * 16 + 32)
            for b in range(2):
                outputs(TT - 2 + b, b)

        @block.scalar
        def _(act):
            act.sem_inc(s_copied, RING_S)
            act.sem_inc(t_copied, RING_T)

            def copy_scores(n, b):
                for c in range(CH):
                    act.wait_ge(s_ready, n * CH + (c + 1))
                    nc.scalar.activation(score[b][:, 512 * c:512 * c + 512], ps[:, c % RING_S, :], ACT.Copy).then_inc(s_copied, 1)

            def exponentials(n, b):
                act.wait_ge(exp_may, n + 1)
                nc.scalar.activation(score[b], score[b], ACT.Exp, bias=negmax[b]).then_inc(exp_done, 1)

            def copy_weights(n, b):
                act.wait_ge(o_ready, n + 1)
                for c in range(CH):
                    act.wait_ge(t_ready, n * CH + (CH + c + 2))
                    nc.scalar.activation(big[4][:, 512 * c:512 * c + 512], ps[:, PS_T + c % RING_T, :], ACT.Copy).then_inc(t_copied, 1)

            copy_scores(0, 0)
            exponentials(0, 0)
            copy_scores(1, 1)
            with act.Fori(0, PAIRS) as r:
                for b in range(2):
                    n = r * 2 + b
                    copy_weights(n, b)
                    copy_scores(n + 2, b)
                    exponentials(n + 1, 1 - b)
            copy_weights(TT - 2, 0)
            exponentials(TT - 1, 1)
            copy_weights(TT - 1, 1)

        @block.vector
        def _(dve):
            dve.sem_inc(o_done, 2)
            STEPS = 7

            def pass_waits():
                dve.sem_inc(passed, 1)

            def take_top(n, b):
                ch = Chain(dve, top_step, n * STEPS)
                dve.wait_ge(s_copied, n * CH + (RING_S + CH))
                dve.wait_ge(t_ready, n * CH + 1)
                for a in range(TOPK // 8):
                    src = score[b] if a == 0 else work[b]
                    pass_waits()
                    ch.link(nc.vector.max(top[b][:, 8 * a:8 * a + 8], src))
                    if a == 0:
                        nc.vector.tensor_scalar(negmax[b], top[b][:, 0:1], -1.0, None, op0=ALU.mult).then_inc(max_step, 1)
                        dve.wait_ge(max_step, n + 1)
                    pass_waits()
                    ins = nc.vector.match_replace(work[b], top[b][:, 8 * a:8 * a + 8], src, TAKEN)
                    if a == 0:
                        ins.then_inc(exp_may, 1)
                        dve.wait_ge(exp_may, n + 1)
                    else:
                        ch.link(ins)
                assert ch.n == STEPS
                dve.wait_ge(exp_done, n + 1)
                dve.wait_ge(o_done, n + 1)
                nc.vector.scalar_tensor_tensor(out=work[b], in0=work[b], scalar=TAKEN, in1=score[b],
                                               op0=ALU.is_equal, op1=ALU.mult, accum_out=total[b]).then_inc(w_ready, 1)

            def add_output(n, b):
                dve.wait_ge(w_ready, n + 1)
                nc.vector.reciprocal(total[b], total[b]).then_inc(inv_step, 1)
                dve.wait_ge(inv_step, n + 1)
                dve.wait_ge(o_ready, n + 2)
                t = tok[:, bass.ds(n, 1), :].rearrange("p t c -> p (t c)")
                nc.vector.scalar_tensor_tensor(out=t, in0=ps[:, PS_A + b, 0:C], scalar=total[b], in1=t,
                                               op0=ALU.mult, op1=ALU.add).then_inc(o_done, 1)

            take_top(0, 0)
            with dve.Fori(0, PAIRS) as r:
                for b in range(2):
                    take_top(r * 2 + (b + 1), 1 - b)
                    add_output(r * 2 + b, b)
            take_top(TT - 1, 1)
            add_output(TT - 2, 0)
            add_output(TT - 1, 1)


def norm_and_route(nc, ctx, ps, big, cst, eps, weight, position, slot_expert, wg, bg, b2, x_slots):
    tok = big[5].rearrange("p (t c) -> p t c", c=C)
    normT = big[2].rearrange("p (k s) -> p k s", k=KC)
    rows = big[3].rearrange("p (t c) -> p t c", c=C)
    with nc.Block() as block:
        layer_norm_tiles(nc, block, ctx, "ln2_", tok, normT, eps, cst, ps, big[3], big[4][:, 0:64], None, None)

    area = big[4]
    at = [64]

    def take(n, lead=None, **dims):
        a = area[:, at[0]:at[0] + n]
        at[0] += n
        return a.rearrange(lead, **dims) if lead else a

    TE = "p (t e) -> p t e"
    wg_t = take(KC * NE, "p (k e) -> p k e", k=KC)
    bg_t = take(NE)
    b2_t = take(C)[0:NE, :]
    logit, best, hit0, hit1, hits, gate, before, count, upto, place = (take(TT * NE, TE, e=NE) for _ in range(10))
    where = take(TT * NE, TE, e=NE).bitcast(U32)
    wheref, pair = (take(TT * 2, TE, e=2) for _ in range(2))
    posf = [take(TT) for _ in range(2)]
    needs = take(NE * NK, "p (e k) -> p e k", k=NK)
    slots, slots_end, slots_at = (take(NE) for _ in range(3))
    passed = take(NS * NE, "p (s e) -> p s e", e=NE)
    owner = take(NS)
    gateT = big[0][0:NE, 0:S]
    iota = cst[:, C_IOTA:C_IOTA + NE]

    def sem(n):
        return ctx.enter_context(nc.semaphore("gate_" + n))

    loaded, logits, step, diff, ratio, gates = sem("loaded"), sem("logits"), sem("step"), sem("diff"), sem("ratio"), sem("gates")
    turned, turned_copied, b2_ready, b2_added = sem("turned"), sem("turned_copied"), sem("b2_ready"), sem("b2_added")
    hits_ready, counts_ready, routed, scattered = sem("hits_ready"), sem("counts_ready"), sem("routed"), sem("scattered")

    with nc.Block() as block:
        @block.sync
        def _(sp):
            sp.dma_start(wg_t[:, :, :], wg.rearrange("(k p) e -> p k e", p=P)).then_inc(loaded, 16)
            sp.dma_start(bg_t, bg).then_inc(loaded, 16)
            sp.dma_start(b2_t, b2).then_inc(loaded, 16)

        @block.gpsimd
        def _(pool):
            pool.wait_ge(routed, 1)
            for t in range(TT):
                for a in range(2):
                    pool.indirect_dma_start(out=x_slots, out_offset=bass.IndirectOffsetOnAxis(ap=position[a][:, t:t + 1], axis=0),
                                            in_=rows[:, t, :], in_offset=None).then_inc(scattered, 16)
            pool.wait_ge(scattered, 16 * 2 * TT)

        @block.tensor
        def _(pe):
            pe.wait_ge(loaded, 48)
            for t in range(TT):
                for k in range(KC):
                    last = nc.tensor.matmul(ps[:, 0, NE * t:NE * t + NE], normT[:, k, P * t:P * t + P], wg_t[:, k, :],
                                            start=(k == 0), stop=(k == KC - 1))
            last.then_inc(logits, 1)
            pe.wait_ge(hits_ready, 1)
            for bank, c in ((1, C_BEFORE), (2, C_ALL)):
                last = nc.tensor.matmul(ps[:, bank, 0:TT * NE], cst[:, c:c + P], hits.rearrange("p t e -> p (t e)"),
                                        start=True, stop=True)
            last.then_inc(counts_ready, 1)
            pe.wait_ge(gates, 1)
            for n in range(TT // 4):
                if n >= 2:
                    pe.wait_ge(turned_copied, n - 1)
                for u in range(4):
                    last = nc.tensor.transpose(ps[0:NE, 6 + n % 2, P * u:P * u + P], gate[:, 4 * n + u, :], cst[:, C_ID:C_ID + P])
                last.then_inc(turned, 1)
            for n in range(TT // 2):
                pe.wait_ge(turned_copied, n // 2 + 1)
                if n >= 3:
                    pe.wait_ge(b2_added, n - 2)
                for u in range(2):
                    t = 2 * n + u
                    last = nc.tensor.matmul(ps[:, 3 + n % 3, C * u:C * u + C], gateT[:, P * t:P * t + P], b2_t,
                                            start=True, stop=True)
                last.then_inc(b2_ready, 1)

        @block.scalar
        def _(act):
            act.wait_ge(diff, 1)
            nc.scalar.activation(pair[:, :, 1], pair[:, :, 1], ACT.Exp).then_inc(ratio, 1)
            for n in range(TT // 4):
                act.wait_ge(turned, n + 1)
                nc.scalar.activation(gateT[:, 512 * n:512 * n + 512], ps[0:NE, 6 + n % 2, :], ACT.Copy).then_inc(turned_copied, 1)

        @block.vector
        def _(dve):
            ch = Chain(dve, step)

            def by_token(a):
                return a.unsqueeze(2).to_broadcast([P, TT, NE])

            def by_expert(a):
                return a.unsqueeze(1).to_broadcast([P, TT, NE])

            dve.wait_ge(loaded, 48)
            dve.wait_ge(logits, 1)
            ch.link(nc.vector.tensor_tensor(out=logit, in0=ps[:, 0, 0:TT * NE].rearrange(TE, e=NE),
                                            in1=by_expert(bg_t), op=ALU.add))
            for t in range(TT):
                ch.step(nc.vector.max(best[:, t, :], logit[:, t, :]))
            ch.wait()
            for t in range(TT):
                ch.step(nc.vector.max_index(where[:, t, :], best[:, t, :], logit[:, t, :]))
            ch.wait()
            ch.link(nc.vector.tensor_copy(wheref, where[:, :, 0:2]))
            nc.vector.tensor_tensor(out=pair[:, :, 1], in0=best[:, :, 1], in1=best[:, :, 0], op=ALU.subtract).then_inc(diff, 1)
            ch.step(nc.vector.tensor_tensor(out=hit0, in0=by_expert(iota), in1=by_token(wheref[:, :, 0]), op=ALU.is_equal))
            ch.link(nc.vector.tensor_tensor(out=hit1, in0=by_expert(iota), in1=by_token(wheref[:, :, 1]), op=ALU.is_equal))
            nc.vector.tensor_tensor(out=hits, in0=hit0, in1=hit1, op=ALU.add).then_inc(hits_ready, 1)
            dve.wait_ge(counts_ready, 1)
            ch.step(nc.vector.tensor_copy(before, ps[:, 1, 0:TT * NE].rearrange(TE, e=NE)))
            ch.link(nc.vector.tensor_copy(count, ps[:, 2, 0:TT * NE].rearrange(TE, e=NE)))
            ones = cst[:, C_ALL:C_ALL + TT]
            for e in range(NE):
                ch.step(nc.vector.tensor_tensor_scan(upto[:, :, e], ones, count[:, :, e], 0.0, op0=ALU.mult, op1=ALU.add))
            ch.wait()
            ch.step(nc.vector.tensor_tensor(out=before, in0=before, in1=upto, op=ALU.add))
            ch.link(nc.vector.tensor_tensor(out=needs, in0=upto[:, TT - 1, :].unsqueeze(2).to_broadcast([P, NE, NK]),
                                            in1=cst[:, C_STEP:C_STEP + NK].unsqueeze(1).to_broadcast([P, NE, NK]), op=ALU.is_gt))
            ch.step(nc.vector.tensor_tensor(out=before, in0=before, in1=count, op=ALU.subtract))
            ch.link(nc.vector.reduce_sum(slots, needs, AX_X))
            ch.link(nc.vector.tensor_tensor_scan(slots_end, ones[:, 0:NE], slots, 0.0, op0=ALU.mult, op1=ALU.add))
            ch.step(nc.vector.tensor_tensor(out=slots_at, in0=slots_end, in1=slots, op=ALU.subtract))
            ch.link(nc.vector.tensor_tensor(out=passed, in0=cst[:, C_SLOT:C_SLOT + NS].unsqueeze(2).to_broadcast([P, NS, NE]),
                                            in1=slots_end.unsqueeze(1).to_broadcast([P, NS, NE]), op=ALU.is_ge))
            ch.step(nc.vector.reduce_sum(owner, passed, AX_X))
            ch.link(nc.vector.tensor_scalar(slots_at, slots_at, float(SLOT), None, op0=ALU.mult))
            ch.step(nc.vector.tensor_scalar(slot_expert[:, :], owner, float(NE - 1), None, op0=ALU.min))
            ch.link(nc.vector.tensor_tensor(out=before, in0=before, in1=by_expert(slots_at), op=ALU.add))
            for a, hit in enumerate((hit0, hit1)):
                ch.link(nc.vector.tensor_tensor(out=place, in0=before, in1=hit, op=ALU.mult))
                ch.link(nc.vector.reduce_sum(posf[a], place, AX_X))
                ch.step(nc.vector.tensor_copy(position[a][:, :], posf[a]))
            ch.wait()
            dve.sem_inc(routed, 1)
            dve.wait_ge(ratio, 1)
            ch.link(nc.vector.tensor_scalar(pair[:, :, 0], pair[:, :, 1], 1.0, None, op0=ALU.add))
            ch.link(nc.vector.reciprocal(weight[:, :, 0], pair[:, :, 0]))
            ch.link(nc.vector.tensor_tensor(out=weight[:, :, 1], in0=pair[:, :, 1], in1=weight[:, :, 0], op=ALU.mult))
            ch.step(nc.vector.tensor_tensor(out=hit0, in0=hit0, in1=by_token(weight[:, :, 0]), op=ALU.mult))
            ch.link(nc.vector.tensor_tensor(out=hit1, in0=hit1, in1=by_token(weight[:, :, 1]), op=ALU.mult))
            nc.vector.tensor_tensor(out=gate, in0=hit0, in1=hit1, op=ALU.add).then_inc(gates, 1)
            for n in range(TT // 2):
                dve.wait_ge(b2_ready, n + 1)
                two = big[5][:, 512 * n:512 * n + 512]
                nc.vector.tensor_tensor(out=two, in0=two, in1=ps[:, 3 + n % 3, :], op=ALU.add).then_inc(b2_added, 1)


def experts(nc, ctx, ps, big, ident, slot_expert, w1, b1, w2, x_slots, y_slots):
    w1_t = [big[0][:, 2048 * b:2048 * b + 2048].rearrange("p (k h) -> p k h", k=KC) for b in range(2)]
    w2_t = [big[0][:, 4096 + 2048 * b:6144 + 2048 * b].rearrange("p (h c) -> p h c", h=HC) for b in range(2)]
    b1_t = [big[4][:, HC * b:HC * b + HC] for b in range(2)]
    xr = [big[1][:, 1024 * b:1024 * b + SQ * C].rearrange("p (t c) -> p t c", c=C) for b in range(2)]
    xT = [big[1][:, 2048 + 1024 * b:2048 + 1024 * b + KC * SLOT].rearrange("p (k s) -> p k s", k=KC) for b in range(2)]
    yr = [big[1][:, 4096 + 1024 * b:4096 + 1024 * b + SQ * C].rearrange("p (t c) -> p t c", c=C) for b in range(2)]
    hT = [big[2][:, 4096 * b:4096 * b + HC * SLOT].rearrange("p (h s) -> p h s", h=HC) for b in range(2)]
    RING_H, PS_X, PS_O = 2, 2, 4
    PAIRS = (NS - 1) // 2

    def sem(n):
        return ctx.enter_context(nc.semaphore("ffn_" + n))

    x_loaded, w_loaded = ([sem(f"{n}_loaded{b}") for b in range(2)] for n in "xw")
    x_turned, x_copied = sem("x_turned"), sem("x_copied")
    h_ready, h_done, o_ready, o_copied = sem("h_ready"), sem("h_done"), sem("o_ready"), sem("o_copied")
    stored = [sem(f"stored{b}") for b in range(2)]

    with nc.Block() as block:
        @block.sync
        def _(sp):
            def load(s, b):
                rows = bass.ds(s * SLOT, SLOT)
                sp.dma_start(xr[b], x_slots[rows, :].rearrange("(t p) c -> p t c", p=P)).then_inc(x_loaded[b], 16)
                e = sp.value_load(slot_expert[0:1, bass.ds(s, 1)], min_val=0, max_val=NE - 1)
                sp.dma_start(w1_t[b], w1[bass.ds(e, 1), :, :].rearrange("e (k p) h -> p (e k) h", p=P)).then_inc(w_loaded[b], 16)
                sp.dma_start(b1_t[b], b1[bass.ds(e, 1), :, :].rearrange("e p h -> (e p) h")).then_inc(w_loaded[b], 16)
                sp.dma_start(w2_t[b], w2[bass.ds(e, 1), :, :].rearrange("e (h p) c -> p (e h) c", p=P)).then_inc(w_loaded[b], 16)

            def next_load(s, b):
                sp.wait_ge(o_ready, s + 1)
                load(s + 2, b)

            def store(s, b):
                sp.wait_ge(o_copied, s + 3)
                sp.dma_start(y_slots[bass.ds(s * SLOT, SLOT), :].rearrange("(t p) c -> p t c", p=P), yr[b]).then_inc(stored[b], 16)

            for b in range(2):
                sp.sem_inc(stored[b], 16)
                load(b, b)
            with sp.Fori(0, PAIRS - 1) as r:
                for b in range(2):
                    next_load(r * 2 + b, b)
                    store(r * 2 + b, b)
            next_load(NS - 3, 0)
            for s in range(NS - 3, NS):
                store(s, s % 2)
            sp.wait_ge(stored[0], 16 * (PAIRS + 2))
            sp.wait_ge(stored[1], 16 * (PAIRS + 1))

        @block.tensor
        def _(pe):
            def turn(s, b, loads):
                pe.wait_ge(x_loaded[b], 16 * loads)
                if not isinstance(s, int):
                    pe.wait_ge(x_copied, s)
                for k in range(KC):
                    for t in range(SQ):
                        last = nc.tensor.transpose(ps[:, PS_X + k, P * t:P * t + P], xr[b][:, t, P * k:P * k + P], ident)
                last.then_inc(x_turned, 1)

            def up(s, b, loads):
                pe.wait_ge(w_loaded[b], 48 * loads)
                pe.wait_ge(x_copied, s + 1)
                for h in range(HC):
                    pe.wait_ge(h_done, s * HC + (h + 1))
                    for k in range(KC):
                        last = nc.tensor.matmul(ps[:, h % RING_H, 0:SLOT], w1_t[b][:, k, P * h:P * h + P], xT[b][:, k, :],
                                                start=(k == 0), stop=(k == KC - 1))
                    last.then_inc(h_ready, 1)

            def down(s, b):
                pe.wait_ge(h_done, s * HC + (RING_H + HC))
                pe.wait_ge(o_copied, s + 1)
                for t in range(SQ):
                    for h in range(HC):
                        last = nc.tensor.matmul(ps[:, PS_O + 2 * b + t // 2, C * (t % 2):C * (t % 2) + C],
                                                hT[b][:, h, P * t:P * t + P], w2_t[b][:, h, :],
                                                start=(h == 0), stop=(h == HC - 1))
                last.then_inc(o_ready, 1)

            turn(0, 0, 1)
            with pe.Fori(0, PAIRS) as r:
                for b in range(2):
                    up(r * 2 + b, b, r + 1)
                    turn(r * 2 + (b + 1), 1 - b, r + (b + 1))
                    down(r * 2 + b, b)
            up(NS - 1, 0, PAIRS + 1)
            down(NS - 1, 0)

        @block.scalar
        def _(act):
            act.sem_inc(h_done, RING_H)

            def gelu(s, b, loads):
                act.wait_ge(w_loaded[b], 48 * loads)
                for h in range(HC):
                    act.wait_ge(h_ready, s * HC + (h + 1))
                    nc.scalar.activation(hT[b][:, h, :], ps[:, h % RING_H, 0:SLOT], ACT.Gelu,
                                         bias=b1_t[b][:, h:h + 1]).then_inc(h_done, 1)

            with act.Fori(0, PAIRS) as r:
                for b in range(2):
                    gelu(r * 2 + b, b, r + 1)
            gelu(NS - 1, 0, PAIRS + 1)

        @block.vector
        def _(dve):
            dve.sem_inc(o_copied, 2)

            def copy_x(s, b):
                dve.wait_ge(x_turned, s + 1)
                nc.vector.tensor_copy(xT[b], ps[:, PS_X:PS_X + KC, 0:SLOT]).then_inc(x_copied, 1)

            def copy_o(s, b, stores):
                dve.wait_ge(o_ready, s + 1)
                dve.wait_ge(stored[b], 16 * stores + 16)
                nc.vector.tensor_copy(big[1][:, 4096 + 1024 * b:4096 + 1024 * b + SQ * C],
                                      ps[:, PS_O + 2 * b:PS_O + 2 * b + 2, :].rearrange("p k c -> p (k c)")[:, 0:SQ * C]
                                      ).then_inc(o_copied, 1)

            copy_x(0, 0)
            with dve.Fori(0, PAIRS) as r:
                for b in range(2):
                    copy_x(r * 2 + (b + 1), 1 - b)
                    copy_o(r * 2 + b, b, r)
            copy_o(NS - 1, 0, PAIRS)


def combine(nc, ctx, big, weight, position, y_slots, out):
    tok = big[5].rearrange("p (t c) -> p t c", c=C)
    RING = 8
    rows = [big[3][:, C * b:C * b + C] for b in range(RING)]
    PART = 8

    def sem(n):
        return ctx.enter_context(nc.semaphore("out_" + n))

    fetched = [sem(f"fetched{b}") for b in range(RING)]
    added, stored = sem("added"), sem("stored")

    with nc.Block() as block:
        @block.gpsimd
        def _(pool):
            for n in range(2 * TT):
                if n >= RING:
                    pool.wait_ge(added, n - RING + 1)
                pool.indirect_dma_start(out=rows[n % RING], out_offset=None, in_=y_slots,
                                        in_offset=bass.IndirectOffsetOnAxis(ap=position[n % 2][:, n // 2:n // 2 + 1], axis=0)
                                        ).then_inc(fetched[n % RING], 16)

        @block.vector
        def _(dve):
            for n in range(2 * TT):
                t, a = n // 2, n % 2
                dve.wait_ge(fetched[n % RING], 16 * (n // RING + 1))
                if a:
                    dve.wait_ge(added, n)
                nc.vector.scalar_tensor_tensor(out=tok[:, t, :], in0=rows[n % RING], scalar=weight[:, t, a:a + 1],
                                               in1=tok[:, t, :], op0=ALU.mult, op1=ALU.add).then_inc(added, 1)

        @block.sync
        def _(sp):
            for n in range(TT // PART):
                sp.wait_ge(added, 2 * PART * (n + 1))
                sp.dma_start(out[n * PART * P:(n + 1) * PART * P, :].rearrange("(t p) c -> p t c", p=P),
                             tok[:, PART * n:PART * n + PART, :]).then_inc(stored, 16)
            sp.wait_ge(stored, 16 * TT // PART)


def constants():
    c = np.zeros((P, C_N), np.float32)
    i = np.arange(P)
    c[:, C_ID:C_ID + P] = np.eye(P)
    c[:, C_GROUP:C_GROUP + P] = (i[:, None] // 8 == i[None, :] // 8) / 8.0
    c[:, C_HEAD:C_HEAD + P] = i[:, None] // D == i[None, :] // D
    c[:, C_FOLD:C_FOLD + D] = i[:, None] % D == np.arange(D)[None, :]
    c[:, C_IOTA:C_IOTA + NE] = np.arange(NE)
    c[:, C_BEFORE:C_BEFORE + P] = i[:, None] < i[None, :]
    c[:, C_ALL:C_ALL + P] = 1.0
    c[:, C_STEP:C_STEP + NK] = np.arange(NK) * SLOT
    c[:, C_SLOT:C_SLOT + NS] = np.arange(NS)
    return c


def kernel(**inputs):
    import concourse.bacc as bacc
    from concourse.bass_utils import run_bass_kernel_spmd

    a = {k: np.asarray(v) for k, v in inputs.items()}
    x = a["x"].reshape(C, S)
    t = a["L0_conv_temperature"].reshape(HEADS)

    def columns(v):
        return v.reshape(-1, P).T

    def rows(v):
        return np.broadcast_to(v.reshape(1, -1), (P, v.size))

    arrays = {
        "x": x, "xT": x.T, "wqkvT": a["L0_conv_w_qkv"].T, "wprojT": a["L0_conv_w_proj"].T,
        "t_col": columns(np.repeat(t, D)), "t_row": rows(t),
        "wq": a["L1_attn_Wq"], "wk": a["L1_attn_Wk"], "wv": a["L1_attn_Wv"],
        "bq": columns(a["L1_attn_bq"]), "bk": columns(a["L1_attn_bk"]),
        "bv": np.concatenate([rows(a["L1_attn_bv"])] * 2, axis=1),
        "wg": a["L1_ffn_Wg"], "bg": rows(a["L1_ffn_bg"]),
        "w1": a["L1_ffn_W1"], "b1": a["L1_ffn_b1"].reshape(NE, HC, P).transpose(0, 2, 1), "w2": a["L1_ffn_W2"], "b2": a["L1_ffn_b2"],
        "consts": constants(),
    }
    arrays = {k + "_in": np.ascontiguousarray(v) for k, v in arrays.items()}
    nc = bacc.Bacc("TRN2", target_bir_lowering=False, num_devices=1)
    args = [nc.dram_tensor(k, v.shape, mybir.dt.from_np(v.dtype), kind="ExternalInput").ap() for k, v in arrays.items()]
    out = nc.dram_tensor("out", (S, C), F32, kind="ExternalOutput").ap()
    build(nc, *args, out)
    r = run_bass_kernel_spmd(nc, [arrays], core_ids=[0])
    return r.results[0]["out"].T.reshape(1, C, 64, 64)
```

```python
from contextlib import ExitStack

import numpy as np

import concourse.bass as bass
from concourse import mybir

P = 128
F32 = mybir.dt.float32
F16 = mybir.dt.float16
F32R = mybir.dt.float32r
U32 = mybir.dt.uint32
I32 = mybir.dt.int32
ALU = mybir.AluOpType
ACT = mybir.ActivationFunctionType
AX_X = mybir.AxisListType.X

C = 256
S = 4096
HEADS = 8
D = C // HEADS
KC = C // P
TT = S // P
ST = S // 512
SUB = S // C
NE = 8
HID = 1024
HC = HID // P
TOPK = 32
GN_EPS = 1e-5
LN_EPS = 1e-5
NORM_EPS = 1e-12
SQ = 3
SLOT = SQ * P
NS = (2 * S + NE * (SLOT - 1)) // SLOT
NK = -(-S // SLOT)
TAKEN = -3.0e38

C_ID, C_GROUP, C_HEAD, C_FOLD, C_IOTA = 0, 128, 256, 384, 416
C_BEFORE, C_ALL = 424, 552
C_STEP = C_ALL + P
C_SLOT = C_STEP + NK
C_N = C_SLOT + NS
assert NS % 2 == 1


class Chain:

    def __init__(self, eng, sem, base=0):
        self.eng, self.sem, self.base, self.n = eng, sem, base, 0

    def step(self, ins):
        ins.then_inc(self.sem, 1)
        self.n += 1

    def wait(self):
        self.eng.wait_ge(self.sem, self.base + self.n)

    def link(self, ins):
        self.step(ins)
        self.wait()


def build(nc, x, xT, wqkvT, wprojT, t_col, t_row, wq, wk, wv, bq, bk, bv, wg, bg, w1, b1, w2, b2, consts, out):
    qk_scr = nc.dram_tensor("qk_scr", (2, 2, C, S), F16, kind="Internal").ap()
    q1_scr = nc.dram_tensor("q1_scr", (TT, P, KC, P), F32, kind="Internal").ap()
    tok_scr = nc.dram_tensor("tok_scr", (S, C), F32, kind="Internal").ap()
    x_slots = nc.dram_tensor("x_slots", (NS * SLOT, C), F32, kind="Internal").ap()
    y_slots = nc.dram_tensor("y_slots", (NS * SLOT, C), F32, kind="Internal").ap()
    with ExitStack() as ctx:
        def sb(name, shape, dt=F32):
            return ctx.enter_context(nc.sbuf_tensor(name, shape, dt))

        base = -(-nc.sbuf_base // 32) * 32
        big = [sb(f"big{i}", [P, 8192]) for i in range(6)]

        def over(name, i, at, cols):
            return nc.alloc_sbuf_tensor_at(name, [P, cols], F32R, offset=base + (8192 * i + at) * 4)

        k_parts = [over("k_hi", 1, 0, 8192), over("k_lo", 0, 0, 8192)]
        v_parts = [over("v_hi", 3, 0, 8192), over("v_lo", 5, 0, 8192)]
        w_parts = over("w_parts", 4, 4096, 4096)
        e_parts = [over(f"e_parts{b}", 3 * b, 0, 8192) for b in range(2)]
        h_parts, x_parts = over("h_parts", 2, 0, 8192), over("x_parts", 4, 0, 2048)
        q_parts = sb("q_parts", [P, 2 * C], F32R)
        extra = sb("extra", [P, 2128])
        cst = sb("cst", [P, C_N])
        ident = cst[:, C_ID:C_ID + P]
        negt = sb("negt", [P, HEADS])
        eps = sb("eps", [P, 2])
        weight = sb("weight", [P, TT, 2])
        position = [sb(f"position{a}", [P, TT], U32) for a in range(2)]
        slot_expert = sb("slot_expert", [P, NS], I32)
        ps = ctx.enter_context(nc.psum_tensor("ps", [P, 8, 512], F32))
        group_norm_and_qkv(nc, ctx, ps, big, cst, eps, negt, x, wqkvT, t_col, t_row, consts, qk_scr)
        attention_0(nc, ctx, ps, big, cst, negt, qk_scr, x_slots)
        project_and_norm(nc, ctx, ps, big, cst, eps, xT, wprojT)
        qkv_1(nc, ctx, ps, big, wq, wk, wv, bq, bk, bv, q1_scr, tok_scr, k_parts, v_parts)
        attention_1(nc, ctx, ps, big, extra, cst, q1_scr, tok_scr, q_parts, k_parts, v_parts, w_parts)
        w_loaded = [ctx.enter_context(nc.semaphore(f"ffn_w_loaded{b}")) for b in range(2)]

        def load_weights(sp, s, b):
            e = sp.value_load(slot_expert[0:1, bass.ds(s, 1)], min_val=0, max_val=NE - 1)
            to = big[1][:, 4096 * b:4096 * b + 4096]
            sp.dma_start(to[:, 0:2048].rearrange("p (k h) -> p k h", k=KC),
                         w1[bass.ds(e, 1), :, :].rearrange("e (k p) h -> p (e k) h", p=P)).then_inc(w_loaded[b], 16)
            sp.dma_start(to[:, 2048:4096].rearrange("p (h c) -> p h c", h=HC),
                         w2[bass.ds(e, 1), :, :].rearrange("e (h p) c -> p (e h) c", p=P)).then_inc(w_loaded[b], 16)
            return e

        norm_and_route(nc, ctx, ps, big, cst, eps, weight, position, slot_expert, wg, bg, b2, x_slots, tok_scr, load_weights)
        experts(nc, ctx, ps, big, ident, slot_expert, b1, x_slots, y_slots, e_parts, h_parts, x_parts, w_loaded, load_weights)
        combine(nc, ctx, big, weight, position, y_slots, out)


def group_norm_and_qkv(nc, ctx, ps, big, cst, eps, negt, x, wqkvT, t_col, t_row, consts, qk_scr):
    RING = 4
    xn = big[2].rearrange("p (k s) -> p k s", k=KC)
    w = big[3][:, 0:KC * 3 * C].rearrange("p (k o) -> p k o", k=KC)
    stage = big[4]
    sq, y = ([stage[:, 1024 * a + 512 * b:1024 * a + 512 * b + 512] for b in range(2)] for a in range(2))
    hi, lo = ([stage[:, 2048 + 512 * a + 256 * b:2304 + 512 * a + 256 * b].bitcast(F16) for b in range(2)] for a in range(2))
    ssT = [stage[:, 3072 + 512 * b:3584 + 512 * b].rearrange("p (g d) -> p g d", d=D) for b in range(RING)]
    inv = [stage[:, 5120 + 512 * b:5632 + 512 * b].rearrange("p (g d) -> p g d", d=D) for b in range(2)]
    nrm = [big[5][:, 256 + 16 * b:272 + 16 * b] for b in range(RING)]
    small = big[5]
    stats = small[:, 0:96].rearrange("p (k g n) -> p k g n", k=KC, n=6)
    mv = small[:, 96:100].rearrange("p (k n) -> p k n", k=KC)
    dev = small[:, 100:102]
    var = small[:, 102:104]
    rstd = small[:, 104:106]
    gmean = small[:, 108:112].rearrange("p (k n) -> p k n", k=KC)
    tcol = small[:, 112:114]
    trow = small[:, 114:122]

    def sem(name):
        return ctx.enter_context(nc.semaphore(name))

    PARTS = 4
    loaded_x = [sem(f"loaded_x{n}") for n in range(KC * PARTS)]
    loaded_w, loaded_c = sem("loaded_w"), sem("loaded_c")
    gn_step = sem("gn_step")
    stats_ready, gmean_ready, dev_ready, gvar_ready = sem("stats_ready"), sem("gmean_ready"), sem("dev_ready"), sem("gvar_ready")
    var_ready, std_ready, xn_ready = sem("var_ready"), sem("std_ready"), sem("xn_ready")
    qk_ready, sq_ready, ss_ready, nrm_ready = sem("qk_ready"), sem("sq_ready"), sem("ss_ready"), sem("nrm_ready")
    hi_ready, turned = sem("hi_ready"), sem("turned")
    y_step, split_ready, split_stored = sem("y_step"), sem("split_ready"), [sem("split_stored_even"), sem("split_stored_odd")]
    v_ready, v_copied = sem("v_ready"), sem("v_copied")

    with nc.Block() as block:
        @block.sync
        def _(sp):
            for n in range(KC * PARTS):
                k, cols = n // PARTS, slice(S // PARTS * (n % PARTS), S // PARTS * (n % PARTS + 1))
                sp.dma_start(xn[:, k, cols], x[P * k:P * k + P, cols]).then_inc(loaded_x[n], 16)
            sp.dma_start(w[:, :, :], wqkvT.rearrange("(k p) o -> p k o", p=P)).then_inc(loaded_w, 16)
            for b in range(2):
                sp.sem_inc(split_stored[b], 16)
            for ot in range(4):
                with sp.Fori(0, ST // 2) as i:
                    for b in range(2):
                        sp.wait_ge(split_ready, (i * 2 + b) + (ot * ST + 1))
                        for part, src in ((0, hi[b]), (1, lo[b])):
                            sp.dma_start(qk_scr[ot // 2, part, P * (ot % 2):P * (ot % 2) + P,
                                                bass.ds(i * 1024 + b * 512, 512)], src).then_inc(split_stored[b], 16)
            for b in range(2):
                sp.wait_ge(split_stored[b], 16 + 32 * 4 * ST // 2)

        @block.gpsimd
        def _(pool):
            pool.dma_start(cst[:, :], consts).then_inc(loaded_c, 16)
            pool.dma_start(tcol, t_col).then_inc(loaded_c, 16)
            pool.dma_start(trow, t_row).then_inc(loaded_c, 16)
            for ot in range(4):
                with pool.Fori(0, ST // 2) as i:
                    for b in range(2):
                        pool.wait_ge(hi_ready, i * 2 + (b + ot * ST + 1))
                        nc.gpsimd.tensor_tensor(out=lo[b], in0=y[b], in1=hi[b], op=ALU.subtract).then_inc(split_ready, 1)

        @block.vector
        def _(dve):
            dve.sem_inc(y_step, 13)
            ch = Chain(dve, gn_step)
            ch.step(nc.vector.memset(eps[:, 0:1], GN_EPS))
            ch.step(nc.vector.memset(eps[:, 1:2], LN_EPS))
            dve.wait_ge(loaded_c, 48)
            ch.link(nc.vector.tensor_scalar(negt[:, :], trow, -1.0, None, op0=ALU.mult))
            ch.step(nc.vector.tensor_tensor(out=negt[:, :], in0=negt[:, :], in1=trow, op=ALU.min))
            for k in range(KC):
                for g in range(ST):
                    dve.wait_ge(loaded_x[k * PARTS + g * PARTS // ST], 16)
                    ch.step(nc.vector.bn_stats(stats[:, k, g, :], xn[:, k, 512 * g:512 * g + 512]))
            ch.wait()
            for k in range(KC):
                nc.vector.bn_aggr(mv[:, k, :], stats[:, k, :, :]).then_inc(stats_ready, 1)
            dve.wait_ge(gmean_ready, 1)
            dve.wait_ge(stats_ready, KC)
            ch.link(nc.vector.tensor_copy(gmean[:, :, :], ps[:, 0, 0:4].rearrange("p (k n) -> p k n", k=KC)))
            ch.link(nc.vector.tensor_tensor(out=dev, in0=mv[:, :, 0], in1=gmean[:, :, 0], op=ALU.subtract))
            nc.vector.tensor_tensor(out=dev, in0=dev, in1=dev, op=ALU.mult).then_inc(dev_ready, 1)
            dve.wait_ge(gvar_ready, 1)
            nc.vector.tensor_tensor(out=var, in0=gmean[:, :, 1], in1=ps[:, 1, 0:2], op=ALU.add).then_inc(var_ready, 1)
            dve.wait_ge(std_ready, 1)
            ch.link(nc.vector.reciprocal(rstd, var))
            for k in range(KC):
                nc.vector.tensor_scalar(xn[:, k, :], xn[:, k, :], gmean[:, k, 0:1], rstd[:, k:k + 1],
                                        op0=ALU.subtract, op1=ALU.mult).then_inc(xn_ready, 1)
            def turn(n, b):
                dve.wait_ge(ss_ready, n + 3)
                nc.vector.transpose(ssT[b], ps[:, RING + b % 2, :].rearrange("p (g d) -> p g d", d=D)).then_inc(turned, 1)

            def normalise(n, b, ot, stored):
                yc = Chain(dve, y_step, n * 4 + 13)
                dve.wait_ge(nrm_ready, n + 1)
                yc.link(nc.vector.tensor_scalar(nrm[b], nrm[b], NORM_EPS, None, op0=ALU.max))
                yc.link(nc.vector.reciprocal(nrm[b], nrm[b]))
                yc.link(nc.vector.transpose(inv[b % 2], nrm[b].unsqueeze(2).to_broadcast([P, 16, D])))
                dve.wait_ge(split_stored[b % 2], stored)
                yc.link(nc.vector.scalar_tensor_tensor(
                    out=y[b % 2], in0=ps[:, b, :], scalar=tcol[:, ot:ot + 1] if ot < 2 else 1.0,
                    in1=inv[b % 2].rearrange("p g d -> p (g d)"), op0=ALU.mult, op1=ALU.mult))
                nc.vector.tensor_copy(hi[b % 2], y[b % 2]).then_inc(hi_ready, 1)

            for ot in range(4):
                with dve.Fori(0, ST // RING) as i:
                    for b in range(RING + 1):
                        if b < RING:
                            turn(i * RING + (b + ot * ST), b)
                        if b > 0:
                            normalise(i * RING + (b - 1 + ot * ST), b - 1, ot, i * (16 * RING) + (16 + 16 * (ot * ST + (b - 1) // 2 * 2)))

        @block.scalar
        def _(act):
            act.wait_ge(var_ready, 1)
            act.wait_ge(gn_step, 1)
            nc.scalar.activation(var, var, ACT.Sqrt, bias=eps[:, 0:1]).then_inc(std_ready, 1)
            for ot in range(4):
                with act.Fori(0, ST // RING) as i:
                    for b in range(RING + 1):
                        n = i * RING + (b + ot * ST)
                        if b < RING:
                            act.wait_ge(qk_ready, n + 1)
                            act.wait_ge(ss_ready, n + 1)
                            nc.scalar.activation(sq[b % 2], ps[:, b, :], ACT.Square).then_inc(sq_ready, 1)
                        if b > 0:
                            act.wait_ge(turned, n + 2)
                            nc.scalar.activation(nrm[b - 1], ssT[b - 1][:, :, 0], ACT.Sqrt).then_inc(nrm_ready, 1)
            for t in range(TT // 2):
                act.wait_ge(v_ready, t + 1)
                nc.scalar.activation(big[0][:, 512 * t:512 * t + 512], ps[:, 6 + t % 2, :], ACT.Copy).then_inc(v_copied, 1)

        @block.tensor
        def _(pe):
            pe.sem_inc(ss_ready, 2)
            pe.sem_inc(turned, 2)
            pe.wait_ge(loaded_c, 48)
            pe.wait_ge(stats_ready, KC)
            nc.tensor.matmul(ps[:, 0, 0:4], cst[:, C_GROUP:C_GROUP + P], mv[:, :, :].rearrange("p k n -> p (k n)"),
                             start=True, stop=True).then_inc(gmean_ready, 1)
            pe.wait_ge(dev_ready, 1)
            nc.tensor.matmul(ps[:, 1, 0:2], cst[:, C_GROUP:C_GROUP + P], dev, start=True, stop=True).then_inc(gvar_ready, 1)
            pe.wait_ge(loaded_w, 16)
            pe.wait_ge(xn_ready, KC)
            for ot in range(4):
                with pe.Fori(0, ST // RING) as i:
                    for b in range(RING + 1):
                        n = i * RING + (b + ot * ST)
                        if b < RING:
                            pe.wait_ge(y_step, n * 4 + 1)
                            for k in range(KC):
                                last = nc.tensor.matmul(ps[:, b, :], w[:, k, P * ot:P * ot + P],
                                                        xn[:, k, bass.ds(i * (512 * RING) + b * 512, 512)],
                                                        start=(k == 0), stop=(k == KC - 1))
                            last.then_inc(qk_ready, 1)
                        if b > 0:
                            pe.wait_ge(sq_ready, n)
                            pe.wait_ge(turned, n)
                            nc.tensor.matmul(ps[:, RING + (b - 1) % 2, :], cst[:, C_HEAD:C_HEAD + P], sq[(b - 1) % 2],
                                             start=True, stop=True).then_inc(ss_ready, 1)
            for t in range(TT // 2):
                if t >= 2:
                    pe.wait_ge(v_copied, t - 1)
                for u in range(2):
                    for k in range(KC):
                        last = nc.tensor.matmul(ps[:, 6 + t % 2, 256 * u:256 * u + 256],
                                                xn[:, k, P * (2 * t + u):P * (2 * t + u) + P], w[:, k, 2 * C:3 * C],
                                                start=(k == 0), stop=(k == KC - 1))
                last.then_inc(v_ready, 1)


def attention_0(nc, ctx, ps, big, cst, negt, qk_scr, x_slots):
    TILES = ST // 2
    GROUPS = TT // 4
    NG = TILES * GROUPS
    NU = 2 * NG
    RUNS = 2 * HEADS
    RING_S, RING_P = 3, 4
    LAG = 2
    FOLD_AT = 6
    PE_SUMS = (1, 5)
    v0 = big[0].rearrange("p (t c) -> p t c", c=C)
    image = big[1].rearrange("p (f j c) -> p f j c", f=2, j=SUB)
    kst = [big[2][:, 2048 * b:2048 * b + 2048].bitcast(F16) for b in range(2)]
    qst = [big[2][:, 4096 + 2048 * b:6144 + 2048 * b].bitcast(F16) for b in range(2)]
    probs = big[3].rearrange("p (r t s) -> p r t s", r=RING_P, t=4)
    vh = [big[4][:, 1024 * b:1024 * b + 1024].rearrange("p (t d) -> p t d", d=D) for b in range(2)]
    outT = big[4][:, 2048:4096]
    den = big[4][:, 4096:6144]
    tmp = [big[5][:, 1024 * b:1024 * b + 1024] for b in range(2)]
    acc = big[5][:, 2048:3072]
    ones = big[5][:, 3072:3104]
    rden = big[5][:, 3136:3136 + SUB]
    numT, denT, quot = (big[5][:, 3648 + 512 * b:4160 + 512 * b] for b in range(3))
    bound = [big[5][:, 3104 + b:3105 + b] for b in range(2)]
    PS_O, PS_D = 6, 7
    FILLS = 8
    fill = NS * SLOT * C // P // FILLS
    zeros = big[5][:, 5184:5184 + fill]
    assert 5184 + fill <= 8192 and fill * FILLS * P == NS * SLOT * C

    def by_pe(g):
        return g % GROUPS in PE_SUMS

    upto = [sum(not by_pe(a) for a in range(g + 1)) for g in range(NG)]
    NDV = upto[-1]
    upto = {g: upto[g] if g >= 0 else upto[g + NG] - NDV for g in range(-NG, NG)}

    FOLD_PLACE = 2 * FOLD_AT
    PLACES = NU + 2
    assert PLACES % RING_S == 0

    def place(u):
        return u if u < FOLD_PLACE else u + 1

    def holder_before(p):
        p -= RING_S
        while p == -1:
            p -= RING_S
        if p == FOLD_PLACE:
            return "fold"
        if p < 0:
            return p + PLACES - 1 - NU
        return p if p < FOLD_PLACE else p - 1

    def runs(eng, body):
        body(0, 0, 0, 0)
        with eng.Fori(0, RUNS // 4 - 1) as i:
            for k in (1, 2, 3, 4):
                body(i * 4 + k, i + k // 4, k // 2 % 2, k % 2)
        for n in range(RUNS - 3, RUNS):
            body(n, n // 4, n // 2 % 2, n % 2)

    def sem(name):
        return ctx.enter_context(nc.semaphore(name))

    heads_loaded = [sem("heads_loaded_even"), sem("heads_loaded_odd")]
    vh_ready, zeros_ready, filled = sem("vh_ready"), sem("zeros_ready"), sem("filled")
    s_ready, exp_done, pv_done, sum_done = sem("s_ready"), sem("exp_done"), sem("pv_done"), sem("sum_done")
    sum_step, ones_ready = sem("sum_step"), sem("ones_ready")
    o_copied, den_done, acc_done = sem("o_copied"), sem("den_done"), sem("acc_done")
    fold_done, image_done, rden_done = sem("fold_done"), sem("image_done"), sem("rden_done")
    quot_done, turn_done = sem("quot_done"), sem("turn_done")

    with nc.Block() as block:
        @block.sync
        def _(sp):
            def load(hb, rows):
                for a in range(2):
                    for part in range(2):
                        at = 64 * a + 32 * part
                        sp.dma_start(qst[hb][at:at + D, :], qk_scr[0, part, rows, :]).then_inc(heads_loaded[hb], 16)
                        sp.dma_start(kst[hb][at:at + D, :], qk_scr[1, a, rows, :]).then_inc(heads_loaded[hb], 16)

            for hb in range(2):
                load(hb, bass.ds(hb * D, D))
            sp.wait_ge(zeros_ready, 1)
            for f in range(FILLS):
                sp.dma_start(x_slots.rearrange("(p r) c -> p (r c)", p=P)[:, fill * f:fill * f + fill], zeros).then_inc(filled, 16)
            sp.wait_ge(filled, 16 * FILLS)
            with sp.Fori(0, HEADS // 2 - 1) as hp:
                for hb in range(2):
                    sp.wait_ge(fold_done, hp * 4 + (1 + 2 * (hb + 1)))
                    load(hb, bass.ds(hp * 2 * D + (hb + 2) * D, D))

        @block.gpsimd
        def _(pool):
            def load(hb, head, cols):
                nc.gpsimd.tensor_copy(bound[hb], negt[:, head]).then_inc(vh_ready, 1)
                nc.gpsimd.tensor_copy(vh[hb], v0[:, :, cols]).then_inc(vh_ready, 1)

            for hb in range(2):
                load(hb, bass.ds(hb, 1), bass.ds(hb * D, D))
            nc.gpsimd.memset(zeros, 0.0).then_inc(zeros_ready, 1)

            def rows(n, hp, hb, half):
                pool.wait_ge(quot_done, n + 1)
                nc.gpsimd.tensor_copy(image[:, half, :, bass.ds(hp * 2 * D + hb * D, D)],
                                      quot.rearrange("p (j d) -> p j d", d=D)).then_inc(image_done, 1)

            with pool.Fori(0, HEADS // 2 - 1) as hp:
                for hb in range(2):
                    for half in range(2):
                        rows(hp * 4 + (2 * hb + half), hp, hb, half)
                    load(hb, bass.ds(hp * 2 + (hb + 2), 1), bass.ds(hp * 2 * D + (hb + 2) * D, D))
            for n in range(RUNS - 4, RUNS):
                rows(n, n // 4, n // 2 % 2, n % 2)

        @block.scalar
        def _(act):
            act.sem_inc(exp_done, RING_S)

            def copy_out(n, t):
                act.wait_ge(pv_done, n * NG + (RING_P + GROUPS * (t + 1)))
                if t == 0:
                    act.wait_ge(fold_done, n + 1)
                nc.scalar.activation(outT[:, 512 * t:512 * t + 512], ps[:, PS_O, :], ACT.Copy).then_inc(o_copied, 1)

            def run(n, hp, hb, half):
                act.wait_ge(vh_ready, hp * 4 + 2 * (hb + 1))
                for g in range(NG):
                    act.wait_ge(pv_done, n * NG + (g + 1))
                    if not by_pe(g):
                        act.wait_ge(sum_done, n * NDV + (3 + upto[g - RING_P]))
                    for u in (2 * g, 2 * g + 1):
                        act.wait_ge(s_ready, n * NU + (u + 1))
                        at = 2 * (place(u) % RING_S)
                        nc.scalar.activation(probs[:, g % RING_P, 2 * (u % 2):2 * (u % 2) + 2, :], ps[:, at:at + 2, :],
                                             ACT.Exp, bias=bound[hb]).then_inc(exp_done, 1)
                        if u % (2 * GROUPS) == 2 * (LAG - 1):
                            if g >= GROUPS:
                                copy_out(n, g // GROUPS - 1)
                            elif not isinstance(n, int) or n > 0:
                                copy_out(n - 1, TILES - 1)

            runs(act, run)
            copy_out(RUNS - 1, TILES - 1)

        @block.vector
        def _(dve):
            nc.vector.memset(ones, 1.0).then_inc(ones_ready, 1)
            dve.sem_inc(sum_done, 3)

            def add_pe_sums(n, t):
                dve.wait_ge(pv_done, n * NG + (RING_P + GROUPS * t + PE_SUMS[-1] + 1))
                dve.wait_ge(acc_done, n * TILES + (t + 1))
                d = den[:, 512 * t:512 * t + 512]
                nc.vector.scalar_tensor_tensor(out=d, in0=ps[:, PS_D, :], scalar=1.0 / D, in1=d,
                                               op0=ALU.mult, op1=ALU.add).then_inc(den_done, 1)

            def fold(n):
                dve.wait_ge(fold_done, n + 2)
                at = 2 * (FOLD_PLACE % RING_S)
                nc.vector.transpose(numT.rearrange("p (j d) -> p j d", d=D),
                                    ps[:, at, :].rearrange("p (c j) -> p j c", j=SUB)).then_inc(turn_done, 1)
                nc.vector.transpose(denT.rearrange("p (j d) -> p j d", d=D),
                                    ps[:, at + 1, :].rearrange("p (c j) -> p j c", j=SUB)).then_inc(turn_done, 1)
                dve.wait_ge(turn_done, n * 2 + 3)
                nc.vector.reciprocal(rden, denT.rearrange("p (j d) -> p j d", d=D)[:, :, 0]).then_inc(rden_done, 1)
                dve.wait_ge(rden_done, n + 1)
                dve.wait_ge(image_done, n + 1)
                nc.vector.tensor_tensor(out=quot.rearrange("p (j d) -> p j d", d=D), in0=numT.rearrange("p (j d) -> p j d", d=D),
                                        in1=rden.unsqueeze(2).to_broadcast([P, SUB, D]), op=ALU.mult).then_inc(quot_done, 1)

            def run(n, hp, hb, half):
                first_run = isinstance(n, int) and n == 0
                ch = Chain(dve, sum_step, n * (NDV - TILES))
                for t in range(TILES):
                    first = True
                    for g in range(GROUPS * t, GROUPS * (t + 1)):
                        if g == FOLD_AT and not first_run:
                            fold(n - 1)
                        if not by_pe(g):
                            dve.wait_ge(exp_done, n * NU + (RING_S + 2 * g + 2))
                            a, b = probs[:, g % RING_P, 0:2, :], probs[:, g % RING_P, 2:4, :]
                            if first:
                                nc.vector.tensor_tensor(out=acc, in0=a, in1=b, op=ALU.add).then_inc(sum_done, 1)
                            else:
                                nc.vector.tensor_tensor(out=tmp[g % 2], in0=a, in1=b, op=ALU.add).then_inc(sum_done, 1)
                                dve.wait_ge(sum_done, n * NDV + (3 + upto[g]))
                                ch.link(nc.vector.tensor_tensor(out=acc, in0=acc, in1=tmp[g % 2], op=ALU.add))
                            first = False
                        if g % GROUPS == 0:
                            if t > 0:
                                add_pe_sums(n, t - 1)
                            elif not first_run:
                                add_pe_sums(n - 1, TILES - 1)
                    if t == 0:
                        dve.wait_ge(fold_done, n + 1)
                    nc.vector.tensor_tensor(out=den[:, 512 * t:512 * t + 512], in0=acc[:, 0:512],
                                            in1=acc[:, 512:1024], op=ALU.add).then_inc(acc_done, 1)
                    dve.wait_ge(acc_done, n * TILES + (t + 1))

            runs(dve, run)
            add_pe_sums(RUNS - 1, TILES - 1)
            fold(RUNS - 1)

        @block.tensor
        def _(pe):
            pe.sem_inc(fold_done, 1)
            pe.sem_inc(image_done, 1)
            pe.sem_inc(turn_done, 1)
            pe.sem_inc(o_copied, 1)
            pe.sem_inc(den_done, 1)
            pe.sem_inc(pv_done, RING_P)
            pe.wait_ge(ones_ready, 1)

            def ring_free(n, p):
                v = holder_before(p)
                if v == "fold":
                    pe.wait_ge(turn_done, n * 2 + 1)
                else:
                    pe.wait_ge(exp_done, n * NU + (RING_S + v + 1))

            def scores(n, hb, half, u):
                ring_free(n, place(u))
                at = 2 * (place(u) % RING_S)
                for a in range(2):
                    k = 2 * (u % (2 * GROUPS)) + a
                    last = nc.tensor.matmul(ps[:, at + a, :], kst[hb][:, P * k:P * k + P],
                                            qst[hb][:, 2048 * half + 512 * (u // (2 * GROUPS)):][:, 0:512],
                                            start=True, stop=True)
                last.then_inc(s_ready, 1)

            def weighted(n, hb, g):
                t, r = g // GROUPS, g % GROUPS
                pe.wait_ge(exp_done, n * NU + (RING_S + 2 * g + 2))
                if r == 0:
                    pe.wait_ge(o_copied, n * TILES + (t + 1))
                for j in range(4):
                    last = nc.tensor.matmul(ps[32 * j:32 * j + 32, PS_O, :], vh[hb][:, 4 * r + j, :],
                                            probs[:, g % RING_P, j, :], start=(r == 0), stop=(r == GROUPS - 1),
                                            tile_position=(0, 32 * j))
                if not by_pe(g):
                    last.then_inc(pv_done, 1)

            def summed(n, g):
                t, r = g // GROUPS, g % GROUPS
                if r == PE_SUMS[0]:
                    pe.wait_ge(den_done, n * TILES + (t + 1))
                for j in range(4):
                    last = nc.tensor.matmul(ps[32 * j:32 * j + 32, PS_D, :], ones, probs[:, g % RING_P, j, :],
                                            start=(r == PE_SUMS[0]), stop=(r == PE_SUMS[-1]), tile_position=(0, 32 * j))
                last.then_inc(pv_done, 1)

            def fold(n):
                pe.wait_ge(o_copied, n * TILES + (TILES + 1))
                pe.wait_ge(den_done, n * TILES + (TILES + 1))
                at = 2 * (FOLD_PLACE % RING_S)
                for bank, w, a in ((at, cst[:, C_FOLD:C_FOLD + D], outT), (at + 1, ones, den)):
                    for t in range(TILES):
                        last = nc.tensor.matmul(ps[32 * t:32 * t + 32, bank, :], w, a[:, 512 * t:512 * t + 512],
                                                start=True, stop=True, tile_position=(0, 32 * t))
                last.then_inc(fold_done, 1)

            def run(n, hp, hb, half):
                first_run = isinstance(n, int) and n == 0
                pe.wait_ge(heads_loaded[hb], hp * 128 + 128)
                pe.wait_ge(vh_ready, hp * 4 + 2 * (hb + 1))
                for g in range(NG):
                    if g == FOLD_AT and not first_run:
                        ring_free(n, FOLD_PLACE)
                        fold(n - 1)
                    scores(n, hb, half, 2 * g)
                    if g >= LAG:
                        m, mb, w = n, hb, g - LAG
                    else:
                        m, mb, w = n - 1, hb if half else 1 - hb, NG + g - LAG
                    if g >= LAG or not first_run:
                        weighted(m, mb, w)
                    scores(n, hb, half, 2 * g + 1)
                    if by_pe(w) and (g >= LAG or not first_run):
                        summed(m, w)

            runs(pe, run)
            for g in range(NG - LAG, NG):
                weighted(RUNS - 1, 1, g)
                if by_pe(g):
                    summed(RUNS - 1, g)
            fold(RUNS - 1)


def layer_norm_tiles(nc, block, ctx, name, tok, normT, eps, cst, ps, stage, small, add, rows, use=None):
    NB = TT // 4

    def sem(n):
        return ctx.enter_context(nc.semaphore(name + n))

    step, var_ready, std_ready, norm_ready = sem("step"), sem("var_ready"), sem("std_ready"), sem("norm_ready")
    turned, turned_copied, add_ready, added = sem("turned"), sem("turned_copied"), sem("add_ready"), sem("added")
    norm = [stage[:, 1024 * b:1024 * b + 1024].rearrange("p (t c) -> p t c", t=4) for b in range(stage.shape[1] // 1024)]
    RING_N = len(norm)
    LOADS = 4
    loaded = [sem(f"loaded{n}") for n in range(LOADS)]
    stats = small[:, 0:24].rearrange("p (t n) -> p t n", n=6)
    mv = [small[:, 24 + 8 * b:32 + 8 * b].rearrange("p (t n) -> p t n", n=2) for b in range(2)]
    std = [small[:, 40 + 4 * b:44 + 4 * b] for b in range(2)]

    @block.sync
    def _(sp):
        T = TT // LOADS
        for n in range(LOADS):
            sp.dma_start(tok[:, T * n:T * n + T, :], rows[P * T * n:P * T * (n + 1), :].rearrange("(t p) c -> p t c", p=P)
                         ).then_inc(loaded[n], 16)

    @block.vector
    def _(dve):
        ch = Chain(dve, step)
        for n in range(NB + 1):
            if n < NB:
                b = n % 2
                if n >= 2:
                    dve.wait_ge(norm_ready, 4 * (n - 1))
                t4 = tok[:, 4 * n:4 * n + 4, :]
                dve.wait_ge(loaded[n * LOADS // NB], 16)
                if add is not None:
                    dve.wait_ge(add_ready, n + 1)
                    nc.vector.tensor_tensor(out=t4, in0=t4, in1=ps[:, 2 * b:2 * b + 2, :].rearrange("p b (t c) -> p (b t) c", c=C),
                                            op=ALU.add).then_inc(added, 1)
                    dve.wait_ge(added, n + 1)
                ch.wait()
                for t in range(4):
                    ch.step(nc.vector.bn_stats(stats[:, t, :], t4[:, t, :]))
                ch.wait()
                for t in range(4):
                    ch.step(nc.vector.bn_aggr(mv[b][:, t, :], stats[:, t, :]))
                ch.wait()
                nc.vector.tensor_copy(std[b], mv[b][:, :, 1]).then_inc(var_ready, 1)
            if n >= 1:
                m, b = n - 1, (n - 1) % 2
                dve.wait_ge(std_ready, m + 1)
                ch.link(nc.vector.reciprocal(std[b], std[b]))
                if m >= RING_N:
                    dve.wait_ge(turned, m - RING_N + 1)
                for t in range(4):
                    nc.vector.tensor_scalar(norm[m % RING_N][:, t, :], tok[:, 4 * m + t, :], mv[b][:, t, 0:1], std[b][:, t:t + 1],
                                            op0=ALU.subtract, op1=ALU.mult).then_inc(norm_ready, 1)

    @block.scalar
    def _(act):
        for n in range(NB + 1):
            if n < NB:
                act.wait_ge(var_ready, n + 1)
                nc.scalar.activation(std[n % 2], std[n % 2], ACT.Sqrt, bias=eps[:, 1:2]).then_inc(std_ready, 1)
            if n >= 1:
                m = n - 1
                act.wait_ge(turned, m + 1)
                for k in range(KC):
                    nc.scalar.activation(normT[:, k, 512 * m:512 * m + 512], ps[:, 4 + 2 * (m % 2) + k, :], ACT.Copy).then_inc(turned_copied, 1)

    @block.tensor
    def _(pe):
        if add is not None:
            add(pe, 0, 0).then_inc(add_ready, 1)
        for n in range(NB + 2):
            if n < NB - 1 and add is not None:
                if n >= 1:
                    pe.wait_ge(added, n)
                add(pe, n + 1, 2 * ((n + 1) % 2)).then_inc(add_ready, 1)
            if 1 <= n <= NB:
                m, b = n - 1, (n - 1) % 2
                pe.wait_ge(norm_ready, 4 * (m + 1))
                if m >= 2:
                    pe.wait_ge(turned_copied, KC * (m - 1))
                for t in range(4):
                    for k in range(KC):
                        last = nc.tensor.transpose(ps[:, 4 + 2 * b + k, P * t:P * t + P], norm[m % RING_N][:, t, P * k:P * k + P],
                                                   cst[:, C_ID:C_ID + P])
                last.then_inc(turned, 1)
            if n >= 2 and use is not None:
                pe.wait_ge(turned_copied, KC * (n - 1))
                use(pe, n - 2)


def project_and_norm(nc, ctx, ps, big, cst, eps, xT, wprojT):
    image = big[1].rearrange("p (f j c) -> p f j c", f=2, j=SUB)
    tok = big[5].rearrange("p (t c) -> p t c", c=C)
    normT = big[2].rearrange("p (k s) -> p k s", k=KC)
    wp = big[4][:, 0:KC * C].rearrange("p (k c) -> p k c", k=KC)
    wp_loaded = ctx.enter_context(nc.semaphore("wp_loaded"))

    def add(pe, n, bank):
        if n == 0:
            pe.wait_ge(wp_loaded, 16)
        for t in range(4):
            i = 4 * n + t
            for f in range(2):
                last = nc.tensor.matmul(ps[:, bank + t // 2, C * (t % 2):C * (t % 2) + C],
                                        image[:, f, i // 2, P * (i % 2):P * (i % 2) + P], wp[:, f, :],
                                        start=(f == 0), stop=(f == 1))
        return last

    with nc.Block() as block:
        layer_norm_tiles(nc, block, ctx, "ln1_", tok, normT, eps, cst, ps, big[3][:, 0:2048], big[4][:, 4096:4160], add, xT)

        @block.gpsimd
        def _(pool):
            pool.dma_start(wp[:, :, :], wprojT.rearrange("(k p) c -> p k c", p=P)).then_inc(wp_loaded, 16)


def qkv_1(nc, ctx, ps, big, wq, wk, wv, bq, bk, bv, q1_scr, tok_scr, k_parts, v_parts):
    normT = big[2].rearrange("p (k s) -> p k s", k=KC)
    k_hi, k_lo = (a.rearrange("p (k s) -> p k s", k=KC) for a in k_parts)
    tok = big[5].rearrange("p (t c) -> p t c", c=C)
    wts = [big[4][:, 512 * n:512 * n + 512].rearrange("p (k c) -> p k c", k=KC) for n in range(3)]
    bvb = big[4][:, 1536:2048]
    bcol = big[4][:, 2048:2052]
    v_sum = big[4][:, 4608:5120]
    qst = [big[4][:, 2560 + 512 * n:3072 + 512 * n] for n in range(4)]

    def sem(n):
        return ctx.enter_context(nc.semaphore("qkv1_" + n))

    loaded, ready, moved, stored = sem("loaded"), sem("ready"), sem("moved"), [sem(f"stored{n}") for n in range(4)]
    tok_stored, step = sem("tok_stored"), sem("step")
    NQ = KC * ST
    NV = TT // 2

    def bank(n):
        return n % 8

    def product(n):
        for k in range(KC):
            if n < 2 * NQ:
                o, st = (n % NQ) // ST, n % ST
                yield (ps[:, bank(n), :], wts[n // NQ][:, k, P * o:P * o + P], normT[:, k, 512 * st:512 * st + 512], k)

    with nc.Block() as block:
        @block.sync
        def _(sp):
            for w, t in ((wq, wts[0]), (wk, wts[1]), (wv, wts[2])):
                sp.dma_start(t[:, :, :], w.rearrange("(k p) c -> p k c", p=P)).then_inc(loaded, 16)
            for n, b in enumerate((bq, bk)):
                sp.dma_start(bcol[:, 2 * n:2 * n + 2], b).then_inc(loaded, 16)
            sp.dma_start(bvb, bv).then_inc(loaded, 16)
            sp.dma_start(tok_scr.rearrange("(t p) c -> p t c", p=P), tok[:, :, :]).then_inc(tok_stored, 16)
            for n in range(NQ):
                o, st = n // ST, n % ST
                sp.wait_ge(moved, n + 1)
                sp.dma_start(q1_scr[4 * st:4 * st + 4, :, o, :].rearrange("t p s -> p t s"),
                             qst[n % 4].rearrange("p (t s) -> p t s", t=4)).then_inc(stored[n % 4], 16)
            for n in range(4):
                sp.wait_ge(stored[n], 16 * NQ // 4)
            sp.wait_ge(tok_stored, 16)

        @block.tensor
        def _(pe):
            pe.wait_ge(loaded, 96)
            for n in range(2 * NQ):
                if n >= 8:
                    pe.wait_ge(moved, n - 7)
                for o, l, r, k in product(n):
                    last = nc.tensor.matmul(o, l, r, start=(k == 0), stop=(k == KC - 1))
                last.then_inc(ready, 1)
            for m in range(NV):
                n = 2 * NQ + m
                pe.wait_ge(moved, n - 7)
                for u in range(2):
                    t = 2 * m + u
                    for k in range(KC):
                        last = nc.tensor.matmul(ps[:, bank(n), C * u:C * u + C], normT[:, k, P * t:P * t + P],
                                                wts[2][:, k, :], start=(k == 0), stop=(k == KC - 1))
                last.then_inc(ready, 1)

        @block.vector
        def _(dve):
            ch = Chain(dve, step)
            dve.wait_ge(loaded, 96)
            for n in range(2 * NQ + NV):
                dve.wait_ge(ready, n + 1)
                o, st = (n % NQ) // ST, n % ST
                bias = bcol[:, 2 * (n // NQ) + o:][:, 0:1] if n < 2 * NQ else None
                if n < NQ:
                    if n >= 4:
                        dve.wait_ge(stored[n % 4], 16 * (n // 4))
                    nc.vector.tensor_scalar(qst[n % 4], ps[:, bank(n), :], bias, None, op0=ALU.add).then_inc(moved, 1)
                elif n < 2 * NQ:
                    hi, lo = (k[:, o, 512 * st:512 * st + 512] for k in (k_hi, k_lo))
                    ch.link(nc.vector.tensor_scalar(hi, ps[:, bank(n), :], bias, None, op0=ALU.add))
                    nc.vector.scalar_tensor_tensor(out=lo, in0=ps[:, bank(n), :], scalar=bias, in1=hi.bitcast(F32),
                                                   op0=ALU.add, op1=ALU.subtract).then_inc(moved, 1)
                else:
                    m = n - 2 * NQ
                    hi, lo = (a[:, 512 * m:512 * m + 512] for a in v_parts)
                    ch.wait()
                    nc.vector.tensor_tensor(out=v_sum, in0=ps[:, bank(n), :], in1=bvb, op=ALU.add).then_inc(moved, 1)
                    dve.wait_ge(moved, n + 1)
                    ch.link(nc.vector.tensor_copy(hi, v_sum))
                    dve.wait_ge(tok_stored, 16)
                    ch.step(nc.vector.tensor_tensor(out=lo, in0=v_sum, in1=hi.bitcast(F32), op=ALU.subtract))


def attention_1(nc, ctx, ps, big, extra, cst, q1_scr, tok_scr, q_parts, k_parts, v_parts, w_parts):
    ident, ones = cst[:, C_ID:C_ID + P], cst[:, C_ALL:C_ALL + P]
    k_hi, k_lo = (a.rearrange("p (k s) -> p k s", k=KC) for a in k_parts)
    v_hi, v_lo = (a.rearrange("p (t c) -> p t c", c=C) for a in v_parts)
    score = big[2][:, 0:S]
    work = [big[2][:, S:2 * S], big[4][:, 0:S]]
    RING_W = 4
    w_hi, w_lo = ([w_parts[:, 1024 * r + 512 * a:][:, 0:512] for r in range(RING_W)] for a in range(2))
    wT = [extra[:, 512 * n:512 * n + 512] for n in range(2)]
    tok = [extra[:, 1024 + C * b:1024 + C * b + C] for b in range(2)]
    qT = extra[:, 1536:1792]
    q_hi, q_lo = q_parts[:, 0:C], q_parts[:, C:2 * C]
    pieces = extra[:, 1792:2048]
    sm = extra[:, 2048:2128]
    top = [sm[:, TOPK * b:TOPK * b + TOPK] for b in range(2)]
    negmax, total, fail = ([sm[:, 64 + 2 * n + b:65 + 2 * n + b] for b in range(2)] for n in range(3))
    eighth, left = sm[:, 70:71], sm[:, 71:72]
    fails = sm[:, 72:73].bitcast(I32)
    CH = S // 512
    RING_S, RING_T = 4, 2
    PS_T, PS_A, PS_F = 4, 6, 7
    PAIRS = TT // 2 - 1
    PIECE = 128
    LAG = 2
    EXPS = 4

    def sem(n):
        return ctx.enter_context(nc.semaphore("a1_" + n))

    q_loaded = sem("q_loaded")
    passed, s_ready, s_copied, top_step = sem("passed"), sem("s_ready"), sem("s_copied"), sem("top_step")
    exp_may, exp_done, w_ready = sem("exp_may"), sem("exp_done"), sem("w_ready")
    fail_ready, fails_ready, fails_step, whole_step, inv_step = (
        sem("fail_ready"), sem("fails_ready"), sem("fails_step"), sem("whole_step"), sem("inv_step"))
    t_ready, hi_ready, lo_ready, v_done, o_done = sem("t_ready"), sem("hi_ready"), sem("lo_ready"), sem("v_done"), sem("o_done")
    q_may, q_hi_ready, q_split = sem("q_may"), sem("q_hi_ready"), sem("q_split")
    tok_loaded, tok_stored = ([sem(f"tok_{n}_even"), sem(f"tok_{n}_odd")] for n in ("loaded", "stored"))

    with nc.Block() as block:
        @block.sync
        def _(sp):
            def load_q(n):
                sp.dma_start(qT.rearrange("p (k s) -> p k s", k=KC), q1_scr[n, :, :, :].rearrange("t p k s -> (t p) k s")
                             ).then_inc(q_loaded, 16)

            def load_tok(n, b):
                sp.dma_start(tok[b], tok_scr[n, :]).then_inc(tok_loaded[b], 16)

            def store_tok(n, b):
                sp.wait_ge(o_done, n + 3)
                sp.dma_start(tok_scr[bass.ds(n * P, P), :], tok[b]).then_inc(tok_stored[b], 16)

            for b in range(2):
                if b == 1:
                    sp.wait_ge(q_split, 1)
                load_q(slice(b, b + 1))
                load_tok(slice(P * b, P * b + P), b)
            with sp.Fori(0, PAIRS) as r:
                for b in range(2):
                    n = r * 2 + b
                    sp.wait_ge(q_split, n + 2)
                    load_q(bass.ds(n + 2, 1))
                    store_tok(n, b)
                    sp.wait_ge(tok_stored[b], r * 16 + 16)
                    load_tok(bass.ds(n * P + 2 * P, P), b)
            for b in range(2):
                store_tok(TT - 2 + b, b)
            for b in range(2):
                sp.wait_ge(tok_stored[b], 16 * TT // 2)

        @block.gpsimd
        def _(pool):
            def split_q(n):
                pool.wait_ge(q_loaded, n * 16 + 16)
                pool.wait_ge(s_ready, n * CH + 2 * CH)
                pool.sem_inc(q_may, 1)
                nc.gpsimd.tensor_copy(q_hi, qT).then_inc(q_hi_ready, 1)
                pool.wait_ge(q_hi_ready, n + 1)
                nc.gpsimd.tensor_tensor(out=q_lo, in0=qT, in1=q_hi.bitcast(F32), op=ALU.subtract).then_inc(q_split, 1)

            def second_part(n, c):
                pool.wait_ge(hi_ready, n * CH + (RING_T + c + 1))
                nc.gpsimd.tensor_tensor(out=w_lo[c % RING_W], in0=wT[c % 2], in1=w_hi[c % RING_W].bitcast(F32),
                                        op=ALU.subtract).then_inc(lo_ready, 1)

            def tile(n, more=True):
                for c in range(CH):
                    if c == CH // 2 and more:
                        split_q(n + 2)
                    second_part(n, c)

            for b in range(2):
                split_q(b)
            with pool.Fori(0, PAIRS) as r:
                for b in range(2):
                    tile(r * 2 + b)
            for b in range(2):
                tile(TT - 2 + b, more=False)

        @block.tensor
        def _(pe):
            pe.sem_inc(v_done, RING_W)
            pe.sem_inc(hi_ready, RING_T)
            pe.sem_inc(lo_ready, 2)
            pe.sem_inc(s_ready, 2 * CH)

            def in_parts(out, left_hi, left_lo, right_hi, right_lo, start, stop):
                nc.tensor.matmul(out, left_hi, right_hi, start=start, stop=False)
                nc.tensor.matmul(out, left_hi, right_lo, start=False, stop=False)
                return nc.tensor.matmul(out, left_lo, right_hi, start=False, stop=stop)

            def scores(n, c):
                if c == 0:
                    pe.wait_ge(q_split, n + 1)
                pe.wait_ge(s_copied, n * CH + (c + 1))
                for k in range(KC):
                    cols = slice(512 * c, 512 * c + 512)
                    last = in_parts(ps[:, c % RING_S, :], q_hi[:, P * k:P * k + P], q_lo[:, P * k:P * k + P],
                                    k_hi[:, k, cols], k_lo[:, k, cols], k == 0, k == KC - 1)
                last.then_inc(s_ready, 1)

            def values(n, c):
                pe.wait_ge(lo_ready, n * CH + (c + 3))
                if c == 0:
                    pe.wait_ge(o_done, n + 2)
                for u in range(4):
                    t = 4 * c + u
                    last = in_parts(ps[:, PS_A, 0:C], w_hi[c % RING_W][:, P * u:P * u + P], w_lo[c % RING_W][:, P * u:P * u + P],
                                    v_hi[:, t, :], v_lo[:, t, :], t == 0, t == TT - 1)
                last.then_inc(v_done, 1)

            def count_fails(n, b):
                pe.wait_ge(fail_ready, n + 1)
                nc.tensor.matmul(ps[:, PS_F, 0:1], ones, fail[b], start=True, stop=True).then_inc(fails_ready, 1)

            def turn(n, b, c):
                if c == 0:
                    pe.wait_ge(w_ready, n + 1)
                pe.wait_ge(hi_ready, n * CH + (c + 1))
                for u in range(4):
                    t = 4 * c + u
                    last = nc.tensor.transpose(ps[:, PS_T + c % RING_T, P * u:P * u + P], work[b][:, P * t:P * t + P], ident)
                last.then_inc(t_ready, 1)

            def tile(n, b, scores_too=True, next_turns=True):
                for c in range(LAG, CH):
                    if c == CH - 2 and next_turns:
                        count_fails(n + 1, 1 - b)
                    turn(n, b, c)
                    values(n, c - LAG)
                for c in range(CH):
                    if c >= CH - LAG and next_turns:
                        turn(n + 1, 1 - b, c - (CH - LAG))
                    if scores_too:
                        scores(n + 2, c)
                    if c < LAG:
                        values(n, CH - LAG + c)

            for c in range(CH):
                scores(0, c)
            count_fails(0, 0)
            for c in range(CH):
                if c >= CH - LAG:
                    turn(0, 0, c - (CH - LAG))
                scores(1, c)
            with pe.Fori(0, PAIRS) as r:
                for b in range(2):
                    tile(r * 2 + b, b)
            tile(TT - 2, 0, scores_too=False)
            tile(TT - 1, 1, scores_too=False, next_turns=False)

        @block.scalar
        def _(act):
            act.sem_inc(s_copied, RING_S)

            def copy_scores(n, c):
                if c == 0 and (not isinstance(n, int) or n > 0):
                    act.wait_ge(w_ready, n)
                act.wait_ge(s_ready, n * CH + (2 * CH + c + 1))
                nc.scalar.activation(score[:, 512 * c:512 * c + 512], ps[:, c % RING_S, :], ACT.Copy).then_inc(s_copied, 1)

            def exponentials(n, b, part):
                if part == 0:
                    act.wait_ge(exp_may, n + 1)
                cols = slice(S // EXPS * part, S // EXPS * (part + 1))
                nc.scalar.activation(work[b][:, cols], score[:, cols], ACT.Exp, bias=negmax[b]).then_inc(exp_done, 1)

            def split_weights(n, c):
                act.wait_ge(v_done, n * CH + (c + 1))
                act.wait_ge(t_ready, n * CH + (c + 1))
                act.wait_ge(lo_ready, n * CH + (c + 1))
                nc.scalar.activation(wT[c % 2], ps[:, PS_T + c % RING_T, :], ACT.Copy)
                nc.scalar.activation(w_hi[c % RING_W], ps[:, PS_T + c % RING_T, :], ACT.Copy).then_inc(hi_ready, 1)

            def tile(n, b, scores_too=True, next_weights=True):
                for c in range(LAG, CH):
                    split_weights(n, c)
                    if c < LAG + EXPS and next_weights:
                        exponentials(n + 1, 1 - b, c - LAG)
                for c in range(CH):
                    if c >= CH - LAG and next_weights:
                        split_weights(n + 1, c - (CH - LAG))
                    if scores_too:
                        copy_scores(n + 2, c)

            for c in range(CH):
                copy_scores(0, c)
            for part in range(EXPS):
                exponentials(0, 0, part)
            for c in range(CH):
                if c >= CH - LAG:
                    split_weights(0, c - (CH - LAG))
                copy_scores(1, c)
            with act.Fori(0, PAIRS) as r:
                for b in range(2):
                    tile(r * 2 + b, b)
            tile(TT - 2, 0, scores_too=False)
            tile(TT - 1, 1, scores_too=False, next_weights=False)

        @block.vector
        def _(dve):
            dve.sem_inc(o_done, 2)
            TAKE_STEPS, WHOLE_STEPS = 11, TOPK // 4

            def pass_waits():
                dve.sem_inc(passed, 1)

            def take_top(n, b):
                ch = Chain(dve, top_step, n * TAKE_STEPS)
                for c in range(CH):
                    dve.wait_ge(s_copied, n * CH + (RING_S + c + 1))
                    pass_waits()
                    for g in range(4 * c, 4 * c + 4):
                        ins = nc.vector.max(pieces[:, 8 * g:8 * g + 8], score[:, PIECE * g:PIECE * g + PIECE])
                ch.link(ins)
                ch.step(nc.vector.tensor_reduce(eighth, pieces.rearrange("p (g e) -> p g e", e=8)[:, :, 7], axis=AX_X, op=ALU.max))
                for a in range(TOPK // 8):
                    eight = top[b][:, 8 * a:8 * a + 8]
                    pass_waits()
                    ch.link(nc.vector.max(eight, pieces))
                    if a == 0:
                        nc.vector.tensor_scalar(negmax[b], top[b][:, 0:1], -1.0, None, op0=ALU.mult).then_inc(exp_may, 1)
                    pass_waits()
                    ch.link(nc.vector.match_replace(pieces, eight, pieces, TAKEN))
                ch.link(nc.vector.tensor_reduce(left, pieces, axis=AX_X, op=ALU.max))
                assert ch.n == TAKE_STEPS
                nc.vector.scalar_tensor_tensor(out=fail[b], in0=eighth, scalar=left, in1=top[b][:, TOPK - 1:TOPK],
                                               op0=ALU.max, op1=ALU.is_ge).then_inc(fail_ready, 1)

            def weigh(n, b):
                dve.wait_ge(fails_ready, n + 1)
                nc.vector.tensor_copy(fails, ps[:, PS_F, 0:1]).then_inc(fails_step, 1)
                dve.wait_ge(fails_step, n + 1)
                pass_waits()
                failed = dve.value_load(fails[0:1, :], min_val=0, max_val=P)
                dve.wait_ge(exp_done, n * EXPS + EXPS)
                dve.wait_ge(o_done, n + 1)
                pass_waits()
                with dve.If(failed > 0):
                    ch = Chain(dve, whole_step, n * WHOLE_STEPS)
                    for a in range(TOPK // 8):
                        eight = top[b][:, 8 * a:8 * a + 8]
                        pass_waits()
                        ch.link(nc.vector.max(eight, score))
                        pass_waits()
                        ch.link(nc.vector.match_replace(score, eight, score, TAKEN))
                    assert ch.n == WHOLE_STEPS
                    nc.vector.scalar_tensor_tensor(out=work[b], in0=score, scalar=TAKEN, in1=work[b],
                                                   op0=ALU.is_equal, op1=ALU.mult, accum_out=total[b]).then_inc(w_ready, 1)
                with dve.Else():
                    dve.sem_inc(whole_step, WHOLE_STEPS)
                    nc.vector.scalar_tensor_tensor(out=work[b], in0=score, scalar=top[b][:, TOPK - 1:TOPK], in1=work[b],
                                                   op0=ALU.is_ge, op1=ALU.mult, accum_out=total[b]).then_inc(w_ready, 1)

            def add_output(n, b, loads):
                dve.wait_ge(w_ready, n + 1)
                nc.vector.reciprocal(total[b], total[b]).then_inc(inv_step, 1)
                dve.wait_ge(inv_step, n + 1)
                dve.wait_ge(tok_loaded[b], loads)
                dve.wait_ge(v_done, n * CH + (RING_W + CH))
                nc.vector.scalar_tensor_tensor(out=tok[b], in0=ps[:, PS_A, 0:C], scalar=total[b], in1=tok[b],
                                               op0=ALU.mult, op1=ALU.add).then_inc(o_done, 1)

            for b in range(2):
                take_top(b, b)
                weigh(b, b)
            with dve.Fori(0, PAIRS) as r:
                for b in range(2):
                    n = r * 2 + b
                    add_output(n, b, r * 16 + 16)
                    take_top(n + 2, b)
                    weigh(n + 2, b)
            for b in range(2):
                add_output(TT - 2 + b, b, 16 * TT // 2)


def norm_and_route(nc, ctx, ps, big, cst, eps, weight, position, slot_expert, wg, bg, b2, x_slots, tok_scr, load_weights):
    tok = big[5].rearrange("p (t c) -> p t c", c=C)
    normT = big[2].rearrange("p (k s) -> p k s", k=KC)
    rows = big[3].rearrange("p (t c) -> p t c", c=C)
    area = big[4]
    at = [64]

    def take(n, lead=None, **dims):
        a = area[:, at[0]:at[0] + n]
        at[0] += n
        return a.rearrange(lead, **dims) if lead else a

    TE = "p (t e) -> p t e"
    wg_t = take(KC * NE, "p (k e) -> p k e", k=KC)
    bg_t = take(NE)
    b2_t = take(C)[0:NE, :]
    logit, best, hit0, hit1, hits, gate, before, count, upto, place = (take(TT * NE, TE, e=NE) for _ in range(10))
    where = take(TT * NE, TE, e=NE).bitcast(U32)
    wheref, pair = (take(TT * 2, TE, e=2) for _ in range(2))
    posf = [take(TT) for _ in range(2)]
    needs = take(NE * NK, "p (e k) -> p e k", k=NK)
    slots, slots_end, slots_at = (take(NE) for _ in range(3))
    passed = take(NS * NE, "p (s e) -> p s e", e=NE)
    owner = take(NS)
    gateT = big[0][0:NE, 0:S]
    iota = cst[:, C_IOTA:C_IOTA + NE]

    def sem(n):
        return ctx.enter_context(nc.semaphore("gate_" + n))

    wg_loaded = sem("wg_loaded")

    def gate_logits(pe, n):
        if n == 0:
            pe.wait_ge(wg_loaded, 16)
        for t in range(4 * n, 4 * n + 4):
            for k in range(KC):
                nc.tensor.matmul(ps[:, 0, NE * t:NE * t + NE], normT[:, k, P * t:P * t + P], wg_t[:, k, :],
                                 start=(k == 0), stop=(k == KC - 1))

    with nc.Block() as block:
        layer_norm_tiles(nc, block, ctx, "ln2_", tok, normT, eps, cst, ps, big[3], big[4][:, 0:64], None, tok_scr, gate_logits)

        @block.gpsimd
        def _(pool):
            pool.dma_start(wg_t[:, :, :], wg.rearrange("(k p) e -> p k e", p=P)).then_inc(wg_loaded, 16)
            pool.wait_ge(wg_loaded, 16)

    loaded, step, diff, ratio, gates = sem("loaded"), sem("step"), sem("diff"), sem("ratio"), sem("gates")
    turned, turned_copied, b2_ready, b2_added = sem("turned"), sem("turned_copied"), sem("b2_ready"), sem("b2_added")
    hits_ready, counts_ready, routed, scattered = sem("hits_ready"), sem("counts_ready"), sem("routed"), sem("scattered")

    with nc.Block() as block:
        @block.sync
        def _(sp):
            sp.dma_start(bg_t, bg).then_inc(loaded, 16)
            sp.dma_start(b2_t, b2).then_inc(loaded, 16)
            sp.wait_ge(routed, 1)
            for b in range(2):
                load_weights(sp, b, b)

        @block.gpsimd
        def _(pool):
            pool.wait_ge(routed, 1)
            for t in range(TT):
                for a in range(2):
                    pool.indirect_dma_start(out=x_slots, out_offset=bass.IndirectOffsetOnAxis(ap=position[a][:, t:t + 1], axis=0),
                                            in_=rows[:, t, :], in_offset=None).then_inc(scattered, 16)
            pool.wait_ge(scattered, 16 * 2 * TT)

        @block.tensor
        def _(pe):
            pe.wait_ge(loaded, 32)
            pe.wait_ge(hits_ready, 1)
            for bank, c in ((1, C_BEFORE), (2, C_ALL)):
                last = nc.tensor.matmul(ps[:, bank, 0:TT * NE], cst[:, c:c + P], hits.rearrange("p t e -> p (t e)"),
                                        start=True, stop=True)
            last.then_inc(counts_ready, 1)
            pe.wait_ge(gates, 1)
            for n in range(TT // 4):
                if n >= 2:
                    pe.wait_ge(turned_copied, n - 1)
                for u in range(4):
                    last = nc.tensor.transpose(ps[0:NE, 6 + n % 2, P * u:P * u + P], gate[:, 4 * n + u, :], cst[:, C_ID:C_ID + P])
                last.then_inc(turned, 1)
            for n in range(TT // 2):
                pe.wait_ge(turned_copied, n // 2 + 1)
                if n >= 3:
                    pe.wait_ge(b2_added, n - 2)
                for u in range(2):
                    t = 2 * n + u
                    last = nc.tensor.matmul(ps[:, 3 + n % 3, C * u:C * u + C], gateT[:, P * t:P * t + P], b2_t,
                                            start=True, stop=True)
                last.then_inc(b2_ready, 1)

        @block.scalar
        def _(act):
            act.wait_ge(diff, 1)
            nc.scalar.activation(pair[:, :, 1], pair[:, :, 1], ACT.Exp).then_inc(ratio, 1)
            for n in range(TT // 4):
                act.wait_ge(turned, n + 1)
                nc.scalar.activation(gateT[:, 512 * n:512 * n + 512], ps[0:NE, 6 + n % 2, :], ACT.Copy).then_inc(turned_copied, 1)

        @block.vector
        def _(dve):
            ch = Chain(dve, step)

            def by_token(a):
                return a.unsqueeze(2).to_broadcast([P, TT, NE])

            def by_expert(a):
                return a.unsqueeze(1).to_broadcast([P, TT, NE])

            dve.wait_ge(loaded, 32)
            ch.link(nc.vector.tensor_tensor(out=logit, in0=ps[:, 0, 0:TT * NE].rearrange(TE, e=NE),
                                            in1=by_expert(bg_t), op=ALU.add))
            for t in range(TT):
                ch.step(nc.vector.max(best[:, t, :], logit[:, t, :]))
            ch.wait()
            for t in range(TT):
                ch.step(nc.vector.max_index(where[:, t, :], best[:, t, :], logit[:, t, :]))
            ch.wait()
            ch.link(nc.vector.tensor_copy(wheref, where[:, :, 0:2]))
            nc.vector.tensor_tensor(out=pair[:, :, 1], in0=best[:, :, 1], in1=best[:, :, 0], op=ALU.subtract).then_inc(diff, 1)
            ch.step(nc.vector.tensor_tensor(out=hit0, in0=by_expert(iota), in1=by_token(wheref[:, :, 0]), op=ALU.is_equal))
            ch.link(nc.vector.tensor_tensor(out=hit1, in0=by_expert(iota), in1=by_token(wheref[:, :, 1]), op=ALU.is_equal))
            nc.vector.tensor_tensor(out=hits, in0=hit0, in1=hit1, op=ALU.add).then_inc(hits_ready, 1)
            dve.wait_ge(counts_ready, 1)
            ch.step(nc.vector.tensor_copy(before, ps[:, 1, 0:TT * NE].rearrange(TE, e=NE)))
            ch.link(nc.vector.tensor_copy(count, ps[:, 2, 0:TT * NE].rearrange(TE, e=NE)))
            ones = cst[:, C_ALL:C_ALL + TT]
            for e in range(NE):
                ch.step(nc.vector.tensor_tensor_scan(upto[:, :, e], ones, count[:, :, e], 0.0, op0=ALU.mult, op1=ALU.add))
            ch.wait()
            ch.step(nc.vector.tensor_tensor(out=before, in0=before, in1=upto, op=ALU.add))
            ch.link(nc.vector.tensor_tensor(out=needs, in0=upto[:, TT - 1, :].unsqueeze(2).to_broadcast([P, NE, NK]),
                                            in1=cst[:, C_STEP:C_STEP + NK].unsqueeze(1).to_broadcast([P, NE, NK]), op=ALU.is_gt))
            ch.step(nc.vector.tensor_tensor(out=before, in0=before, in1=count, op=ALU.subtract))
            ch.link(nc.vector.reduce_sum(slots, needs, AX_X))
            ch.link(nc.vector.tensor_tensor_scan(slots_end, ones[:, 0:NE], slots, 0.0, op0=ALU.mult, op1=ALU.add))
            ch.step(nc.vector.tensor_tensor(out=slots_at, in0=slots_end, in1=slots, op=ALU.subtract))
            ch.link(nc.vector.tensor_tensor(out=passed, in0=cst[:, C_SLOT:C_SLOT + NS].unsqueeze(2).to_broadcast([P, NS, NE]),
                                            in1=slots_end.unsqueeze(1).to_broadcast([P, NS, NE]), op=ALU.is_ge))
            ch.step(nc.vector.reduce_sum(owner, passed, AX_X))
            ch.link(nc.vector.tensor_scalar(slots_at, slots_at, float(SLOT), None, op0=ALU.mult))
            ch.step(nc.vector.tensor_scalar(slot_expert[:, :], owner, float(NE - 1), None, op0=ALU.min))
            ch.link(nc.vector.tensor_tensor(out=before, in0=before, in1=by_expert(slots_at), op=ALU.add))
            for a, hit in enumerate((hit0, hit1)):
                ch.link(nc.vector.tensor_tensor(out=place, in0=before, in1=hit, op=ALU.mult))
                ch.link(nc.vector.reduce_sum(posf[a], place, AX_X))
                ch.step(nc.vector.tensor_copy(position[a][:, :], posf[a]))
            ch.wait()
            dve.sem_inc(routed, 1)
            dve.wait_ge(ratio, 1)
            ch.link(nc.vector.tensor_scalar(pair[:, :, 0], pair[:, :, 1], 1.0, None, op0=ALU.add))
            ch.link(nc.vector.reciprocal(weight[:, :, 0], pair[:, :, 0]))
            ch.link(nc.vector.tensor_tensor(out=weight[:, :, 1], in0=pair[:, :, 1], in1=weight[:, :, 0], op=ALU.mult))
            ch.step(nc.vector.tensor_tensor(out=hit0, in0=hit0, in1=by_token(weight[:, :, 0]), op=ALU.mult))
            ch.link(nc.vector.tensor_tensor(out=hit1, in0=hit1, in1=by_token(weight[:, :, 1]), op=ALU.mult))
            nc.vector.tensor_tensor(out=gate, in0=hit0, in1=hit1, op=ALU.add).then_inc(gates, 1)
            for n in range(TT // 2):
                dve.wait_ge(b2_ready, n + 1)
                two = big[5][:, 512 * n:512 * n + 512]
                nc.vector.tensor_tensor(out=two, in0=two, in1=ps[:, 3 + n % 3, :], op=ALU.add).then_inc(b2_added, 1)


def experts(nc, ctx, ps, big, ident, slot_expert, b1, x_slots, y_slots, e_parts, h_parts, x_parts, w_loaded, load_weights):
    WN = KC * HID
    raw = [big[1][:, 2 * WN * b:2 * WN * b + 2 * WN] for b in range(2)]
    e_hi, e_lo = ([e[:, 2 * WN * a:2 * WN * a + 2 * WN] for e in e_parts] for a in range(2))
    h_hi, h_lo = (h_parts[:, 4096 * a:4096 * a + HC * SLOT].rearrange("p (h s) -> p h s", h=HC) for a in range(2))
    x_hi, x_lo = (x_parts[:, 1024 * a:1024 * a + KC * SLOT].rearrange("p (k s) -> p k s", k=KC) for a in range(2))
    b1_t = [big[4][:, 2048 + HC * b:2048 + HC * b + HC] for b in range(2)]
    hidden = [big[4][:, 2112 + 512 * r:2112 + 512 * r + SLOT] for r in range(2)]
    xr = [big[4][:, 4096 + 1024 * b:4096 + 1024 * b + SQ * C].rearrange("p (t c) -> p t c", c=C) for b in range(2)]
    yr = [big[4][:, 6144 + 1024 * b:6144 + 1024 * b + SQ * C] for b in range(2)]
    RING_H, PS_X, PS_O = 2, 2, 4
    PAIRS = (NS - 1) // 2
    PIECES = HC

    def w1_of(part, k, h):
        return part[:, HID * k + P * h:HID * k + P * h + P]

    def w2_of(part, h):
        return part[:, WN + C * h:WN + C * h + C]

    def sem(n):
        return ctx.enter_context(nc.semaphore("ffn_" + n))

    x_loaded, b1_loaded = ([sem(f"{n}_loaded{b}") for b in range(2)] for n in ("x", "b1"))
    w_hi_ready, w_split = sem("w_hi_ready"), sem("w_split")
    x_turned, x_hi_ready, x_split = sem("x_turned"), sem("x_hi_ready"), sem("x_split")
    h_ready, h_done, h_hi_ready, h_split = sem("h_ready"), sem("h_done"), sem("h_hi_ready"), sem("h_split")
    o_ready, o_copied = sem("o_ready"), sem("o_copied")
    stored = [sem(f"stored{b}") for b in range(2)]

    with nc.Block() as block:
        @block.sync
        def _(sp):
            def load_x(s, b):
                sp.dma_start(xr[b], x_slots[bass.ds(s * SLOT, SLOT), :].rearrange("(t p) c -> p t c", p=P)).then_inc(x_loaded[b], 16)

            def load_b1(e, b):
                sp.dma_start(b1_t[b], b1[bass.ds(e, 1), :, :].rearrange("e p h -> (e p) h")).then_inc(b1_loaded[b], 16)

            def next_loads(s, b):
                sp.wait_ge(w_split, s * PIECES + PIECES)
                e = load_weights(sp, s + 2, b)
                sp.wait_ge(x_turned, s + 1)
                load_x(s + 2, b)
                sp.wait_ge(h_done, s * HC + (RING_H + HC))
                load_b1(e, b)

            def store(s, b):
                sp.wait_ge(o_copied, s + 3)
                sp.dma_start(y_slots[bass.ds(s * SLOT, SLOT), :].rearrange("(t p) c -> p t c", p=P),
                             yr[b].rearrange("p (t c) -> p t c", c=C)).then_inc(stored[b], 16)

            for b in range(2):
                sp.sem_inc(stored[b], 16)
                load_x(b, b)
                load_b1(sp.value_load(slot_expert[0:1, b:b + 1], min_val=0, max_val=NE - 1), b)
            with sp.Fori(0, PAIRS - 1) as r:
                for b in range(2):
                    next_loads(r * 2 + b, b)
                    store(r * 2 + b, b)
            next_loads(NS - 3, 0)
            for s in range(NS - 3, NS):
                store(s, s % 2)
            sp.wait_ge(stored[0], 16 * (PAIRS + 2))
            sp.wait_ge(stored[1], 16 * (PAIRS + 1))

        @block.gpsimd
        def _(pool):
            def second_parts(s, b):
                for n in range(PIECES):
                    cols = slice(2 * WN // PIECES * n, 2 * WN // PIECES * (n + 1))
                    pool.wait_ge(w_hi_ready, s * PIECES + (n + 1))
                    nc.gpsimd.tensor_tensor(out=e_lo[b][:, cols], in0=raw[b][:, cols], in1=e_hi[b][:, cols].bitcast(F32),
                                            op=ALU.subtract).then_inc(w_split, 1)

            with pool.Fori(0, PAIRS) as r:
                for b in range(2):
                    second_parts(r * 2 + b, b)
            second_parts(NS - 1, 0)

        @block.tensor
        def _(pe):
            pe.sem_inc(o_ready, 1)

            def in_parts(out, left_hi, left_lo, right_hi, right_lo, start, stop):
                nc.tensor.matmul(out, left_hi, right_hi, start=start, stop=False)
                nc.tensor.matmul(out, left_hi, right_lo, start=False, stop=False)
                return nc.tensor.matmul(out, left_lo, right_hi, start=False, stop=stop)

            def turn(s, b, loads):
                pe.wait_ge(x_loaded[b], 16 * loads)
                if not isinstance(s, int):
                    pe.wait_ge(x_split, s)
                for k in range(KC):
                    for t in range(SQ):
                        last = nc.tensor.transpose(ps[:, PS_X + k, P * t:P * t + P], xr[b][:, t, P * k:P * k + P], ident)
                last.then_inc(x_turned, 1)

            def up(s, b):
                pe.wait_ge(w_split, s * PIECES + PIECES)
                pe.wait_ge(x_split, s + 1)
                for h in range(HC):
                    pe.wait_ge(h_done, s * HC + (h + 1))
                    for k in range(KC):
                        last = in_parts(ps[:, h % RING_H, 0:SLOT], w1_of(e_hi[b], k, h), w1_of(e_lo[b], k, h),
                                        x_hi[:, k, :], x_lo[:, k, :], k == 0, k == KC - 1)
                    last.then_inc(h_ready, 1)

            def down(s, b):
                pe.wait_ge(o_copied, s + 1)
                for half, h in ((half, h) for half in range(2) for h in range(HC)):
                    if half == 0:
                        pe.wait_ge(h_split, s * HC + (h + 3))
                    for t in range(half, SQ, 2):
                        last = in_parts(ps[:, PS_O + 2 * b + t // 2, C * (t % 2):C * (t % 2) + C],
                                        h_hi[:, h, P * t:P * t + P], h_lo[:, h, P * t:P * t + P],
                                        w2_of(e_hi[b], h), w2_of(e_lo[b], h), h == 0, h == HC - 1)
                last.then_inc(o_ready, 1)

            turn(0, 0, 1)
            with pe.Fori(0, PAIRS) as r:
                for b in range(2):
                    up(r * 2 + b, b)
                    turn(r * 2 + (b + 1), 1 - b, r + (b + 1))
                    down(r * 2 + b, b)
            up(NS - 1, 0)
            down(NS - 1, 0)

        @block.scalar
        def _(act):
            act.sem_inc(h_done, RING_H)
            act.sem_inc(h_split, 2)

            def first_part(s, b, n, loads):
                if n == 0:
                    act.wait_ge(w_loaded[b], 32 * loads)
                    if not isinstance(s, int):
                        act.wait_ge(o_ready, s)
                cols = slice(2 * WN // PIECES * n, 2 * WN // PIECES * (n + 1))
                nc.scalar.activation(e_hi[b][:, cols], raw[b][:, cols], ACT.Copy).then_inc(w_hi_ready, 1)

            def gelu(s, b, h, loads):
                if h == 0:
                    act.wait_ge(b1_loaded[b], 16 * loads)
                act.wait_ge(h_ready, s * HC + (h + 1))
                act.wait_ge(h_split, s * HC + (h + 1))
                nc.scalar.activation(hidden[h % 2], ps[:, h % RING_H, 0:SLOT], ACT.Gelu, bias=b1_t[b][:, h:h + 1]).then_inc(h_done, 1)

            for n in range(PIECES):
                first_part(0, 0, n, 1)
            with act.Fori(0, PAIRS) as r:
                for b in range(2):
                    for h in range(HC):
                        gelu(r * 2 + b, b, h, r + 1)
                        first_part(r * 2 + (b + 1), 1 - b, h, r + (b + 1))
            for h in range(HC):
                gelu(NS - 1, 0, h, PAIRS + 1)

        @block.vector
        def _(dve):
            dve.sem_inc(o_copied, 2)

            def split_x(s):
                dve.wait_ge(x_turned, s + 1)
                nc.vector.tensor_copy(x_hi, ps[:, PS_X:PS_X + KC, 0:SLOT]).then_inc(x_hi_ready, 1)
                dve.wait_ge(x_hi_ready, s + 1)
                nc.vector.tensor_tensor(out=x_lo, in0=ps[:, PS_X:PS_X + KC, 0:SLOT], in1=x_hi.bitcast(F32),
                                        op=ALU.subtract).then_inc(x_split, 1)

            def split_h(s):
                for h in range(HC):
                    dve.wait_ge(h_done, s * HC + (h + 3))
                    nc.vector.tensor_copy(h_hi[:, h, :], hidden[h % 2]).then_inc(h_hi_ready, 1)
                    dve.wait_ge(h_hi_ready, s * HC + (h + 1))
                    nc.vector.tensor_tensor(out=h_lo[:, h, :], in0=hidden[h % 2], in1=h_hi[:, h, :].bitcast(F32),
                                            op=ALU.subtract).then_inc(h_split, 1)

            def copy_o(s, b, stores):
                dve.wait_ge(o_ready, s + 2)
                dve.wait_ge(stored[b], 16 * stores + 16)
                nc.vector.tensor_copy(yr[b], ps[:, PS_O + 2 * b:PS_O + 2 * b + 2, :].rearrange("p k c -> p (k c)")[:, 0:SQ * C]
                                      ).then_inc(o_copied, 1)

            split_x(0)
            with dve.Fori(0, PAIRS) as r:
                for b in range(2):
                    split_h(r * 2 + b)
                    split_x(r * 2 + (b + 1))
                    copy_o(r * 2 + b, b, r)
            split_h(NS - 1)
            copy_o(NS - 1, 0, PAIRS)


def combine(nc, ctx, big, weight, position, y_slots, out):
    tok = big[5].rearrange("p (t c) -> p t c", c=C)
    RING = 8
    rows = [big[3][:, C * b:C * b + C] for b in range(RING)]
    PART = 8

    def sem(n):
        return ctx.enter_context(nc.semaphore("out_" + n))

    fetched = [sem(f"fetched{b}") for b in range(RING)]
    added, stored = sem("added"), sem("stored")

    with nc.Block() as block:
        @block.gpsimd
        def _(pool):
            for n in range(2 * TT):
                if n >= RING:
                    pool.wait_ge(added, n - RING + 1)
                pool.indirect_dma_start(out=rows[n % RING], out_offset=None, in_=y_slots,
                                        in_offset=bass.IndirectOffsetOnAxis(ap=position[n % 2][:, n // 2:n // 2 + 1], axis=0)
                                        ).then_inc(fetched[n % RING], 16)

        @block.vector
        def _(dve):
            for n in range(2 * TT):
                t, a = n // 2, n % 2
                dve.wait_ge(fetched[n % RING], 16 * (n // RING + 1))
                if a:
                    dve.wait_ge(added, n)
                nc.vector.scalar_tensor_tensor(out=tok[:, t, :], in0=rows[n % RING], scalar=weight[:, t, a:a + 1],
                                               in1=tok[:, t, :], op0=ALU.mult, op1=ALU.add).then_inc(added, 1)

        @block.sync
        def _(sp):
            for n in range(TT // PART):
                sp.wait_ge(added, 2 * PART * (n + 1))
                sp.dma_start(out[n * PART * P:(n + 1) * PART * P, :].rearrange("(t p) c -> p t c", p=P),
                             tok[:, PART * n:PART * n + PART, :]).then_inc(stored, 16)
            sp.wait_ge(stored, 16 * TT // PART)


def constants():
    c = np.zeros((P, C_N), np.float32)
    i = np.arange(P)
    c[:, C_ID:C_ID + P] = np.eye(P)
    c[:, C_GROUP:C_GROUP + P] = (i[:, None] // 8 == i[None, :] // 8) / 8.0
    c[:, C_HEAD:C_HEAD + P] = i[:, None] // D == i[None, :] // D
    c[:, C_FOLD:C_FOLD + D] = i[:, None] % D == np.arange(D)[None, :]
    c[:, C_IOTA:C_IOTA + NE] = np.arange(NE)
    c[:, C_BEFORE:C_BEFORE + P] = i[:, None] < i[None, :]
    c[:, C_ALL:C_ALL + P] = 1.0
    c[:, C_STEP:C_STEP + NK] = np.arange(NK) * SLOT
    c[:, C_SLOT:C_SLOT + NS] = np.arange(NS)
    return c


def kernel(**inputs):
    import concourse.bacc as bacc
    from concourse.bass_utils import run_bass_kernel_spmd

    a = {k: np.asarray(v) for k, v in inputs.items()}
    x = a["x"].reshape(C, S)
    t = a["L0_conv_temperature"].reshape(HEADS)

    def columns(v):
        return v.reshape(-1, P).T

    def rows(v):
        return np.broadcast_to(v.reshape(1, -1), (P, v.size))

    arrays = {
        "x": x, "xT": x.T, "wqkvT": a["L0_conv_w_qkv"].T, "wprojT": a["L0_conv_w_proj"].T,
        "t_col": columns(np.repeat(t, D)), "t_row": rows(t),
        "wq": a["L1_attn_Wq"], "wk": a["L1_attn_Wk"], "wv": a["L1_attn_Wv"],
        "bq": columns(a["L1_attn_bq"]), "bk": columns(a["L1_attn_bk"]),
        "bv": np.concatenate([rows(a["L1_attn_bv"])] * 2, axis=1),
        "wg": a["L1_ffn_Wg"], "bg": rows(a["L1_ffn_bg"]),
        "w1": a["L1_ffn_W1"], "b1": a["L1_ffn_b1"].reshape(NE, HC, P).transpose(0, 2, 1), "w2": a["L1_ffn_W2"], "b2": a["L1_ffn_b2"],
        "consts": constants(),
    }
    arrays = {k + "_in": np.ascontiguousarray(v) for k, v in arrays.items()}
    nc = bacc.Bacc("TRN2", target_bir_lowering=False, num_devices=1)
    args = [nc.dram_tensor(k, v.shape, mybir.dt.from_np(v.dtype), kind="ExternalInput").ap() for k, v in arrays.items()]
    out = nc.dram_tensor("out", (S, C), F32, kind="ExternalOutput").ap()
    build(nc, *args, out)
    r = run_bass_kernel_spmd(nc, [arrays], core_ids=[0])
    return r.results[0]["out"].T.reshape(1, C, 64, 64)
```
